# Optimizing a Trainium2 kernel written in Bass

```python
import numpy as np
import jax
import jax.numpy as jnp

def _softmax(x, axis=-1):
    return jax.nn.softmax(x, axis=axis)

def _gelu(x):
    return jax.nn.gelu(x, approximate=True)

def _silu(x):
    return jax.nn.silu(x)

def _sigmoid(x):
    return jax.nn.sigmoid(x)

def _layernorm(x, axis=-1, eps=1e-05):
    m = jnp.mean(x, axis=axis, keepdims=True)
    v = jnp.var(x, axis=axis, keepdims=True)
    return (x - m) / jnp.sqrt(v + eps)

def _scatter_add(tgt, idx, src, axis=0):
    return tgt.at[idx].add(src)

def _segment_sum(src, seg, n):
    return jax.ops.segment_sum(src, seg, n)
kernel_name = 'mk_decoder_postln_d2_seqx_r8_edbcaf'

def setup_inputs(seed: int=0):
    np.random.seed(seed)
    _w = jnp.asarray

    def _rec_inputs():
        import jax
        import jax.numpy as jnp
        _rk = jax.random.key(seed)
        x = -0.0003929 + 0.9999 * jax.random.normal(jax.random.fold_in(_rk, 1), (2, 256, 128), jnp.float32)
        _lenS = 256 - jax.random.randint(jax.random.fold_in(_rk, 7), (2,), 0, max(1, 256 // 4) + 1, jnp.int32)
        _lenS2 = 512 - jax.random.randint(jax.random.fold_in(_rk, 8), (2,), 0, max(1, 512 // 4) + 1, jnp.int32)
        _ctx_1024P = jax.random.normal(jax.random.fold_in(_rk, 11), (2, 16, 128), jnp.float32)
        _ctx_1024c = jax.random.dirichlet(jax.random.fold_in(_rk, 511), 0.3 * jnp.ones((16,), jnp.float32), (2, 512))
        _ctx_1024t = jnp.einsum('bsk,bkd->bsd', _ctx_1024c, _ctx_1024P)
        _ctx_1024t = _ctx_1024t * jax.lax.rsqrt(jnp.mean(jnp.square(_ctx_1024t)) + 1e-12) * 0.953939
        ctx_1024 = 4.13588e-05 + 0.999923 * (_ctx_1024t + 0.3 * jax.random.normal(jax.random.fold_in(_rk, 611), (2, 512, 128), jnp.float32))
        _validS = jnp.arange(256)[None, :] < _lenS[:, None]
        _validS2 = jnp.arange(512)[None, :] < _lenS2[:, None]
        _causal = jnp.tril(jnp.ones((256, 256), dtype=bool))
        mask_BxS2_bk0 = jnp.logical_not(jnp.broadcast_to(_validS2[:, :], (2, 512)))
        return (x, ctx_1024, mask_BxS2_bk0)
    x, ctx_1024, mask_BxS2_bk0 = _rec_inputs()

    def _L0_attn_setup():
        import jax, jax.numpy as jnp
        import numpy as np
        DIM = 128
        HEADS = 16
        HEAD_DIM = DIM // HEADS
        B, S = (4, 512)
        key = jax.random.key(seed)
        ks = jax.random.split(key, 8)
        sc = 1.0 / np.sqrt(DIM)
        return {'x': jax.random.normal(ks[0], (B, S, DIM), dtype=jnp.float32), 'Wq': jax.random.normal(ks[1], (DIM, DIM), dtype=jnp.float32) * sc, 'Wk': jax.random.normal(ks[2], (DIM, DIM), dtype=jnp.float32) * sc, 'Wv': jax.random.normal(ks[3], (DIM, DIM), dtype=jnp.float32) * sc, 'Wp': jax.random.normal(ks[4], (DIM, DIM), dtype=jnp.float32) * sc, 'bp': jnp.zeros((DIM,), dtype=jnp.float32), 'conv_w': jax.random.normal(ks[5], (DIM, 3), dtype=jnp.float32) * (1.0 / np.sqrt(3.0)), 'conv_b': jnp.zeros((DIM,), dtype=jnp.float32)}
    _L0_attn_all = _L0_attn_setup()
    _L0_attn_in = {k: v for k, v in _L0_attn_all.items() if k in ('Wq', 'Wk', 'Wv', 'Wp', 'bp', 'conv_w', 'conv_b')}
    del _L0_attn_all

    def _L0_xattn_setup():
        import jax, jax.numpy as jnp
        import numpy as np
        H = 128
        B = 8
        L_CHAR = 256
        L_SUB = 128

        def _linear(x, W, b):
            return jnp.einsum('blh,oh->blo', x, W) + b

        def _interp_linear(x, out_len):
            L_in = x.shape[1]
            pos = (jnp.arange(out_len, dtype=x.dtype) + 0.5) * (L_in / out_len) - 0.5
            pos = jnp.clip(pos, 0.0, L_in - 1)
            lo = jnp.floor(pos).astype(jnp.int32)
            hi = jnp.minimum(lo + 1, L_in - 1)
            w = (pos - lo.astype(x.dtype))[None, :, None]
            return x[:, lo] * (1 - w) + x[:, hi] * w
        key = jax.random.key(seed)
        ks = jax.random.split(key, 18)
        s = 0.02
        inp = {'char_emb': jax.random.normal(ks[0], (B, L_CHAR, H), jnp.float32), 'subword_emb': jax.random.normal(ks[1], (B, L_SUB, H), jnp.float32)}
        names = ['Wq_c', 'Wk_s', 'Wv_s', 'Wq_s', 'Wk_c', 'Wv_c']
        for i, n in enumerate(names):
            inp[n] = jax.random.normal(ks[2 + 2 * i], (H, H), jnp.float32) * s
            inp['b' + n[1:]] = jax.random.normal(ks[3 + 2 * i], (H,), jnp.float32) * s
        inp['Wg'] = jax.random.normal(ks[14], (H, 2 * H), jnp.float32) * s
        inp['bg'] = jax.random.normal(ks[15], (H,), jnp.float32) * s
        return inp
    _L0_xattn_all = _L0_xattn_setup()
    _L0_xattn_in = {k: v for k, v in _L0_xattn_all.items() if k in ('Wq_c', 'bq_c', 'Wk_s', 'bk_s', 'Wv_s', 'bv_s', 'Wq_s', 'bq_s', 'Wk_c', 'bk_c', 'Wv_c', 'bv_c', 'Wg', 'bg')}
    del _L0_xattn_all

    def _L0_ffn_setup():
        import jax, jax.numpy as jnp
        import numpy as np
        from jax import lax
        HIDDEN = 128
        INTER = 64
        E = 64
        K = 6
        G = 8
        TG = 4
        NSH = 2
        ISH = INTER * NSH

        def _moe_forward(hidden_states, gate_w, gate_bias, eg_w, eu_w, ed_w, sg_w, su_w, sd_w):
            B, S, H = hidden_states.shape
            x = hidden_states.reshape(-1, H)
            T = x.shape[0]
            shared = jax.nn.silu(x @ sg_w.T) * (x @ su_w.T) @ sd_w.T
            logits = x @ gate_w.T
            scores = jax.nn.sigmoid(logits) + gate_bias
            group_scores = scores.reshape(T, G, E // G).max(axis=-1)
            _, sel_groups = lax.top_k(group_scores, TG)
            group_mask = jnp.zeros((T, G), scores.dtype).at[jnp.arange(T)[:, None], sel_groups].set(1.0)
            mask = jnp.repeat(group_mask, E // G, axis=1)
            masked_scores = scores * mask
            topk_w, topk_i = lax.top_k(masked_scores, K)
            topk_w = topk_w / (topk_w.sum(axis=-1, keepdims=True) + 1e-08)
            comb = jnp.zeros((T, E), x.dtype).at[jnp.arange(T)[:, None], topk_i].add(topk_w)
            h = jax.nn.silu(jnp.einsum('th,eih->eti', x, eg_w)) * jnp.einsum('th,eih->eti', x, eu_w)
            routed = jnp.einsum('eti,ehi,te->th', h, ed_w, comb)
            return (shared + routed).reshape(B, S, H)
        key = jax.random.key(seed)
        ks = jax.random.split(key, 9)
        s = 0.02
        return {'hidden_states': jax.random.normal(ks[0], (1, 128, HIDDEN), jnp.float32), 'gate_w': jax.random.normal(ks[1], (E, HIDDEN), jnp.float32) * s, 'gate_bias': jnp.zeros((E,), jnp.float32), 'eg_w': jax.random.normal(ks[2], (E, INTER, HIDDEN), jnp.float32) * s, 'eu_w': jax.random.normal(ks[3], (E, INTER, HIDDEN), jnp.float32) * s, 'ed_w': jax.random.normal(ks[4], (E, HIDDEN, INTER), jnp.float32) * s, 'sg_w': jax.random.normal(ks[5], (ISH, HIDDEN), jnp.float32) * s, 'su_w': jax.random.normal(ks[6], (ISH, HIDDEN), jnp.float32) * s, 'sd_w': jax.random.normal(ks[7], (HIDDEN, ISH), jnp.float32) * s}
    _L0_ffn_all = _L0_ffn_setup()
    _L0_ffn_in = {k: v for k, v in _L0_ffn_all.items() if k in ('gate_w', 'gate_bias', 'eg_w', 'eu_w', 'ed_w', 'sg_w', 'su_w', 'sd_w')}
    del _L0_ffn_all

    def _L1_attn_setup():
        import jax, jax.numpy as jnp
        import numpy as np
        import math
        D_MODEL, HEADS, KQ = (128, 16, 64)
        B, S = (4, 256)
        key = jax.random.key(seed)
        k0, k1, k2, k3, k4 = jax.random.split(key, 5)
        scale = D_MODEL ** (-0.5)
        return {'x_BSE': jax.random.normal(k0, (B, S, D_MODEL), dtype=jnp.float32), 'w_q': jax.random.normal(k1, (D_MODEL, HEADS, KQ), dtype=jnp.float32) * scale, 'w_k': jax.random.normal(k2, (D_MODEL, HEADS, KQ), dtype=jnp.float32) * scale, 'w_v': jax.random.normal(k3, (D_MODEL, HEADS, KQ), dtype=jnp.float32) * scale, 'w_o': jax.random.normal(k4, (D_MODEL, HEADS, KQ), dtype=jnp.float32) * scale}
    _L1_attn_all = _L1_attn_setup()
    _L1_attn_in = {k: v for k, v in _L1_attn_all.items() if k in ('w_q', 'w_k', 'w_v', 'w_o')}
    del _L1_attn_all

    def _L1_xattn_setup():
        import jax, jax.numpy as jnp
        import numpy as np
        B, T, D, H = (2, 256, 128, 16)
        DK = D // H

        def _split_heads(x):
            b, s, _ = x.shape
            return x.reshape(b, s, H, DK).transpose(0, 2, 1, 3)
        key = jax.random.key(seed)
        ks = jax.random.split(key, 12)
        s = 0.02
        return {'query': jax.random.normal(ks[0], (B, T, D), jnp.float32), 'key': jax.random.normal(ks[1], (B, T, D), jnp.float32), 'value': jax.random.normal(ks[2], (B, T, D), jnp.float32), 'mask': jax.random.randint(ks[3], (B, T), 0, 2) != 0, 'Wq': jax.random.normal(ks[4], (D, D), jnp.float32) * s, 'bq': jnp.zeros((D,), jnp.float32), 'Wk': jax.random.normal(ks[5], (D, D), jnp.float32) * s, 'bk': jnp.zeros((D,), jnp.float32), 'Wv': jax.random.normal(ks[6], (D, D), jnp.float32) * s, 'bv': jnp.zeros((D,), jnp.float32), 'Wo': jax.random.normal(ks[7], (D, D), jnp.float32) * s, 'bo': jnp.zeros((D,), jnp.float32)}
    _L1_xattn_all = _L1_xattn_setup()
    _L1_xattn_in = {k: v for k, v in _L1_xattn_all.items() if k in ('Wq', 'bq', 'Wk', 'bk', 'Wv', 'bv', 'Wo', 'bo')}
    del _L1_xattn_all

    def _L1_ffn_setup():
        import math
        import jax, jax.numpy as jnp
        import numpy as np
        TOP_K = 2
        _GELU_C = math.sqrt(2.0 / math.pi)

        def gelu_new(x):
            return 0.5 * x * (1.0 + jnp.tanh(_GELU_C * (x + 0.044715 * x * x * x)))
        key = jax.random.key(seed)
        ks = jax.random.split(key, 6)
        B, T, C, E, H = (2, 256, 128, 8, 512)
        s_in = 1.0 / math.sqrt(C)
        s_hid = 1.0 / math.sqrt(H)
        return {'x': jax.random.normal(ks[0], (B, T, C), dtype=jnp.float32), 'router_w': jax.random.normal(ks[1], (E, C), dtype=jnp.float32) * s_in, 'w_fc': jax.random.normal(ks[2], (E, C, H), dtype=jnp.float32) * s_in, 'b_fc': jax.random.normal(ks[3], (E, H), dtype=jnp.float32) * 0.02, 'w_proj': jax.random.normal(ks[4], (E, H, C), dtype=jnp.float32) * s_hid, 'b_proj': jax.random.normal(ks[5], (E, C), dtype=jnp.float32) * 0.02}
    _L1_ffn_all = _L1_ffn_setup()
    _L1_ffn_in = {k: v for k, v in _L1_ffn_all.items() if k in ('router_w', 'w_fc', 'b_fc', 'w_proj', 'b_proj')}
    del _L1_ffn_all
    return {'x': x, 'ctx_1024': ctx_1024, 'mask_BxS2_bk0': mask_BxS2_bk0, 'L0_attn_Wq': _L0_attn_in['Wq'], 'L0_attn_Wk': _L0_attn_in['Wk'], 'L0_attn_Wv': _L0_attn_in['Wv'], 'L0_attn_Wp': _L0_attn_in['Wp'], 'L0_attn_bp': _L0_attn_in['bp'], 'L0_attn_conv_w': _L0_attn_in['conv_w'], 'L0_attn_conv_b': _L0_attn_in['conv_b'], 'L0_xattn_Wq_c': _L0_xattn_in['Wq_c'], 'L0_xattn_bq_c': _L0_xattn_in['bq_c'], 'L0_xattn_Wk_s': _L0_xattn_in['Wk_s'], 'L0_xattn_bk_s': _L0_xattn_in['bk_s'], 'L0_xattn_Wv_s': _L0_xattn_in['Wv_s'], 'L0_xattn_bv_s': _L0_xattn_in['bv_s'], 'L0_xattn_Wq_s': _L0_xattn_in['Wq_s'], 'L0_xattn_bq_s': _L0_xattn_in['bq_s'], 'L0_xattn_Wk_c': _L0_xattn_in['Wk_c'], 'L0_xattn_bk_c': _L0_xattn_in['bk_c'], 'L0_xattn_Wv_c': _L0_xattn_in['Wv_c'], 'L0_xattn_bv_c': _L0_xattn_in['bv_c'], 'L0_xattn_Wg': _L0_xattn_in['Wg'], 'L0_xattn_bg': _L0_xattn_in['bg'], 'L0_ffn_gate_w': _L0_ffn_in['gate_w'], 'L0_ffn_gate_bias': _L0_ffn_in['gate_bias'], 'L0_ffn_eg_w': _L0_ffn_in['eg_w'], 'L0_ffn_eu_w': _L0_ffn_in['eu_w'], 'L0_ffn_ed_w': _L0_ffn_in['ed_w'], 'L0_ffn_sg_w': _L0_ffn_in['sg_w'], 'L0_ffn_su_w': _L0_ffn_in['su_w'], 'L0_ffn_sd_w': _L0_ffn_in['sd_w'], 'L1_attn_w_q': _L1_attn_in['w_q'], 'L1_attn_w_k': _L1_attn_in['w_k'], 'L1_attn_w_v': _L1_attn_in['w_v'], 'L1_attn_w_o': _L1_attn_in['w_o'], 'L1_xattn_Wq': _L1_xattn_in['Wq'], 'L1_xattn_bq': _L1_xattn_in['bq'], 'L1_xattn_Wk': _L1_xattn_in['Wk'], 'L1_xattn_bk': _L1_xattn_in['bk'], 'L1_xattn_Wv': _L1_xattn_in['Wv'], 'L1_xattn_bv': _L1_xattn_in['bv'], 'L1_xattn_Wo': _L1_xattn_in['Wo'], 'L1_xattn_bo': _L1_xattn_in['bo'], 'L1_ffn_router_w': _L1_ffn_in['router_w'], 'L1_ffn_w_fc': _L1_ffn_in['w_fc'], 'L1_ffn_b_fc': _L1_ffn_in['b_fc'], 'L1_ffn_w_proj': _L1_ffn_in['w_proj'], 'L1_ffn_b_proj': _L1_ffn_in['b_proj']}

def reference(x, ctx_1024, mask_BxS2_bk0, L0_attn_Wq, L0_attn_Wk, L0_attn_Wv, L0_attn_Wp, L0_attn_bp, L0_attn_conv_w, L0_attn_conv_b, L0_xattn_Wq_c, L0_xattn_bq_c, L0_xattn_Wk_s, L0_xattn_bk_s, L0_xattn_Wv_s, L0_xattn_bv_s, L0_xattn_Wq_s, L0_xattn_bq_s, L0_xattn_Wk_c, L0_xattn_bk_c, L0_xattn_Wv_c, L0_xattn_bv_c, L0_xattn_Wg, L0_xattn_bg, L0_ffn_gate_w, L0_ffn_gate_bias, L0_ffn_eg_w, L0_ffn_eu_w, L0_ffn_ed_w, L0_ffn_sg_w, L0_ffn_su_w, L0_ffn_sd_w, L1_attn_w_q, L1_attn_w_k, L1_attn_w_v, L1_attn_w_o, L1_xattn_Wq, L1_xattn_bq, L1_xattn_Wk, L1_xattn_bk, L1_xattn_Wv, L1_xattn_bv, L1_xattn_Wo, L1_xattn_bo, L1_ffn_router_w, L1_ffn_w_fc, L1_ffn_b_fc, L1_ffn_w_proj, L1_ffn_b_proj):
    import jax
    import jax.numpy as jnp

    def _L0_attn_ref(x, Wq, Wk, Wv, Wp, bp, conv_w, conv_b):
        import jax, jax.numpy as jnp
        import numpy as np
        DIM = 128
        HEADS = 16
        HEAD_DIM = DIM // HEADS
        B, S = (4, 512)
        b, s, d = x.shape

        def split_heads(t):
            return t.reshape(b, s, HEADS, HEAD_DIM).transpose(0, 2, 1, 3)
        q = split_heads(x @ Wq.T)
        k = split_heads(x @ Wk.T)
        v = split_heads(x @ Wv.T)
        q = jax.nn.elu(q) + 1.0
        k = jax.nn.elu(k) + 1.0
        kv_state = jnp.einsum('bhnd,bhne->bhde', k, v)
        k_state = k.sum(axis=2)
        attn_out = jnp.einsum('bhnd,bhde->bhne', q, kv_state)
        denom = jnp.maximum(jnp.einsum('bhnd,bhd->bhn', q, k_state), 1e-06)[..., None]
        attn_out = (attn_out / denom).transpose(0, 2, 1, 3).reshape(b, s, d)
        xp = jnp.pad(x, ((0, 0), (1, 1), (0, 0)))
        local = xp[:, :-2, :] * conv_w[:, 0] + xp[:, 1:-1, :] * conv_w[:, 1] + xp[:, 2:, :] * conv_w[:, 2] + conv_b
        return (attn_out + local) @ Wp.T + bp

    def _L0_xattn_ref(char_emb, subword_emb, Wq_c, bq_c, Wk_s, bk_s, Wv_s, bv_s, Wq_s, bq_s, Wk_c, bk_c, Wv_c, bv_c, Wg, bg):
        import jax, jax.numpy as jnp
        import numpy as np
        H = 128
        B = 8
        L_CHAR = 256
        L_SUB = 128

        def _linear(x, W, b):
            return jnp.einsum('blh,oh->blo', x, W) + b

        def _interp_linear(x, out_len):
            L_in = x.shape[1]
            pos = (jnp.arange(out_len, dtype=x.dtype) + 0.5) * (L_in / out_len) - 0.5
            pos = jnp.clip(pos, 0.0, L_in - 1)
            lo = jnp.floor(pos).astype(jnp.int32)
            hi = jnp.minimum(lo + 1, L_in - 1)
            w = (pos - lo.astype(x.dtype))[None, :, None]
            return x[:, lo] * (1 - w) + x[:, hi] * w
        h = char_emb.shape[-1]
        scale = 1.0 / jnp.sqrt(jnp.asarray(h, char_emb.dtype))
        Q_char = _linear(char_emb, Wq_c, bq_c)
        K_sub = _linear(subword_emb, Wk_s, bk_s)
        V_sub = _linear(subword_emb, Wv_s, bv_s)
        scores = jnp.einsum('bqh,bkh->bqk', Q_char, K_sub) * scale
        char2sub = jnp.einsum('bqk,bkh->bqh', jax.nn.softmax(scores, axis=-1), V_sub)
        Q_sub = _linear(subword_emb, Wq_s, bq_s)
        K_char = _linear(char_emb, Wk_c, bk_c)
        V_char = _linear(char_emb, Wv_c, bv_c)
        scores2 = jnp.einsum('bqh,bkh->bqk', Q_sub, K_char) * scale
        sub2char = jnp.einsum('bqk,bkh->bqh', jax.nn.softmax(scores2, axis=-1), V_char)
        L_char = char_emb.shape[1]
        if sub2char.shape[1] != L_char:
            sub2char = _interp_linear(sub2char, L_char)
        gate_in = jnp.concatenate([char2sub, sub2char], axis=-1)
        gate = jax.nn.sigmoid(jnp.einsum('blh,oh->blo', gate_in, Wg) + bg)
        return gate * char2sub + (1 - gate) * sub2char

    def _L0_ffn_ref(hidden_states, gate_w, gate_bias, eg_w, eu_w, ed_w, sg_w, su_w, sd_w):
        import jax, jax.numpy as jnp
        import numpy as np
        from jax import lax
        HIDDEN = 128
        INTER = 64
        E = 64
        K = 6
        G = 8
        TG = 4
        NSH = 2
        ISH = INTER * NSH

        def _moe_forward(hidden_states, gate_w, gate_bias, eg_w, eu_w, ed_w, sg_w, su_w, sd_w):
            B, S, H = hidden_states.shape
            x = hidden_states.reshape(-1, H)
            T = x.shape[0]
            shared = jax.nn.silu(x @ sg_w.T) * (x @ su_w.T) @ sd_w.T
            logits = x @ gate_w.T
            scores = jax.nn.sigmoid(logits) + gate_bias
            group_scores = scores.reshape(T, G, E // G).max(axis=-1)
            _, sel_groups = lax.top_k(group_scores, TG)
            group_mask = jnp.zeros((T, G), scores.dtype).at[jnp.arange(T)[:, None], sel_groups].set(1.0)
            mask = jnp.repeat(group_mask, E // G, axis=1)
            masked_scores = scores * mask
            topk_w, topk_i = lax.top_k(masked_scores, K)
            topk_w = topk_w / (topk_w.sum(axis=-1, keepdims=True) + 1e-08)
            comb = jnp.zeros((T, E), x.dtype).at[jnp.arange(T)[:, None], topk_i].add(topk_w)
            h = jax.nn.silu(jnp.einsum('th,eih->eti', x, eg_w)) * jnp.einsum('th,eih->eti', x, eu_w)
            routed = jnp.einsum('eti,ehi,te->th', h, ed_w, comb)
            return (shared + routed).reshape(B, S, H)
        return _moe_forward(hidden_states, gate_w, gate_bias, eg_w, eu_w, ed_w, sg_w, su_w, sd_w)

    def _L1_attn_ref(x_BSE, w_q, w_k, w_v, w_o):
        import jax, jax.numpy as jnp
        import numpy as np
        import math
        D_MODEL, HEADS, KQ = (128, 16, 64)
        B, S = (4, 256)
        q_BSHK = jnp.einsum('BSE,EHK->BSHK', x_BSE, w_q)
        k_BMHK = jnp.einsum('BSE,EHK->BSHK', x_BSE, w_k)
        v_BMHK = jnp.einsum('BSE,EHK->BSHK', x_BSE, w_v)
        Kq = q_BSHK.shape[-1]
        logits_BSHM = jnp.einsum('BSHK,BMHK->BSHM', q_BSHK, k_BMHK) / math.sqrt(Kq)
        Sdim = logits_BSHM.shape[1]
        qpos = jnp.arange(Sdim)[:, None]
        mpos = jnp.arange(Sdim)[None, :]
        mask = jnp.where(qpos >= mpos, 0.0, -jnp.inf)[None, :, None, :]
        probs_BSHM = jax.nn.softmax(logits_BSHM + mask, axis=3)
        out_BSHK = jnp.einsum('BSHM,BMHK->BSHK', probs_BSHM, v_BMHK)
        return jnp.einsum('BSHK,EHK->BSE', out_BSHK, w_o)

    def _L1_xattn_ref(query, key, value, mask, Wq, bq, Wk, bk, Wv, bv, Wo, bo):
        import jax, jax.numpy as jnp
        import numpy as np
        B, T, D, H = (2, 256, 128, 16)
        DK = D // H

        def _split_heads(x):
            b, s, _ = x.shape
            return x.reshape(b, s, H, DK).transpose(0, 2, 1, 3)
        q = _split_heads(query @ Wq.T + bq)
        k = _split_heads(key @ Wk.T + bk)
        v = _split_heads(value @ Wv.T + bv)
        scale = 1.0 / np.sqrt(DK).astype(np.float32)
        scores = jnp.einsum('bhtd,bhsd->bhts', q, k) * scale
        scores = jnp.where(mask[:, None, None, :], scores, -jnp.inf)
        attn = jax.nn.softmax(scores, axis=-1)
        out = jnp.einsum('bhts,bhsd->bhtd', attn, v)
        out = out.transpose(0, 2, 1, 3).reshape(query.shape[0], -1, D)
        return out @ Wo.T + bo

    def _L1_ffn_ref(x, router_w, w_fc, b_fc, w_proj, b_proj):
        import math
        import jax, jax.numpy as jnp
        import numpy as np
        TOP_K = 2
        _GELU_C = math.sqrt(2.0 / math.pi)

        def gelu_new(x):
            return 0.5 * x * (1.0 + jnp.tanh(_GELU_C * (x + 0.044715 * x * x * x)))
        B, T, C = x.shape
        E = router_w.shape[0]
        N = B * T
        xf = x.reshape(N, C)
        logits = xf @ router_w.T
        probs = jax.nn.softmax(logits, axis=-1)
        topk_probs, topk_idx = jax.lax.top_k(probs, TOP_K)
        topk_probs = topk_probs / jnp.sum(topk_probs, axis=-1, keepdims=True)
        combine = jnp.zeros((N, E), dtype=x.dtype).at[jnp.arange(N)[:, None], topk_idx].add(topk_probs)
        h = gelu_new(jnp.einsum('nc,ech->neh', xf, w_fc) + b_fc)
        out = jnp.einsum('neh,ehc->nec', h, w_proj) + b_proj
        y = jnp.einsum('nec,ne->nc', out, combine)
        return y.reshape(B, T, C)
    x = _layernorm(x + _L0_attn_ref(x, L0_attn_Wq, L0_attn_Wk, L0_attn_Wv, L0_attn_Wp, L0_attn_bp, L0_attn_conv_w, L0_attn_conv_b), axis=-1)
    x = _layernorm(x + _L0_xattn_ref(x, ctx_1024, L0_xattn_Wq_c, L0_xattn_bq_c, L0_xattn_Wk_s, L0_xattn_bk_s, L0_xattn_Wv_s, L0_xattn_bv_s, L0_xattn_Wq_s, L0_xattn_bq_s, L0_xattn_Wk_c, L0_xattn_bk_c, L0_xattn_Wv_c, L0_xattn_bv_c, L0_xattn_Wg, L0_xattn_bg), axis=-1)
    x = _layernorm(x + _L0_ffn_ref(x, L0_ffn_gate_w, L0_ffn_gate_bias, L0_ffn_eg_w, L0_ffn_eu_w, L0_ffn_ed_w, L0_ffn_sg_w, L0_ffn_su_w, L0_ffn_sd_w), axis=-1)
    x = _layernorm(x + _L1_attn_ref(x, L1_attn_w_q, L1_attn_w_k, L1_attn_w_v, L1_attn_w_o), axis=-1)
    x = _layernorm(x + _L1_xattn_ref(x, ctx_1024, ctx_1024, mask_BxS2_bk0, L1_xattn_Wq, L1_xattn_bq, L1_xattn_Wk, L1_xattn_bk, L1_xattn_Wv, L1_xattn_bv, L1_xattn_Wo, L1_xattn_bo), axis=-1)
    x = _layernorm(x + _L1_ffn_ref(x, L1_ffn_router_w, L1_ffn_w_fc, L1_ffn_b_fc, L1_ffn_w_proj, L1_ffn_b_proj), axis=-1)
    return x

_drawn_inputs = setup_inputs


def setup_inputs(seed=0):
    import zlib

    import numpy as np

    out = dict(_drawn_inputs(seed))
    spreads = {'L0_attn_bp': (0.0, 0.1),
     'L0_attn_conv_b': (0.0, 0.1),
     'L0_ffn_gate_bias': (0.0, 0.422),
     'L1_xattn_bq': (0.0, 1.866),
     'L1_xattn_bk': (0.0, 2.0),
     'L1_xattn_bv': (0.0, 0.1),
     'L1_xattn_bo': (0.0, 0.1)}
    factors = {'L0_xattn_Wq_c': 8.0,
     'L0_xattn_bq_c': 17.091,
     'L0_xattn_Wk_s': 4.304,
     'L0_xattn_bk_s': 64.0,
     'L0_xattn_Wq_s': 4.07,
     'L0_xattn_bq_s': 8.0,
     'L0_xattn_Wk_c': 8.0,
     'L0_xattn_bk_c': 64.0,
     'L0_xattn_Wg': 4.05,
     'L0_xattn_bg': 8.0,
     'L0_ffn_gate_w': 4.289,
     'L0_ffn_eg_w': 3.512,
     'L0_ffn_eu_w': 3.334,
     'L0_ffn_ed_w': 3.342,
     'L1_xattn_Wq': 8.0,
     'L1_xattn_Wk': 4.323,
     'L1_ffn_b_fc': 6.16,
     'L1_ffn_b_proj': 4.145,
     'L0_ffn_su_w': 2.859,
     'L0_ffn_sd_w': 4.267}
    for name, (base, spread) in spreads.items():
        noise = np.random.default_rng([zlib.crc32(name.encode()), seed]).standard_normal(out[name].shape)
        drawn = base * np.exp(spread * noise) if base else spread * noise
        out[name] = jnp.asarray(drawn.astype(out[name].dtype))
    for name, factor in factors.items():
        out[name] = (out[name] * factor).astype(out[name].dtype)
    return out
```

```python
from contextlib import ExitStack

import numpy as np
import concourse.bass as bass
from concourse import mybir

F32 = mybir.dt.float32
F32R = mybir.dt.float32r
U8 = mybir.dt.uint8
ALU = mybir.AluOpType
ACT = mybir.ActivationFunctionType
AX = mybir.AxisListType.X

D = 128
NB = 2
S = 256
SC = 512
T = NB * S
C = NB * SC
TT = T // 128
HD = 8
NH = 16
E0, I0 = 64, 64
G0, TG0, K0 = 8, 4, 6
NP = E0 // 2
KQ = 64
HP = NH // 2
E1, H1, K1 = 8, 512, 2
HC = H1 // 128
NEG = -1.0e30

IDENT = [("ident", D)]
FRONT = [("xT", T), ("WqT", D), ("WkvT", 2 * D), ("conv", 4), ("blocks", D), ("heads", NH), ("x_tok", T), ("WpT", D)]
CROSS = [("ctxT", C), ("KsT_w", D), ("QsT_w", D), ("Vs_w", D), ("QcT_w", D), ("KcT_w", D), ("Vc_w", D),
         ("gate_w", 2 * D), ("cols", 5)]
ROUTE = [("gw", E0), ("reset8", TT * G0), ("reset64", TT * E0), ("rw", E1)]
HEADS = [("wo", NH * KQ), ("causal", 128), ("half", 2)]
MASKED = [("Kr_w", 4 * D), ("Qr_w", 4 * D), ("V_w", D), ("O_w", D), ("qb", 4), ("kb", 4), ("sel", 12)]
EW = H1 + HC * D + HC
PACKS = {"ident": IDENT, "front": FRONT, "cross": CROSS, "route": ROUTE, "heads": HEADS, "masked": MASKED}
ROWS = [("bp", D), ("bvs", D), ("bvc", D), ("gbias", E0), ("bv", D), ("bo", D)]
SEL_LO_Q, SEL_LO_K, SEL_HEAD, SEL_MASK, SEL_MAX, SEL_MAXES = 0, 1, 2, 6, 7, 11
HR = 3 * HD
MR = 96
KR = 112


def width(pack):
    return sum(n for _, n in pack)


def build(nc, packs, rows, bproj, maskin, stream, heads_w, experts_w, out):
    with ExitStack() as ctx:
        early = ExitStack()
        late = ExitStack()
        late4 = ExitStack()
        late5 = ExitStack()

        def sb(name, shape, dt=F32, stack=ctx):
            return stack.enter_context(nc.sbuf_tensor(name, shape, dt))

        def sem(name):
            return ctx.enter_context(nc.semaphore(name))

        psum = ctx.enter_context(nc.psum_tensor("psum", [128, 8, 512], F32))
        pk = {n: sb("pk_" + n, [128, width(p)]) for n, p in PACKS.items() if n not in ("front", "cross")}
        rowb = sb("rowb", [128, width(ROWS)])
        bpj = sb("bpj", [E1, D])
        maskb = sb("maskb", [128, C], U8)

        x_tok = sb("x_tok", [128, TT, D])
        res = sb("res", [128, TT, D])
        z = sb("z", [128, TT, D])
        stats = sb("stats", [128, TT, 6])
        mv = sb("mv", [128, TT, 2])
        vare = sb("vare", [128, TT])
        rstd = sb("rstd", [128, TT])
        mhalf = sb("mhalf", [128, TT])
        one1 = sb("one", [128, 1])
        xT = sb("xT_f32", [128, T])
        xh = sb("xh", [128, T], F32R)
        xl = sb("xl", [128, T], F32R)
        identr = sb("identr", [128, 128], F32R)
        causr = sb("causr", [128, 128], F32R)
        KX = sb("k4_packed", [128, 4, C], F32R)
        Vx = sb("v4_and_one", [128, C // 128, NH, HD + 1])
        raw = sb("pair_raw", [128, 4, 512])
        whi = sb("pair_hi", [128, 4, 384], F32R)
        wlo = sb("pair_lo", [128, 4, 256], F32R)
        gwh = sb("gwh", [128, E0], F32R)
        gwl = sb("gwl", [128, E0], F32R)
        rwh = sb("rwh", [128, E1], F32R)
        rwl = sb("rwl", [128, E1], F32R)
        sg = sb("silu_gate", [128, 2, T])
        h1 = sb("h_unweighted", [128, 2, T])
        hh = sb("h_weighted", [128, 2, T])
        score = sb("score", [128, TT, E0])
        gsc = sb("group_score", [128, TT, G0])
        m8 = sb("top8", [128, TT, 8])
        cnt = sb("count_above", [128, TT])
        gt = sb("above", [128, TT * E0])
        eq = sb("equal", [128, TT * E0])
        cum = sb("equal_so_far", [128, TT * E0])
        selg = sb("selected", [128, TT * E0])
        wsum = sb("weight_sum", [128, TT])
        comb = sb("comb", [128, TT, E0])
        combhl = sb("comb_hi_lo", [128, TT, 128])
        combT = sb("comb_T", [128, T], F32R)
        for n in ("front", "cross"):
            pk[n] = sb("pk_" + n, [128, width(PACKS[n])], stack=early)
        at = {}

        def place(n):
            o = 0
            for name, w in PACKS[n]:
                at[name] = pk[n][:, o:o + w]
                o += w

        for n in pk:
            place(n)
        o = 0
        for name, w in ROWS:
            at[name] = rowb[:, o:o + w]
            o += w
        ident = at["ident"]

        s_in = {n: sem("in_" + n) for n in [*PACKS, "rows", "bproj", "mask"]}
        s_y = sem("y_summed")
        s_res = sem("residual_biased")
        s_var = sem("variance")
        s_rstd = sem("rstd_powed")
        s_xn = sem("x_normed")
        s_xT = sem("x_transposed")
        s_xh = sem("x_hi")
        s_xl = sem("x_lo")
        s_out = sem("output_stored")
        s_dve = sem("dve_step")
        s_pool = sem("pool_step")
        s_act = sem("act_step")
        s_mh = sem("minus_half_set")

        block = ctx.enter_context(nc.Block())
        count = {"dve": 0, "pool": 0, "act": 0}

        def dstep(dve, ins):
            count["dve"] += 1
            ins.then_inc(s_dve, 1)
            dve.wait_ge(s_dve, count["dve"])

        def pstep(pool, ins):
            count["pool"] += 1
            ins.then_inc(s_pool, 1)
            pool.wait_ge(s_pool, count["pool"])

        def tiles(ap, n=TT):
            return ap.rearrange("p (t d) -> p t d", t=n)

        Y = tiles(psum[:, 7, :])

        def norm_vector(dve, n, residual):
            dve.wait_ge(s_y, n + 1)
            zz = Y
            if residual is not None:
                zz = z[:]
                dstep(dve, dve.tensor_tensor(zz, Y, residual, ALU.add))
            for i in range(TT):
                ins = dve.bn_stats(stats[:, i, :], zz[:, i, :])
            dstep(dve, ins)
            for i in range(TT):
                ins = dve.bn_aggr(mv[:, i, :], stats[:, i, :])
            dstep(dve, ins)
            dve.tensor_scalar(vare[:], mv[:, :, 1], 1e-5, None, ALU.add).then_inc(s_var, 1)
            dve.wait_ge(s_rstd, n + 1)
            for i in range(TT):
                ins = dve.tensor_scalar(x_tok[:, i, :], zz[:, i, :], mv[:, i, 0:1], rstd[:, i:i + 1],
                                        ALU.subtract, ALU.mult)
            ins.then_inc(s_xn, 1)

        def norm_pool(pool, n):
            pool.wait_ge(s_var, n + 1)
            if n == 0:
                pool.wait_ge(s_mh, 1)
            pool.tensor_tensor(rstd[:], vare[:], mhalf[:], ALU.pow).then_inc(s_rstd, 1)

        def norm_tensor(pe, n):
            pe.wait_ge(s_xn, n + 1)
            for i in range(TT):
                ins = pe.transpose(psum[:, 6, i * 128:i * 128 + 128], x_tok[:, i, :], ident)
            ins.then_inc(s_xT, 1)

        def norm_scalar(act, n):
            act.wait_ge(s_xT, n + 1)
            act.activation(xT[:] if n == 0 else xh[:], psum[:, 6, :], ACT.Copy).then_inc(s_xh, 1)

        def norm_lo(dve, n):
            dve.wait_ge(s_xh, n + 1)
            dve.tensor_tensor(xl[:], psum[:, 6, :], xh[:].bitcast(F32), ALU.subtract).then_inc(s_xl, 1)

        def three(pe, out_, wh, wl, ah, al, start=True, stop=True):
            pe.matmul(out_, wh, ah, start=start, stop=False)
            pe.matmul(out_, wl, ah, start=False, stop=False)
            return pe.matmul(out_, wh, al, start=False, stop=stop)

        kmin = sb("kmin", [128, TT, D], stack=early)
        kphi = sb("kphi", [128, TT, D], stack=early)
        qmin = sb("qmin", [128, T], stack=early)
        qphi = sb("qphi", [128, T], stack=early)
        v_one = sb("v_one", [128, TT, D + 1], stack=early)
        kvm = sb("kvm", [128, NB, D + NH], stack=early)
        rden = sb("rden", [128, TT, NH], stack=early)
        att = sb("att", [128, TT, D], stack=early)
        loc = sb("loc", [128, NB, S], stack=early)
        aT = sb("aT", [128, T], stack=early)
        KsT = sb("KsT", [128, C], stack=early)
        QsT = sb("QsT", [128, C], stack=early)
        Vs = sb("Vs", [128, C // 128, D], stack=early)

        s_q = sem("q_projected")
        s_kv = sem("kv_projected")
        s_km = sem("kq_below_zero")
        s_ke = sem("kq_exp")
        s_phi = sem("kq_features")
        s_v = sem("v_copied")
        s_vone = sem("v_ones_set")
        s_st = sem("state_summed")
        s_stm = sem("state_masked")
        s_num = sem("numerators")
        s_att = sem("attention")
        s_attT = sem("attention_transposed")
        s_aT = sem("attention_plus_local")
        s_cps = sem("context_projected")
        s_cev = sem("context_copied")
        s_cv = sem("context_values")
        s_cvd = sem("context_values_biased")

        num = psum[:, 1:3, :].rearrange("p a (i n) -> p (a i) n", i=2)
        state = psum[:, 3, :].rearrange("p (b n) -> p b n", b=NB)

        def context_kq(pe, k):
            w, h = (at["KsT_w"], at["QsT_w"])[k // 2], k % 2
            if k == 0:
                pe.wait_ge(s_in["cross"], 16)
            if k >= 2:
                pe.wait_ge(s_cev, k - 1)
            pe.matmul(psum[:, 4 + k % 2, :], w, at["ctxT"][:, h * 512:h * 512 + 512],
                      start=True, stop=True).then_inc(s_cps, 1)

        def stage0_tensor(pe):
            pe.wait_ge(s_in["ident"], 16)
            pe.wait_ge(s_in["front"], 16)
            for a in range(2):
                for i in range(TT):
                    ins = pe.matmul(psum[:, 1 + a, i * 128:i * 128 + 128], at["xT"][:, i * 128:i * 128 + 128],
                                    at["WkvT"][:, a * D:a * D + D], start=True, stop=True)
                ins.then_inc(s_kv, 1)
            pe.matmul(psum[:, 0, :], at["WqT"], at["xT"], start=True, stop=True).then_inc(s_q, 1)
            context_kq(pe, 0)
            context_kq(pe, 1)
            pe.wait_ge(s_phi, 1)
            pe.wait_ge(s_v, 1)
            pe.wait_ge(s_vone, 1)
            for b in range(NB):
                for i in range(2):
                    ins = pe.matmul(state[:, b, 0:D + 1], kphi[:, 2 * b + i, :], v_one[:, 2 * b + i, :],
                                    start=i == 0, stop=i == 1)
            ins.then_inc(s_st, 1)
            context_kq(pe, 2)
            context_kq(pe, 3)
            pe.wait_ge(s_stm, 1)
            pe.wait_ge(s_phi, 2)
            for i in range(TT):
                ins = pe.matmul(num[:, i, 0:D + NH], qphi[:, i * 128:i * 128 + 128], kvm[:, i // 2, :],
                                start=True, stop=True)
            ins.then_inc(s_num, 1)
            pe.wait_ge(s_cev, 4)
            for i in range(C // 128):
                ins = pe.matmul(psum[:, 4 + i // 4, i % 4 * 128:i % 4 * 128 + 128],
                                at["ctxT"][:, i * 128:i * 128 + 128], at["Vs_w"], start=True, stop=True)
            ins.then_inc(s_cv, 1)
            pe.wait_ge(s_att, 1)
            for i in range(TT):
                ins = pe.transpose(psum[:, 0, i * 128:i * 128 + 128], att[:, i, :], ident)
            ins.then_inc(s_attT, 1)
            pe.wait_ge(s_aT, 1)
            for i in range(TT):
                ins = pe.matmul(Y[:, i, :], aT[:, i * 128:i * 128 + 128], at["WpT"], start=True, stop=True)
            ins.then_inc(s_y, 1)
            kv4_tensor(pe, 0)
            norm_tensor(pe, 0)

        def stage0_vector(dve):
            dve.wait_ge(s_kv, 1)
            dve.tensor_scalar(kmin[:], tiles(psum[:, 1, :]), 0.0, None, ALU.min).then_inc(s_km, 1)
            dve.wait_ge(s_q, 1)
            dve.tensor_scalar(qmin[:], psum[:, 0, :], 0.0, None, ALU.min).then_inc(s_km, 1)
            dve.wait_ge(s_ke, 1)
            dve.scalar_tensor_tensor(kphi[:], tiles(psum[:, 1, :]), 0.0, kmin[:], ALU.max, ALU.add).then_inc(s_phi, 1)
            dve.wait_ge(s_ke, 2)
            dve.scalar_tensor_tensor(qphi[:], psum[:, 0, :], 0.0, qmin[:], ALU.max, ALU.add).then_inc(s_phi, 1)
            xs = at["xT"].rearrange("p (b s) -> p b s", b=NB)
            cw = at["conv"]
            dstep(dve, dve.tensor_scalar(loc[:], xs, cw[:, 1:2], cw[:, 3:4], ALU.mult, ALU.add))
            dstep(dve, dve.scalar_tensor_tensor(loc[:, :, 1:S], xs[:, :, 0:S - 1], cw[:, 0:1], loc[:, :, 1:S],
                                                ALU.mult, ALU.add))
            dstep(dve, dve.scalar_tensor_tensor(loc[:, :, 0:S - 1], xs[:, :, 1:S], cw[:, 2:3],
                                                loc[:, :, 0:S - 1], ALU.mult, ALU.add))
            dve.wait_ge(s_st, 1)
            dve.tensor_tensor(kvm[:, :, 0:D], state[:, :, 0:D],
                              at["blocks"].rearrange("p (o d) -> p o d", o=1).broadcast_to([128, NB, D]), ALU.mult)
            for b in range(NB):
                ins = dve.tensor_scalar(kvm[:, b, D:D + NH], at["heads"], state[:, b, D:D + 1], None, ALU.mult)
            ins.then_inc(s_stm, 1)
            dve.wait_ge(s_num, 1)
            dstep(dve, dve.tensor_scalar(rden[:], num[:, :, D:D + NH], 1e-6, None, ALU.max))
            dstep(dve, dve.reciprocal(rden[:], rden[:]))
            dve.tensor_tensor(att[:].rearrange("p t (h d) -> p t h d", h=NH),
                              num[:, :, 0:D].rearrange("p t (h d) -> p t h d", h=NH),
                              rden[:].rearrange("p t (h o) -> p t h o", o=1).broadcast_to([128, TT, NH, HD]),
                              ALU.mult).then_inc(s_att, 1)
            dve.wait_ge(s_attT, 1)
            dve.tensor_tensor(aT[:], psum[:, 0, :], loc[:].rearrange("p b s -> p (b s)"), ALU.add).then_inc(s_aT, 1)
            dve.wait_ge(s_cv, 1)
            dve.wait_ge(s_in["rows"], 16)
            dve.tensor_tensor(Vs[:], psum[:, 4:6, :].rearrange("p a (t d) -> p (a t) d", t=4),
                              at["bvs"].rearrange("p (o d) -> p o d", o=1).broadcast_to([128, 8, D]),
                              ALU.add).then_inc(s_cvd, 1)
            dve.wait_ge(s_res, 1)
            norm_vector(dve, 0, res[:])
            kv4_vector(dve, 0)

        def stage0_scalar(act):
            act.wait_ge(s_km, 1)
            act.activation(kmin[:], kmin[:], ACT.Exp).then_inc(s_ke, 1)
            act.wait_ge(s_km, 2)
            act.activation(qmin[:], qmin[:], ACT.Exp).then_inc(s_ke, 1)
            act.wait_ge(s_kv, 2)
            act.activation(v_one[:, :, 0:D], tiles(psum[:, 2, :]), ACT.Copy).then_inc(s_v, 1)
            for k in range(4):
                act.wait_ge(s_cps, k + 1)
                act.activation((KsT, QsT)[k // 2][:, k % 2 * 512:k % 2 * 512 + 512], psum[:, 4 + k % 2, :],
                               ACT.Identity, bias=at["cols"][:, k // 2:k // 2 + 1]).then_inc(s_cev, 1)
            kv4_scalar(act, 0)
            norm_scalar(act, 0)

        def stage0_pool(pool):
            pool.memset(mhalf[:], -0.5).then_inc(s_mh, 1)
            pool.memset(v_one[:, :, D:D + 1], 1.0).then_inc(s_vone, 1)
            pool.memset(Vx[:, :, :, HD:HD + 1], 1.0).then_inc(s_v4o, 1)
            pool.wait_ge(s_in["front"], 16)
            pool.wait_ge(s_in["rows"], 16)
            pool.tensor_tensor(res[:], tiles(at["x_tok"]),
                               at["bp"].rearrange("p (o d) -> p o d", o=1).broadcast_to([128, TT, D]),
                               ALU.add).then_inc(s_res, 1)
            norm_pool(pool, 0)

        kxf = sb("k4_biased", [128, 4, 512], stack=early)
        kxr = sb("k4_rounded", [128, 4, 512], F32R, stack=early)
        km = sb("mask4_added", [128, C], stack=early)
        kones = sb("mask4_rows", [128, C], stack=early)
        s_k4 = sem("k4_projected")
        s_k4a = sem("k4_copied")
        s_k4d = sem("k4_split")
        s_v4 = sem("v4_projected")
        s_v4c = sem("v4_biased")
        s_v4o = sem("v4_ones_set")
        s_kx = sem("kv4_ready")

        def kv4_tensor(pe, part):
            pe.wait_ge(s_in["masked"], 16)
            if not part:
                pe.wait_ge(s_cvd, 1)
            for n in range(4 * part, 4 * part + 4):
                if n % 4 >= 2:
                    pe.wait_ge(s_k4a, n - 1)
                pe.matmul(psum[:, (4, 0)[part] + n % 2, :], at["Kr_w"][:, n // 2 * D:n // 2 * D + D],
                          at["ctxT"][:, n % 2 * 512:n % 2 * 512 + 512], start=True, stop=True).then_inc(s_k4, 1)
            if not part:
                for i in range(C // 128):
                    ins = pe.matmul(psum[:, 1 + i // 4, i % 4 * 128:i % 4 * 128 + 128],
                                    at["ctxT"][:, i * 128:i * 128 + 128], at["V_w"], start=True, stop=True)
                ins.then_inc(s_v4, 1)

        def kv4_scalar(act, part):
            act.wait_ge(s_in["masked"], 16)
            for n in range(4 * part, 4 * part + 4):
                act.wait_ge(s_k4, n + 1)
                if part:
                    act.wait_ge(s_k4d, n - 3)
                bias = at["kb"][:, n // 2:n // 2 + 1]
                act.activation(kxf[:, n % 4, :], psum[:, (4, 0)[part] + n % 2, :], ACT.Identity, bias=bias)
                act.activation(kxr[:, n % 4, :], psum[:, (4, 0)[part] + n % 2, :], ACT.Identity,
                               bias=bias).then_inc(s_k4a, 1)

        def kv4_vector(dve, part):
            dve.wait_ge(s_in["masked"], 16)
            for n in range(4 * part, 4 * part + 4):
                dve.wait_ge(s_k4a, n + 1)
                dve.scalar_tensor_tensor(KX[:, n // 2, n % 2 * 512:n % 2 * 512 + 512], kxr[:, n % 4, :].bitcast(F32),
                                         at["sel"][:, SEL_LO_K:SEL_LO_K + 1], kxf[:, n % 4, :],
                                         ALU.mult, ALU.add).then_inc(s_k4d, 1)
            if part:
                dve.wait_ge(s_in["mask"], 16)
                m = slice(MR, 128)
                dstep(dve, dve.tensor_scalar(km[m, :], maskb[m, :], -NEG, NEG, ALU.mult, ALU.add))
                dstep(dve, dve.tensor_scalar(kones[m, :], km[m, :], at["sel"][m, SEL_MASK:SEL_MASK + 1],
                                             at["sel"][m, SEL_MAXES:SEL_MAXES + 1], ALU.mult, ALU.add))
                dve.wait_ge(s_k4d, 8)
                for t in range(4):
                    ins = dve.tensor_copy(KX[m, t, :], kones[m, :])
                ins.then_inc(s_kx, 1)
            else:
                dve.wait_ge(s_v4, 1)
                dve.wait_ge(s_v4o, 1)
                dve.tensor_tensor(Vx[:, :, :, 0:HD],
                                  psum[:, 1:3, :].rearrange("p a (t h d) -> p (a t) h d", t=4, h=NH),
                                  at["bv"].rearrange("p (o h d) -> p o h d", o=1, h=NH).broadcast_to([128, 8, NH, HD]),
                                  ALU.add).then_inc(s_v4c, 1)

        QcT = sb("QcT", [128, T], stack=early)
        KcT = sb("KcT", [128, T], stack=early)
        Vc = sb("Vc", [128, TT, D], stack=early)
        P1 = sb("P1", [128, TT, SC], stack=early)
        P2 = sb("P2", [128, 8, S], stack=early)
        P1T = sb("P1T", [128, NB, 4, S], stack=early)
        P2T = sb("P2T", [128, NB, 2, SC], stack=early)
        mx1 = sb("mx1", [128, TT], stack=early)
        mx2 = sb("mx2", [128, 8], stack=early)
        sm1 = sb("sm1", [128, TT], stack=early)
        sm2 = sb("sm2", [128, 8], stack=early)
        c2s = sb("c2s", [128, T], stack=early)
        s2c = sb("s2c", [128, T], stack=early)
        gth = sb("gth", [128, T], stack=early)
        dif = sb("dif", [128, T], stack=early)
        hbg = sb("hbg", [128, 1], stack=early)
        SCALE1 = 1.0 / float(np.sqrt(np.float32(D)))

        s_p1 = sem("x_projected")
        s_p1c = sem("x_qk_copied")
        s_p1v = sem("x_v_biased")
        s_s1 = sem("scores_by_token")
        s_s2 = sem("scores_by_context")
        s_m1 = sem("max_by_token")
        s_m2 = sem("max_by_context")
        s_e1 = sem("exp_by_token")
        s_e2 = sem("exp_by_context")
        s_n1 = sem("probs_by_token")
        s_n2 = sem("probs_by_context")
        s_t1 = sem("probs_by_token_T")
        s_t2 = sem("probs_by_context_T")
        s_t1c = sem("probs_by_token_T_copied")
        s_t2c = [sem(f"probs_by_context_T_copied_{b}") for b in range(NB)]
        s_o1 = sem("tokens_attended")
        s_o2 = sem("context_attended")
        s_o1c = sem("tokens_attended_copied")
        s_o2c = sem("context_attended_paired")
        s_g = sem("gate_summed")
        s_gt = sem("gate_tanh")
        s_mix = sem("gated")
        s_hbg = sem("half_gate_bias")
        BK2 = [0, 1, 2, 7]

        def s2_at(k):
            return psum[:, BK2[k // 2], k % 2 * S:k % 2 * S + S]

        def stage1_tensor(pe):
            pe.wait_ge(s_xh, 1)
            pe.matmul(psum[:, 0, :], at["QcT_w"], xT[:], start=True, stop=True).then_inc(s_p1, 1)
            pe.wait_ge(s_v4c, 1)
            pe.matmul(psum[:, 1, :], at["KcT_w"], xT[:], start=True, stop=True).then_inc(s_p1, 1)
            for i in range(TT):
                ins = pe.matmul(psum[:, 2, i * 128:i * 128 + 128], xT[:, i * 128:i * 128 + 128], at["Vc_w"],
                                start=True, stop=True)
            ins.then_inc(s_p1, 1)
            pe.wait_ge(s_p1c, 1)
            pe.wait_ge(s_cev, 4)
            pe.wait_ge(s_cvd, 1)
            for i in range(TT):
                pe.matmul(psum[:, 3 + i, :], QcT[:, i * 128:i * 128 + 128], KsT[:, i // 2 * SC:i // 2 * SC + SC],
                          start=True, stop=True).then_inc(s_s1, 1)
            pe.wait_ge(s_p1c, 2)
            pe.wait_ge(s_p1v, 1)
            for k in range(8):
                ins = pe.matmul(s2_at(k), QsT[:, k * 128:k * 128 + 128], KcT[:, k // 4 * S:k // 4 * S + S],
                                start=True, stop=True)
                if k % 2:
                    ins.then_inc(s_s2, 1)
            pe.wait_ge(s_e1, TT)
            for i in range(TT):
                pe.wait_ge(s_n1, i + 1)
                for j in range(4):
                    bk = 3 + 2 * (i // 2) + j // 2
                    o_ = j % 2 * S + i % 2 * 128
                    ins = pe.transpose(psum[:, bk, o_:o_ + 128], P1[:, i, j * 128:j * 128 + 128], ident)
                if i % 2:
                    ins.then_inc(s_t1, 1)
            pe.wait_ge(s_e2, 8)
            for k in range(8):
                pe.wait_ge(s_n2, k + 1)
                for j in range(2):
                    ins = pe.transpose(psum[:, BK2[k // 4 * 2 + j], k % 4 * 128:k % 4 * 128 + 128],
                                       P2[:, k, j * 128:j * 128 + 128], ident)
                if k % 4 == 3:
                    ins.then_inc(s_t2, 1)
            pe.wait_ge(s_t1c, 2)
            for b in range(NB):
                for j in range(4):
                    ins = pe.matmul(psum[:, 3, b * S:b * S + S], Vs[:, b * 4 + j, :], P1T[:, b, j, :],
                                    start=j == 0, stop=j == 3)
            ins.then_inc(s_o1, 1)
            for b in range(NB):
                pe.wait_ge(s_t2c[b], 1)
                for j in range(2):
                    ins = pe.matmul(psum[:, 4 + b, :], Vc[:, b * 2 + j, :], P2T[:, b, j, :],
                                    start=j == 0, stop=j == 1)
                ins.then_inc(s_o2, 1)
            pe.wait_ge(s_o1c, 1)
            pe.matmul(psum[:, 6, :], at["gate_w"][:, 0:D], c2s[:], start=True, stop=False)
            pe.wait_ge(s_o2c, 2)
            pe.matmul(psum[:, 6, :], at["gate_w"][:, D:2 * D], s2c[:], start=False, stop=True).then_inc(s_g, 1)
            kv4_tensor(pe, 1)
            pe.wait_ge(s_mix, 1)
            for i in range(TT):
                ins = pe.transpose(Y[:, i, :], gth[:, i * 128:i * 128 + 128], ident)
            ins.then_inc(s_y, 1)
            norm_tensor(pe, 1)

        def stage1_scalar(act):
            for k, dst in enumerate((QcT, KcT)):
                act.wait_ge(s_p1, k + 1)
                act.activation(dst[:], psum[:, k, :], ACT.Identity,
                               bias=at["cols"][:, 2 + k:3 + k]).then_inc(s_p1c, 1)
            for i in range(TT):
                act.wait_ge(s_m1, i + 1)
                act.activation(P1[:, i, :], psum[:, 3 + i, :], ACT.Exp, bias=mx1[:, i:i + 1], scale=SCALE1,
                               accum_out=sm1[:, i:i + 1]).then_inc(s_e1, 1)
            for k in range(8):
                act.wait_ge(s_m2, k // 2 + 1)
                act.activation(P2[:, k, :], s2_at(k), ACT.Exp, bias=mx2[:, k:k + 1], scale=SCALE1,
                               accum_out=sm2[:, k:k + 1]).then_inc(s_e2, 1)
            for b in range(NB):
                act.wait_ge(s_t1, b + 1)
                act.activation(P1T[:, b, :, :].rearrange("p (a j) s -> p a (j s)", a=2),
                               psum[:, 3 + 2 * b:5 + 2 * b, :], ACT.Copy).then_inc(s_t1c, 1)
            act.wait_ge(s_t2, 2)
            for j in range(2):
                ins = act.activation(P2T[:, 1, j, :], psum[:, BK2[2 + j], :], ACT.Copy)
            ins.then_inc(s_t2c[1], 1)
            stage2_early_scalar(act)
            act.wait_ge(s_o1, 1)
            act.activation(c2s[:], psum[:, 3, :], ACT.Copy).then_inc(s_o1c, 1)
            act.wait_ge(s_g, 1)
            act.wait_ge(s_hbg, 1)
            act.activation(gth[:], psum[:, 6, :], ACT.Tanh, bias=hbg[:, 0:1], scale=0.5).then_inc(s_gt, 1)
            kv4_scalar(act, 1)
            norm_scalar(act, 1)

        def stage1_vector(dve):
            dve.tensor_scalar(hbg[:], at["cols"][:, 4:5], 0.5, None, ALU.mult).then_inc(s_hbg, 1)
            dve.wait_ge(s_p1, 3)
            dve.tensor_tensor(Vc[:], tiles(psum[:, 2, :]),
                              at["bvc"].rearrange("p (o d) -> p o d", o=1).broadcast_to([128, TT, D]),
                              ALU.add).then_inc(s_p1v, 1)
            for i in range(TT):
                dve.wait_ge(s_s1, i + 1)
                dstep(dve, dve.tensor_reduce(mx1[:, i:i + 1], psum[:, 3 + i, :], AX, ALU.max))
                dve.tensor_scalar(mx1[:, i:i + 1], mx1[:, i:i + 1], -SCALE1, None, ALU.mult).then_inc(s_m1, 1)
            for k in range(4):
                dve.wait_ge(s_s2, k + 1)
                m = mx2[:, 2 * k:2 * k + 2]
                dstep(dve, dve.tensor_reduce(m, psum[:, BK2[k], :].rearrange("p (a s) -> p a s", a=2), AX, ALU.max))
                dve.tensor_scalar(m, m, -SCALE1, None, ALU.mult).then_inc(s_m2, 1)
            dve.wait_ge(s_e1, TT)
            dstep(dve, dve.reciprocal(sm1[:], sm1[:]))
            for i in range(TT):
                dve.tensor_scalar(P1[:, i, :], P1[:, i, :], sm1[:, i:i + 1], None, ALU.mult).then_inc(s_n1, 1)
            dve.wait_ge(s_e2, 8)
            dstep(dve, dve.reciprocal(sm2[:], sm2[:]))
            for k in range(8):
                dve.tensor_scalar(P2[:, k, :], P2[:, k, :], sm2[:, k:k + 1], 0.5, ALU.mult,
                                  ALU.mult).then_inc(s_n2, 1)
            dve.wait_ge(s_t2, 1)
            dve.tensor_copy(P2T[:, 0, :, :], psum[:, 0:2, :]).then_inc(s_t2c[0], 1)
            for b in range(NB):
                dve.wait_ge(s_o2, b + 1)
                dve.tensor_reduce(s2c[:, b * S:b * S + S], psum[:, 4 + b, :].rearrange("p (s o) -> p s o", o=2),
                                  AX, ALU.add).then_inc(s_o2c, 1)
            dve.wait_ge(s_o2c, 2)
            dve.wait_ge(s_o1c, 1)
            dstep(dve, dve.tensor_tensor(dif[:], c2s[:], s2c[:], ALU.subtract))
            dve.wait_ge(s_gt, 1)
            dstep(dve, dve.scalar_tensor_tensor(gth[:], gth[:], 1.0, dif[:], ALU.add, ALU.mult))
            dve.scalar_tensor_tensor(gth[:], gth[:], 0.5, s2c[:], ALU.mult, ALU.add).then_inc(s_mix, 1)
            norm_vector(dve, 1, x_tok[:])
            norm_lo(dve, 1)
            kv4_vector(dve, 1)

        def stage1_pool(pool):
            constants_pool(pool)
            norm_pool(pool, 1)

        early.close()

        Qrh = sb("q4_w_hi", [128, 4 * D], F32R, stack=late4)
        Qrl = sb("q4_w_lo", [128, 4 * D], F32R, stack=late4)
        xq = sb("q4_biased", [128, T], stack=late4)
        rq = sb("q4_rounded", [128, T], F32R, stack=late4)
        yq = sb("q4_split", [128, T], stack=late4)
        Qx = sb("q4_heads", [128, 2, 4, T], F32R, stack=late4)
        mxt = sb("max4", [128, TT, 128], stack=late4)
        PT4 = sb("probs4_T", [128, 4, 512], stack=late4)
        rs4 = sb("sums4_inverse", [128, TT, 4], stack=late4)
        att4 = sb("attended4", [128, TT, D], stack=late4)
        aT4 = sb("attended4_T", [128, T], stack=late4)


        s_raw = [sem(f"pair_loaded_{i}") for i in range(4)]
        s_const = sem("rounded_constants")
        s_whi = sem("pair_hi_made")
        s_wlo = sem("pair_lo_made")
        s_lg = sem("logits")
        s_th = sem("logits_tanh")
        s_pg = sem("pair_gate")
        s_pu = sem("pair_up")
        s_pc = sem("pair_weights_spread")
        s_silu = sem("pair_silu")
        s_h1 = sem("pair_h_unweighted")
        s_h = sem("pair_h")
        s_d = sem("pair_down")
        s_comb = sem("combine_weights")
        s_cT = sem("combine_weights_T")
        s_combT = sem("combine_weights_T_copied")
        LOOPS = (NP - 4) // 4

        def bc(ap, n):
            return ap.rearrange("p (a o) -> p a o", o=1).broadcast_to([128, ap.shape[1], n])

        def top_k(dve, v, n, k, reset):
            f = selg[:, 0:TT * n].rearrange("p (t e) -> p t e", t=TT)
            g_, e_, c_ = (a[:, 0:TT * n].rearrange("p (t e) -> p t e", t=TT) for a in (gt, eq, cum))
            for i in range(TT):
                ins = dve.max(m8[:, i, :], v[:, i, :])
            dstep(dve, ins)
            thr = m8[:, :, k - 1:k].broadcast_to([128, TT, n])
            dve.tensor_tensor(g_, v, thr, ALU.is_gt)
            dstep(dve, dve.tensor_tensor(e_, v, thr, ALU.is_equal))
            dve.tensor_tensor_scan(cum[:, 0:TT * n], reset, eq[:, 0:TT * n], 0.0, ALU.mult, ALU.add)
            dstep(dve, dve.tensor_reduce(cnt[:], g_, AX, ALU.add))
            dstep(dve, dve.tensor_scalar(cnt[:], cnt[:], -1.0, float(k), ALU.mult, ALU.add))
            dstep(dve, dve.tensor_tensor(c_, c_, bc(cnt[:], n), ALU.is_le))
            dstep(dve, dve.tensor_tensor(e_, e_, c_, ALU.mult))
            dstep(dve, dve.tensor_tensor(f, e_, g_, ALU.add))
            return f

        def normalised(dve, v, chosen, n, eps):
            c_ = comb[:].rearrange("p t e -> p (t e)")[:, 0:TT * n].rearrange("p (t e) -> p t e", t=TT)
            dstep(dve, dve.tensor_tensor(c_, v, chosen, ALU.mult))
            dstep(dve, dve.tensor_reduce(wsum[:], c_, AX, ALU.add))
            if eps:
                dstep(dve, dve.tensor_scalar(wsum[:], wsum[:], eps, None, ALU.add))
            dstep(dve, dve.reciprocal(wsum[:], wsum[:]))
            dstep(dve, dve.tensor_tensor(c_, c_, bc(wsum[:], n), ALU.mult))
            return c_

        def stage2_load(sp, p, slot):
            sp.dma_start(raw[:, slot, :], stream[p + 1, :, :]).then_inc(s_raw[slot], 16)

        def stage2_sync(sp):
            for p in range(-1, 3):
                stage2_load(sp, p, p % 4)
            with sp.Fori(0, LOOPS) as it:
                for j in range(4):
                    sp.wait_ge(s_d, it * 4 + j + 1)
                    stage2_load(sp, it * 4 + j + 3, (j + 3) % 4)
            sp.wait_ge(s_d, NP - 3)
            stage2_load(sp, NP - 1, (NP - 1) % 4)

        def constants_pool(pool):
            pool.wait_ge(s_in["route"], 16)
            pstep(pool, pool.tensor_copy(gwh[:], at["gw"]))
            pool.tensor_tensor(gwl[:], at["gw"], gwh[:].bitcast(F32), ALU.subtract)
            pstep(pool, pool.tensor_copy(rwh[:], at["rw"]))
            pool.tensor_tensor(rwl[:], at["rw"], rwh[:].bitcast(F32), ALU.subtract)
            pool.tensor_copy(identr[:], ident)
            pool.wait_ge(s_in["heads"], 16)
            pool.tensor_copy(causr[:], at["causal"]).then_inc(s_const, 1)

        def pair_lo(pool, p, slot):
            pool.wait_ge(s_whi, p + 2)
            pool.tensor_tensor(wlo[:, slot, :], raw[:, slot, 0:256], whi[:, slot, 0:256].bitcast(F32),
                               ALU.subtract).then_inc(s_wlo, 1)

        def stage2_pool(pool):
            for p in range(-1, 1):
                pair_lo(pool, p, p % 4)
            with pool.Fori(0, LOOPS) as it:
                for j in range(4):
                    pair_lo(pool, it * 4 + j + 1, (j + 1) % 4)
            for p in range(NP - 3, NP):
                pair_lo(pool, p, p % 4)
            norm_pool(pool, 2)

        def pair_hi(act, q, slot, turn):
            act.wait_ge(s_raw[slot], turn * 16 + 16)
            act.activation(whi[:, slot, :], raw[:, slot, 0:384], ACT.Copy).then_inc(s_whi, 1)

        def pair_silu(act, p, par):
            act.wait_ge(s_pg, p + 2)
            act.wait_ge(s_h1, p)
            act.activation(sg[:, par, :], psum[:, par, :], ACT.Silu).then_inc(s_silu, 1)

        def stage2_early_scalar(act):
            pair_hi(act, -1, 3, 0)
            pair_hi(act, 0, 0, 0)
            pair_hi(act, 1, 1, 0)

        def stage2_scalar(act):
            act.wait_ge(s_lg, 1)
            act.activation(score[:], psum[:, 5, 0:TT * E0].rearrange("p (t e) -> p t e", t=TT), ACT.Tanh,
                           scale=0.5).then_inc(s_th, 1)
            act.wait_ge(s_pg, 1)
            act.activation(sg[:, 1, :], psum[:, 1, :], ACT.Silu).then_inc(s_silu, 1)
            pair_hi(act, 2, 2, 0)
            pair_silu(act, 0, 0)
            act.wait_ge(s_cT, 1)
            act.activation(combT[:], psum[:, 6, :], ACT.Copy).then_inc(s_combT, 1)
            act.wait_ge(s_pu, 1)
            with act.Fori(0, LOOPS) as it:
                for j in range(4):
                    q = (j + 3) % 4
                    act.wait_ge(s_pc, it * 4 + j)
                    pair_hi(act, None, q, it + 1)
                    pair_silu(act, it * 4 + j + 1, (j + 1) % 2)
            act.wait_ge(s_pc, NP - 4)
            pair_hi(act, NP - 1, 3, NP // 4)
            for p in range(NP - 3, NP):
                pair_silu(act, p, p % 2)
            norm_scalar(act, 2)

        def pair_h1(dve, p, par):
            dve.wait_ge(s_silu, p + 2)
            dve.wait_ge(s_pu, p + 2)
            dve.tensor_tensor(h1[:, par, :], psum[:, 2 + par, :], sg[:, par, :], ALU.mult).then_inc(s_h1, 1)

        def pair_h(dve, p, par):
            dve.wait_ge(s_pc, p + 1)
            dve.wait_ge(s_h1, p + 2)
            dve.wait_ge(s_d, p)
            dve.tensor_tensor(hh[:, par, :], psum[:, 4 + par, :], h1[:, par, :], ALU.mult).then_inc(s_h, 1)

        def stage2_vector(dve):
            dve.wait_ge(s_th, 1)
            dve.wait_ge(s_in["route"], 16)
            dstep(dve, dve.tensor_scalar(score[:], score[:], 0.5, 0.5, ALU.mult, ALU.add))
            dstep(dve, dve.tensor_tensor(score[:], score[:],
                                         at["gbias"].rearrange("p (o e) -> p o e", o=1).broadcast_to([128, TT, E0]),
                                         ALU.add))
            by_group = score[:].rearrange("p t (g e) -> p (t g) e", g=G0)
            dstep(dve, dve.tensor_reduce(gsc[:].rearrange("p t g -> p (t g)"), by_group, AX, ALU.max))
            top_k(dve, gsc[:], G0, TG0, at["reset8"])
            dstep(dve, dve.tensor_tensor(by_group, by_group, bc(selg[:, 0:TT * G0], E0 // G0), ALU.mult))
            chosen = top_k(dve, score[:], E0, K0, at["reset64"])
            normalised(dve, score[:], chosen, E0, 1e-8)
            dstep(dve, dve.tensor_copy(combhl[:, :, 0:E0].bitcast(F32R), comb[:]))
            dve.tensor_tensor(combhl[:, :, E0:2 * E0], comb[:], combhl[:, :, 0:E0], ALU.subtract).then_inc(s_comb, 1)
            pair_h1(dve, -1, 1)
            dve.wait_ge(s_h1, 1)
            dve.tensor_copy(hh[:, 1, :], h1[:, 1, :]).then_inc(s_h, 1)
            pair_h1(dve, 0, 0)
            pair_h(dve, 0, 0)
            with dve.Fori(0, LOOPS) as it:
                for j in range(4):
                    pair_h1(dve, it * 4 + j + 1, (j + 1) % 2)
                    pair_h(dve, it * 4 + j + 1, (j + 1) % 2)
            for p in range(NP - 3, NP):
                pair_h1(dve, p, p % 2)
                pair_h(dve, p, p % 2)
            norm_vector(dve, 2, x_tok[:])
            norm_lo(dve, 2)

        def pair_gate_up(pe, p, slot, par):
            pe.wait_ge(s_wlo, p + 2)
            if not isinstance(p, int) or p > 0:
                pe.wait_ge(s_h, p)
            three(pe, psum[:, par, :], whi[:, slot, 0:128], wlo[:, slot, 0:128], xh[:], xl[:]).then_inc(s_pg, 1)
            three(pe, psum[:, 2 + par, :], whi[:, slot, 128:256], wlo[:, slot, 128:256], xh[:], xl[:]).then_inc(s_pu, 1)

        def pair_spread(pe, slot, par):
            pe.matmul(psum[:, 4 + par, :], whi[:, slot, 256:384], combT[:], start=True, stop=True).then_inc(s_pc, 1)

        def pair_down(pe, p, slot, par, first=False, last=False, done=s_d):
            pe.wait_ge(s_h, p + 2)
            for i in range(TT):
                ins = pe.matmul(Y[:, i, :], hh[:, par, i * 128:i * 128 + 128], raw[:, slot, 384:512],
                                start=first and i == 0, stop=last, skip_group_check=True)
            ins.then_inc(done, 1)

        def stage2_tensor(pe):
            pe.wait_ge(s_xh, 2)
            pe.wait_ge(s_const, 1)
            pe.wait_ge(s_xl, 1)
            for i in range(TT):
                t = slice(i * 128, i * 128 + 128)
                ins = three(pe, psum[:, 5, i * E0:i * E0 + E0], xh[:, t], xl[:, t], gwh[:], gwl[:])
            ins.then_inc(s_lg, 1)
            pair_gate_up(pe, -1, 3, 1)
            pair_gate_up(pe, 0, 0, 0)
            pe.wait_ge(s_comb, 1)
            for i in range(TT):
                ins = pe.transpose(psum[:, 6, i * 128:i * 128 + 128], combhl[:, i, :], ident)
            ins.then_inc(s_cT, 1)
            pe.wait_ge(s_combT, 1)
            pair_spread(pe, 0, 0)
            pair_down(pe, -1, 3, 1, first=True)
            with pe.Fori(0, LOOPS) as it:
                for j in range(4):
                    pair_gate_up(pe, it * 4 + j + 1, (j + 1) % 4, (j + 1) % 2)
                    pair_spread(pe, (j + 1) % 4, (j + 1) % 2)
                    pair_down(pe, it * 4 + j, j, j % 2)
            for p in range(NP - 3, NP):
                pair_gate_up(pe, p, p % 4, p % 2)
                pair_spread(pe, p % 4, p % 2)
                pair_down(pe, p - 1, (p - 1) % 4, (p - 1) % 2)
            pair_down(pe, NP - 1, (NP - 1) % 4, (NP - 1) % 2, last=True, done=s_y)
            norm_tensor(pe, 2)

        wsr = sb("head_w_raw", [128, 2, 384], stack=late)
        wsh = sb("head_w_hi", [128, 384], F32R, stack=late)
        wsl = sb("head_w_lo", [128, 384], F32R, stack=late)
        QH = sb("q_hi", [128, T], F32R, stack=late)
        QL = sb("q_lo", [128, T], F32R, stack=late)
        KH = sb("k_hi", [128, NB, 2, S], F32R, stack=late)
        KL = sb("k_lo", [128, NB, 2, S], F32R, stack=late)
        Vv = sb("v_heads", [128, 2, TT, 128], stack=late)
        PL = sb("probs_late", [128, 4, S], stack=late)
        PE_ = sb("probs_early", [128, 4, 128], stack=late)
        PTs = sb("probs_heads_T", [128, 3, 512], stack=late)
        nmx = sb("minus_max", [128, 8], stack=late)
        sums = sb("prob_sums", [128, 2, 8], stack=late)
        rsum = sb("prob_sums_inverse", [128, 8], stack=late)
        On = sb("attended_normed", [128, 8, KQ], stack=late)
        OTs = sb("attended_T", [128, T], stack=late)
        SCALE3 = 1.0 / float(np.sqrt(KQ))

        s_wsr = [sem(f"head_w_loaded_{i}") for i in range(2)]
        s_wsh = sem("head_w_hi_made")
        s_ws = sem("head_w_made")
        s_jq = sem("head_q")
        s_jk = sem("head_k")
        s_jv = sem("head_v")
        s_qh = sem("head_q_hi")
        s_kh = sem("head_k_hi")
        s_ql = sem("head_q_lo")
        s_kl = sem("head_k_lo")
        s_vv = sem("head_v_copied")
        s_S = sem("head_scores")
        s_mx = sem("head_max")
        s_nm = sem("head_minus_max")
        s_ex = sem("head_exp")
        s_pt = sem("head_probs_T")
        s_pta = sem("head_probs_T_copied_act")
        s_ptd = sem("head_probs_T_copied_dve")
        s_pv = sem("head_attended")
        s_rs = sem("head_sums_inverted")
        s_on = sem("head_normed")
        s_otp = sem("head_attended_T")
        s_ot = sem("head_attended_T_copied")
        heads_o = at["wo"].rearrange("p (n w) -> p n w", n=HP)
        TILE_OF = (1, 3, 0, 2)
        sc_late = lambda b: psum[:, 3 + b, :].rearrange("p (h m) -> p h m", h=2)
        sc_early = psum[:, 5, :].rearrange("p (b h m) -> p b h m", b=NB, h=2)

        def stage3_load(sp, n, slot):
            sp.dma_start(wsr[:, slot, :], heads_w[n, :, :]).then_inc(s_wsr[slot], 16)

        def stage3_sync(sp):
            sp.wait_ge(s_xn, 2)
            stage3_load(sp, 0, 0)
            stage3_load(sp, 1, 1)
            with sp.Fori(0, HP // 2 - 1) as it:
                for j in range(2):
                    sp.wait_ge(s_ws, it * 2 + j + 1)
                    stage3_load(sp, it * 2 + j + 2, j)

        def stage3_pool(pool):
            pstep(pool, pool.memset(one1[:], 1.0))
            with pool.Fori(0, HP // 2) as it:
                for j in range(2):
                    n = it * 2 + j
                    pool.wait_ge(s_wsr[j], it * 16 + 16)
                    pool.wait_ge(s_jv, n)
                    pool.tensor_tensor(wsh[:], wsr[:, j, :], one1[:].broadcast_to([128, 384]), ALU.mult).then_inc(s_wsh, 1)
                    pool.wait_ge(s_wsh, n + 1)
                    pool.tensor_tensor(wsl[:], wsr[:, j, :], wsh[:].bitcast(F32), ALU.subtract).then_inc(s_ws, 1)
            norm_pool(pool, 3)

        def head_project(pe, n):
            pe.wait_ge(s_ws, n + 1)
            pe.wait_ge(s_vv, n)
            three(pe, psum[:, 0, :], wsh[:, 0:128], wsl[:, 0:128], xh[:], xl[:]).then_inc(s_jq, 1)
            three(pe, psum[:, 1, :], wsh[:, 128:256], wsl[:, 128:256], xh[:], xl[:]).then_inc(s_jk, 1)
            for i in range(TT):
                t = slice(i * 128, i * 128 + 128)
                ins = three(pe, psum[:, 2, t], xh[:, t], xl[:, t], wsh[:, 256:384], wsl[:, 256:384])
            ins.then_inc(s_jv, 1)

        def head_scores(pe, n):
            pe.wait_ge(s_ql, n + 1)
            pe.wait_ge(s_kl, n + 1)
            for b in range(NB):
                q = slice(b * S + 128, b * S + 256)
                o_ = sc_late(b)
                three(pe, o_, QH[:, q], QL[:, q], KH[:, b, :, :], KL[:, b, :, :], stop=False)
                pe.matmul(o_[:, :, 128:256], identr[:],
                          causr[:].rearrange("p (o m) -> p o m", o=1).broadcast_to([128, 2, 128]),
                          start=False, stop=True)
                q = slice(b * S, b * S + 128)
                o_ = sc_early[:, b, :, :]
                three(pe, o_, QH[:, q], QL[:, q], KH[:, b, :, 0:128], KL[:, b, :, 0:128], stop=False)
                ins = pe.matmul(o_, identr[:],
                                causr[:].rearrange("p (o m) -> p o m", o=1).broadcast_to([128, 2, 128]),
                                start=False, stop=True)
            ins.then_inc(s_S, 1)

        def head_turn(pe, n):
            pe.wait_ge(s_ex, n + 1)
            for b in range(NB):
                for h in range(2):
                    k = 2 * b + h
                    pe.transpose(psum[:, b, h * S:h * S + 128], PE_[:, k, :], ident)
                    pe.transpose(psum[:, b, h * S + 128:h * S + 256], PL[:, k, 0:128], ident)
            for k in range(4):
                ins = pe.transpose(psum[:, 2, k * 128:k * 128 + 128], PL[:, k, 128:256], ident)
            ins.then_inc(s_pt, 1)

        def head_attend(pe, n, par):
            pe.wait_ge(s_pta, n + 1)
            pe.wait_ge(s_ptd, n + 1)
            for late in (1, 0):
                for b in range(NB):
                    for h in range(2):
                        k = 2 * b + h
                        o_ = psum[:, 6, (k + 4 * (1 - late)) * KQ:(k + 4 * (1 - late)) * KQ + KQ]
                        c = h * S + 128 * late
                        v = slice(h * KQ, h * KQ + KQ)
                        ins = pe.matmul(o_, PTs[:, b, c:c + 128], Vv[:, par, 2 * b, v], start=True, stop=not late)
                        if late:
                            ins = pe.matmul(o_, PTs[:, 2, k * 128:k * 128 + 128], Vv[:, par, 2 * b + 1, v],
                                            start=False, stop=True)
            ins.then_inc(s_pv, 1)

        def head_output(pe, n, last=False):
            pe.wait_ge(s_on, n + 1)
            for k in range(4):
                c = TILE_OF[k] * 128
                ins = pe.transpose(psum[:, 6, c:c + 128], On[:, 2 * k:2 * k + 2, :].rearrange("p a d -> p (a d)"), ident)
            ins.then_inc(s_otp, 1)
            pe.wait_ge(s_ot, n + 1)
            for i in range(TT):
                ins = pe.matmul(Y[:, i, :], OTs[:, i * 128:i * 128 + 128], heads_o[:, n, :],
                                start=False, stop=last, skip_group_check=True)
            if last:
                ins.then_inc(s_y, 1)

        def stage3_tensor(pe):
            pe.wait_ge(s_xh, 3)
            pe.matmul(psum[:, 7, :], ident, x_tok[:].rearrange("p t d -> p (t d)"), start=True, stop=False,
                      skip_group_check=True)
            pe.wait_ge(s_xl, 2)
            head_project(pe, 0)
            head_scores(pe, 0)
            head_project(pe, 1)

            def body(n, par, scores=True, project=True):
                pe.wait_ge(s_vv, n + 2 if scores else n + 1)
                if scores:
                    pe.wait_ge(s_ql, n + 2)
                    pe.wait_ge(s_kl, n + 2)
                head_turn(pe, n)
                if scores:
                    head_scores(pe, n + 1)
                head_attend(pe, n, par)
                if project:
                    head_project(pe, n + 2)
                head_output(pe, n, last=not scores)

            with pe.Fori(0, (HP - 2) // 2) as it:
                for j in range(2):
                    body(it * 2 + j, j)
            body(HP - 2, 0, project=False)
            body(HP - 1, 1, scores=False, project=False)
            norm_tensor(pe, 3)

        def head_hi(act, n):
            act.wait_ge(s_jq, n + 1)
            act.wait_ge(s_S, n)
            act.activation(QH[:], psum[:, 0, :], ACT.Copy).then_inc(s_qh, 1)
            act.wait_ge(s_jk, n + 1)
            for h in range(2):
                ins = act.activation(KH[:, :, h, :], psum[:, 1, :].rearrange("p (b m) -> p b m", b=NB), ACT.Copy,
                                     scale=at["half"][:, h:h + 1])
            ins.then_inc(s_kh, 1)

        def head_exps(act, n, par):
            act.wait_ge(s_nm, n + 1)
            act.wait_ge(s_pt, n)
            for k in range(4):
                act.activation(PL[:, k, :], sc_late(k // 2)[:, k % 2, :], ACT.Exp, bias=nmx[:, k:k + 1],
                               scale=SCALE3, accum_out=sums[:, par, k:k + 1])
            for k in range(4):
                ins = act.activation(PE_[:, k, :], sc_early[:, k // 2, k % 2, :], ACT.Exp,
                                     bias=nmx[:, 4 + k:5 + k], scale=SCALE3, accum_out=sums[:, par, 4 + k:5 + k])
            ins.then_inc(s_ex, 1)

        def stage3_scalar(act):
            head_hi(act, 0)
            head_exps(act, 0, 0)
            head_hi(act, 1)

            def body(n, par, scores=True, project=True):
                act.wait_ge(s_pt, n + 1)
                act.activation(PTs[:, 0, :], psum[:, 0, :], ACT.Copy).then_inc(s_pta, 1)
                if scores:
                    head_exps(act, n + 1, 1 - par)
                if project:
                    head_hi(act, n + 2)
                act.wait_ge(s_otp, n + 1)
                act.activation(OTs[:], psum[:, 6, :], ACT.Copy).then_inc(s_ot, 1)

            with act.Fori(0, (HP - 2) // 2) as it:
                for j in range(2):
                    body(it * 2 + j, j)
            body(HP - 2, 0, project=False)
            body(HP - 1, 1, scores=False, project=False)
            norm_scalar(act, 3)

        def head_lo(dve, n, par):
            dve.wait_ge(s_qh, n + 1)
            dve.tensor_tensor(QL[:], psum[:, 0, :], QH[:].bitcast(F32), ALU.subtract).then_inc(s_ql, 1)
            dve.wait_ge(s_kh, n + 1)
            for h in range(2):
                ins = dve.scalar_tensor_tensor(KL[:, :, h, :], psum[:, 1, :].rearrange("p (b m) -> p b m", b=NB),
                                               at["half"][:, h:h + 1], KH[:, :, h, :].bitcast(F32),
                                               ALU.mult, ALU.subtract)
            ins.then_inc(s_kl, 1)
            dve.wait_ge(s_jv, n + 1)
            dve.tensor_copy(Vv[:, par, :, :], tiles(psum[:, 2, :])).then_inc(s_vv, 1)

        def head_max(dve, n):
            dve.wait_ge(s_S, n + 1)
            dve.tensor_reduce(nmx[:, 0:4], psum[:, 3:5, :].rearrange("p a (h m) -> p (a h) m", h=2), AX, ALU.max)
            dve.tensor_reduce(nmx[:, 4:8], sc_early.rearrange("p b h m -> p (b h) m"), AX, ALU.max).then_inc(s_mx, 1)
            dve.wait_ge(s_mx, n + 1)
            dve.tensor_scalar(nmx[:], nmx[:], -SCALE3, None, ALU.mult).then_inc(s_nm, 1)

        def stage3_vector(dve):
            head_lo(dve, 0, 0)
            head_max(dve, 0)
            head_lo(dve, 1, 1)

            def body(n, par, scores=True, project=True):
                dve.wait_ge(s_pt, n + 1)
                dve.tensor_copy(PTs[:, 1:3, :], psum[:, 1:3, :]).then_inc(s_ptd, 1)
                dve.reciprocal(rsum[:], sums[:, par, :]).then_inc(s_rs, 1)
                if scores:
                    head_max(dve, n + 1)
                dve.wait_ge(s_pv, n + 1)
                dve.wait_ge(s_rs, n + 1)
                dve.tensor_tensor(On[:], psum[:, 6, :].rearrange("p (k d) -> p k d", d=KQ), bc(rsum[:], KQ),
                                  ALU.mult).then_inc(s_on, 1)
                if project:
                    head_lo(dve, n + 2, par)

            with dve.Fori(0, (HP - 2) // 2) as it:
                for j in range(2):
                    body(it * 2 + j, j)
            body(HP - 2, 0, project=False)
            body(HP - 1, 1, scores=False, project=False)
            norm_vector(dve, 3, None)
            norm_lo(dve, 3)

        SCALE4 = 1.0 / float(np.sqrt(np.float32(HD)))

        s_qw = sem("q4_w_split")
        s_mz = sem("max4_cleared")
        s_qp = sem("q4_projected")
        s_qe = sem("q4_copied")
        s_qy = sem("q4_split_made")
        s_qx = sem("q4_heads_made")
        s_xs = sem("scores4_by_query")
        s_xm = sem("max4_taken")
        s_xt = sem("max4_T")
        s_xqa = sem("max4_in_operand_act")
        s_xqd = sem("max4_in_operand_dve")
        s_ST = sem("scores4_by_key")
        s_xe = sem("exp4")
        s_xp = sem("attended4_summed")
        s_xr = sem("sums4_inverted")
        s_xo = sem("attended4_normed")
        s_x4t = sem("attended4_turned")
        s_x4c = sem("attended4_turned_copied")
        O4 = psum[:, 6, 0:TT * 4 * (HD + 1)].rearrange("p (t h d) -> p t h d", t=TT, h=4)

        def stage4_pool(pool):
            pool.memset(mxt[:], 0.0).then_inc(s_mz, 1)
            pstep(pool, pool.tensor_copy(Qrh[:], at["Qr_w"]))
            pool.tensor_tensor(Qrl[:], at["Qr_w"], Qrh[:].bitcast(F32), ALU.subtract).then_inc(s_qw, 1)
            pool.wait_ge(s_xn, 4)
            pool.tensor_tensor(res[:], x_tok[:],
                               at["bo"].rearrange("p (o d) -> p o d", o=1).broadcast_to([128, TT, D]),
                               ALU.add).then_inc(s_res, 1)
            for t in range(1, 4):
                pool.wait_ge(s_qy, t + 1)
                for j in range(4):
                    ins = pool.tensor_scalar(Qx[:, t % 2, j, :], yq[:], at["sel"][:, SEL_HEAD + j:SEL_HEAD + j + 1],
                                             at["sel"][:, SEL_MASK:SEL_MASK + 1], ALU.mult, ALU.add)
                ins.then_inc(s_qx, 1)
            norm_pool(pool, 4)

        def q4_project(pe, t):
            if t:
                pe.wait_ge(s_xqa, t)
                pe.wait_ge(s_xqd, t)
            w = slice(t * D, t * D + D)
            three(pe, psum[:, 7, :], Qrh[:, w], Qrl[:, w], xh[:], xl[:]).then_inc(s_qp, 1)

        def q4_scores(pe, t, j, u):
            w = 16 * t + 4 * j + u
            if j == 0 and u == 0:
                pe.wait_ge(s_qx, t + 1)
            if w >= 4:
                pe.wait_ge(s_xm, (w - 4) // 2 + 1)
            pe.matmul(psum[:, u, :], Qx[:, t % 2, j, u * 128:u * 128 + 128], KX[:, t, u // 2 * SC:u // 2 * SC + SC],
                      start=True, stop=True).then_inc(s_xs, 1)

        def q4_turn(pe, t):
            pe.wait_ge(s_xm, 8 * (t + 1))
            for i in range(TT):
                ins = pe.transpose(psum[:, 7, i * 128:i * 128 + 128], mxt[:, i, :], ident)
            ins.then_inc(s_xt, 1)

        def k4_scores(pe, t, j, u):
            n, b = 16 * t + 4 * j + u, u // 2
            if j == 0 and u == 0:
                pe.wait_ge(s_xqa, t + 1)
                pe.wait_ge(s_xqd, t + 1)
            if n >= 2:
                pe.wait_ge(s_xe, n - 1)
            for a in range(2):
                k = b * SC + (u % 2 * 2 + a) * 128
                ins = pe.matmul(psum[:, 4 + u % 2, a * S:a * S + S], KX[:, t, k:k + 128],
                                Qx[:, t % 2, j, b * S:b * S + S], start=True, stop=True)
            ins.then_inc(s_ST, 1)

        def v4_attend(pe, t, j, b):
            m = 8 * t + 2 * j + b
            pe.wait_ge(s_xe, 2 * m + 2)
            if m == 8 * t and t:
                pe.wait_ge(s_xo, t)
            for q in range(2):
                for a in range(4):
                    c = a % 2 * S + q * 128
                    ins = pe.matmul(O4[:, 2 * b + q, j, :], PT4[:, (2 * m + a // 2) % 4, c:c + 128],
                                    Vx[:, 4 * b + a, 4 * t + j, :], start=a == 0, stop=a == 3)
            ins.then_inc(s_xp, 1)

        def stage4_tensor(pe):
            pe.wait_ge(s_xh, 4)
            pe.wait_ge(s_xl, 3)
            pe.wait_ge(s_qw, 1)
            pe.wait_ge(s_kx, 1)
            pe.wait_ge(s_mz, 1)
            q4_project(pe, 0)
            for j in range(4):
                for u in range(4):
                    q4_scores(pe, 0, j, u)
            q4_turn(pe, 0)
            for t in range(4):
                if t < 3:
                    q4_project(pe, t + 1)
                for j in range(4):
                    for u in range(4):
                        if t < 3:
                            q4_scores(pe, t + 1, j, u)
                        k4_scores(pe, t, j, u)
                        if u == 0 and (t or j):
                            v4_attend(pe, *divmod(4 * t + j - 1, 4), 1)
                        if u == 2:
                            v4_attend(pe, t, j, 0)
                if t < 3:
                    q4_turn(pe, t + 1)
            v4_attend(pe, 3, 3, 1)
            pe.wait_ge(s_xo, 4)
            for i in range(TT):
                ins = pe.transpose(psum[:, 0, i * 128:i * 128 + 128], att4[:, i, :], ident)
            ins.then_inc(s_x4t, 1)
            pe.wait_ge(s_x4c, 1)
            for i in range(TT):
                ins = pe.matmul(Y[:, i, :], aT4[:, i * 128:i * 128 + 128], at["O_w"], start=True, stop=True)
            ins.then_inc(s_y, 1)
            norm_tensor(pe, 4)

        def stage4_scalar(act):
            act.wait_ge(s_in["masked"], 16)

            def q_copy(t):
                act.wait_ge(s_qp, t + 1)
                if t:
                    act.wait_ge(s_qy, t)
                act.activation(xq[:], psum[:, 7, :], ACT.Identity, bias=at["qb"][:, t:t + 1]).then_inc(s_qe, 1)

            def put_max(t):
                act.wait_ge(s_xt, t + 1)
                act.wait_ge(s_xqd, t + 1)
                for j in range(2):
                    ins = act.activation(Qx[MR:128, t % 2, j, :], psum[MR:128, 7, :], ACT.Identity,
                                         scale=at["sel"][MR:128, SEL_MAX + j:SEL_MAX + j + 1],
                                         bias=at["sel"][MR:128, SEL_MASK:SEL_MASK + 1])
                ins.then_inc(s_xqa, 1)

            q_copy(0)
            put_max(0)
            for t in range(4):
                if t < 3:
                    q_copy(t + 1)
                for k in range(16):
                    n = 16 * t + k
                    act.wait_ge(s_ST, n + 1)
                    if n >= 4:
                        act.wait_ge(s_xp, (n - 4) // 2 + 1)
                    act.activation(PT4[:, n % 4, :], psum[:, 4 + n % 2, :], ACT.Exp, scale=SCALE4).then_inc(s_xe, 1)
                if t < 3:
                    put_max(t + 1)
            act.wait_ge(s_x4t, 1)
            act.activation(aT4[:], psum[:, 0, :], ACT.Copy).then_inc(s_x4c, 1)
            norm_scalar(act, 4)

        def stage4_vector(dve):
            dve.wait_ge(s_mz, 1)

            def q_split(t):
                dve.wait_ge(s_qe, t + 1)
                dstep(dve, dve.tensor_copy(rq[:], xq[:]))
                if t > 1:
                    dve.wait_ge(s_qx, t)
                ins = dve.scalar_tensor_tensor(yq[:], rq[:].bitcast(F32), at["sel"][:, SEL_LO_Q:SEL_LO_Q + 1],
                                               xq[:], ALU.mult, ALU.add)
                ins.then_inc(s_qy, 1)

            def maxima(t, j, between=None):
                for b in range(NB):
                    dve.wait_ge(s_xs, 16 * t + 4 * j + 2 * b + 2)
                    if t and not j and not b:
                        dve.wait_ge(s_xt, t)
                    dve.tensor_reduce(mxt[:, 2 * b:2 * b + 2, MR + j], psum[:, 2 * b:2 * b + 2, :], AX,
                                      ALU.max).then_inc(s_xm, 1)
                    if between is not None and b == 0:
                        norm_heads(between)

            def put_max(t):
                dve.wait_ge(s_xt, t + 1)
                for j in range(2, 4):
                    ins = dve.tensor_scalar(Qx[MR:128, t % 2, j, :], psum[MR:128, 7, :],
                                            at["sel"][MR:128, SEL_MAX + j:SEL_MAX + j + 1],
                                            at["sel"][MR:128, SEL_MASK:SEL_MASK + 1], ALU.mult, ALU.add)
                ins.then_inc(s_xqd, 1)

            def norm_heads(t):
                dve.wait_ge(s_xp, 8 * (t + 1))
                dve.reciprocal(rs4[:], O4[:, :, :, HD]).then_inc(s_xr, 1)
                dve.wait_ge(s_xr, t + 1)
                dve.tensor_tensor(att4[:, :, t * 32:t * 32 + 32].rearrange("p t (h d) -> p t h d", h=4),
                                  O4[:, :, :, 0:HD],
                                  rs4[:].rearrange("p t (h o) -> p t h o", o=1).broadcast_to([128, TT, 4, HD]),
                                  ALU.mult).then_inc(s_xo, 1)

            q_split(0)
            dve.wait_ge(s_qy, 1)
            for j in range(4):
                ins = dve.tensor_scalar(Qx[:, 0, j, :], yq[:], at["sel"][:, SEL_HEAD + j:SEL_HEAD + j + 1],
                                        at["sel"][:, SEL_MASK:SEL_MASK + 1], ALU.mult, ALU.add)
            ins.then_inc(s_qx, 1)
            for j in range(4):
                maxima(0, j)
            put_max(0)
            for t in range(4):
                if t < 3:
                    q_split(t + 1)
                    for j in range(4):
                        maxima(t + 1, j, between=t - 1 if j == 0 and t else None)
                    put_max(t + 1)
                elif t:
                    norm_heads(t - 1)
            norm_heads(3)
            dve.wait_ge(s_res, 2)
            norm_vector(dve, 4, res[:])
            norm_lo(dve, 4)

        late.close()
        dsr = sb("expert_raw", [128, 2, EW], stack=late5)
        fch = sb("expert_up_hi", [128, 2, H1], F32R, stack=late5)
        fcl = sb("expert_up_lo", [128, 2, H1], F32R, stack=late5)
        hT = sb("expert_hidden", [128, 2, HC, T], stack=late5)
        acc = sb("experts_summed", [128, TT, D], stack=late5)
        p5 = sb("probs5", [128, TT, E1], stack=late5)
        mx5 = sb("max5", [128, TT], stack=late5)
        cT5 = sb("combine5_T", [E1, T], stack=late5)

        s_ds = [sem(f"expert_loaded_{i}") for i in range(2)]
        s_fh = sem("expert_up_hi_made")
        s_fl = sem("expert_up_lo_made")
        s_l5 = sem("logits5")
        s_d5 = sem("logits5_less_max")
        s_e5 = sem("exp5")
        s_c5 = sem("combine5")
        s_c5t = sem("combine5_turned")
        s_c5c = sem("combine5_turned_copied")
        s_fc = sem("expert_hidden_chunk_summed")
        s_ge = sem("expert_hidden_chunk_gelu")
        s_pj = sem("expert_output")
        s_ac = sem("expert_added")

        def stage5_load(sp, e, slot):
            sp.dma_start(dsr[:, slot, :], experts_w[e, :, :]).then_inc(s_ds[slot], 16)

        def stage5_sync(sp):
            sp.wait_ge(s_xn, 4)
            stage5_load(sp, 0, 0)
            stage5_load(sp, 1, 1)
            with sp.Fori(0, E1 // 2 - 1) as it:
                for j in range(2):
                    sp.wait_ge(s_pj, it * 2 + j + 1)
                    stage5_load(sp, it * 2 + j + 2, j)

        def stage5_pool(pool):
            with pool.Fori(0, E1 // 2) as it:
                for j in range(2):
                    pool.wait_ge(s_ds[j], it * 16 + 16)
                    pool.tensor_tensor(fch[:, j, :], dsr[:, j, 0:H1], one1[:].broadcast_to([128, H1]),
                                       ALU.mult).then_inc(s_fh, 1)
                    pool.wait_ge(s_fh, it * 2 + j + 1)
                    pool.tensor_tensor(fcl[:, j, :], dsr[:, j, 0:H1], fch[:, j, :].bitcast(F32),
                                       ALU.subtract).then_inc(s_fl, 1)
            norm_pool(pool, 5)

        def expert_up(pe, e, par, first=False):
            pe.wait_ge(s_fl, e + 1)
            for c in range(HC):
                if not first:
                    pe.wait_ge(s_ge, (e - 1) * 4 + c + 1)
                w = slice(c * 128, c * 128 + 128)
                three(pe, psum[:, c, :], fch[:, par, w], fcl[:, par, w], xh[:], xl[:]).then_inc(s_fc, 1)

        def expert_down(pe, e, par):
            pe.wait_ge(s_ge, e * 4 + 4)
            pe.wait_ge(s_ac, e)
            for i in range(TT):
                for c in range(HC):
                    ins = pe.matmul(psum[:, 4 + par, i * 128:i * 128 + 128], hT[:, par, c, i * 128:i * 128 + 128],
                                    dsr[:, par, H1 + c * D:H1 + c * D + D], start=c == 0, stop=c == HC - 1)
            ins.then_inc(s_pj, 1)

        def stage5_tensor(pe):
            pe.wait_ge(s_xh, 5)
            pe.wait_ge(s_xl, 4)
            for i in range(TT):
                t = slice(i * 128, i * 128 + 128)
                ins = three(pe, psum[:, 5, i * E1:i * E1 + E1], xh[:, t], xl[:, t], rwh[:], rwl[:])
            ins.then_inc(s_l5, 1)
            expert_up(pe, 0, 0, first=True)
            pe.wait_ge(s_c5, 1)
            for i in range(TT):
                ins = pe.transpose(psum[0:E1, 5, i * 128:i * 128 + 128], comb5[:, i, :], ident)
            ins.then_inc(s_c5t, 1)
            pe.wait_ge(s_c5c, 1)
            pe.wait_ge(s_in["bproj"], 16)
            for i in range(TT):
                ins = pe.matmul(Y[:, i, :], cT5[:, i * 128:i * 128 + 128], bpj[:], start=True, stop=True)
            ins.then_inc(s_y, 1)
            with pe.Fori(0, E1 // 2 - 1) as it:
                for j in range(2):
                    expert_up(pe, it * 2 + j + 1, 1 - j)
                    expert_down(pe, it * 2 + j, j)
            expert_up(pe, E1 - 1, 1)
            expert_down(pe, E1 - 2, 0)
            expert_down(pe, E1 - 1, 1)

        def expert_gelu(act, e, par, first=False):
            for c in range(HC):
                act.wait_ge(s_fc, e * 4 + c + 1)
                if c == 0 and not first:
                    act.wait_ge(s_pj, e - 1)
                act.activation(hT[:, par, c, :], psum[:, c, :], ACT.Gelu_apprx_tanh,
                               bias=dsr[:, par, H1 + HC * D + c:H1 + HC * D + c + 1]).then_inc(s_ge, 1)

        def stage5_scalar(act):
            act.wait_ge(s_d5, 1)
            act.activation(p5[:], p5[:], ACT.Exp).then_inc(s_e5, 1)
            act.wait_ge(s_ds[0], 16)
            expert_gelu(act, 0, 0, first=True)
            act.wait_ge(s_c5t, 1)
            act.activation(cT5[:], psum[0:E1, 5, :], ACT.Copy).then_inc(s_c5c, 1)
            with act.Fori(0, E1 // 2 - 1) as it:
                for j in range(2):
                    expert_gelu(act, it * 2 + j + 1, 1 - j)
            expert_gelu(act, E1 - 1, 1)

        def expert_add(dve, e, par):
            dve.wait_ge(s_ac, e + 1)
            dve.wait_ge(s_pj, e + 1)
            for i in range(TT):
                ins = dve.scalar_tensor_tensor(acc[:, i, :], psum[:, 4 + par, i * 128:i * 128 + 128],
                                               comb5e[:, i, e, :], acc[:, i, :], ALU.mult, ALU.add)
            ins.then_inc(s_ac, 1)

        comb5 = comb[:].rearrange("p t e -> p (t e)")[:, 0:TT * E1].rearrange("p (t e) -> p t e", t=TT)
        comb5e = comb[:].rearrange("p t e -> p (t e)")[:, 0:TT * E1].rearrange("p (t e o) -> p t e o", t=TT, o=1)

        def stage5_vector(dve):
            lg = psum[:, 5, 0:TT * E1].rearrange("p (t e) -> p t e", t=TT)
            dve.wait_ge(s_l5, 1)
            dstep(dve, dve.tensor_reduce(mx5[:], lg, AX, ALU.max))
            dve.tensor_tensor(p5[:], lg, bc(mx5[:], E1), ALU.subtract).then_inc(s_d5, 1)
            dve.tensor_copy(acc[:], x_tok[:]).then_inc(s_ac, 1)
            dve.wait_ge(s_e5, 1)
            dstep(dve, dve.tensor_reduce(mx5[:], p5[:], AX, ALU.add))
            dstep(dve, dve.reciprocal(mx5[:], mx5[:]))
            dstep(dve, dve.tensor_tensor(p5[:], p5[:], bc(mx5[:], E1), ALU.mult))
            chosen = top_k(dve, p5[:], E1, K1, at["reset8"])
            normalised(dve, p5[:], chosen, E1, 0.0)
            dve.sem_inc(s_c5, 1)
            with dve.Fori(0, E1 // 2) as it:
                for j in range(2):
                    expert_add(dve, it * 2 + j, j)
            dve.wait_ge(s_ac, E1 + 1)
            norm_vector(dve, 5, acc[:])

        late5.close()

        late4.close()


        @block.sync
        def _(sp):
            sp.dma_start(pk["ident"][:], packs["ident"]).then_inc(s_in["ident"], 16)
            sp.dma_start(pk["front"][:], packs["front"]).then_inc(s_in["front"], 16)
            sp.dma_start(rowb[:], rows.broadcast_to([128, width(ROWS)])).then_inc(s_in["rows"], 16)
            for n in ("cross", "route"):
                sp.dma_start(pk[n][:], packs[n]).then_inc(s_in[n], 16)
            sp.dma_start(maskb[MR:128, :], maskin.broadcast_to([128 - MR, C])).then_inc(s_in["mask"], 16)
            sp.dma_start(bpj[:], bproj).then_inc(s_in["bproj"], 16)
            for n in ("masked", "heads"):
                sp.dma_start(pk[n][:], packs[n]).then_inc(s_in[n], 16)
            stage2_sync(sp)
            stage3_sync(sp)
            stage5_sync(sp)
            sp.wait_ge(s_xn, 6)
            sp.dma_start(out, x_tok[:]).then_inc(s_out, 16)
            sp.wait_ge(s_out, 16)

        @block.tensor
        def _(pe):
            stage0_tensor(pe)
            stage1_tensor(pe)
            stage2_tensor(pe)
            stage3_tensor(pe)
            stage4_tensor(pe)
            stage5_tensor(pe)

        @block.vector
        def _(dve):
            stage0_vector(dve)
            stage1_vector(dve)
            stage2_vector(dve)
            stage3_vector(dve)
            stage4_vector(dve)
            stage5_vector(dve)

        @block.scalar
        def _(act):
            stage0_scalar(act)
            stage1_scalar(act)
            stage2_scalar(act)
            stage3_scalar(act)
            stage4_scalar(act)
            stage5_scalar(act)

        @block.gpsimd
        def _(pool):
            stage0_pool(pool)
            stage1_pool(pool)
            stage2_pool(pool)
            stage3_pool(pool)
            stage4_pool(pool)
            stage5_pool(pool)


def kernel(**inputs):
    import concourse.bacc as bacc
    from concourse.bass_utils import run_bass_kernel_spmd

    g = {k: np.asarray(v) for k, v in inputs.items()}
    f = np.float32

    def col(v):
        return v.reshape(-1, 1)

    def tok(v):
        return v.reshape(-1, 128, v.shape[-1]).transpose(1, 0, 2).reshape(128, -1)

    part = np.arange(128)
    heads_of = (part[:, None] // HD == np.arange(NH)[None, :]).astype(f)
    blocks = (part[:, None] // HD == part[None, :] // HD).astype(f)
    causal = np.where(part[None, :] > part[:, None], f(NEG), f(0))
    half = np.stack([part < 64, part >= 64], 1).astype(f)
    sel = np.zeros((128, 12), f)
    sel[:, SEL_LO_Q] = -((part < MR) & (part % HR // HD == 2)).astype(f)
    sel[:, SEL_LO_K] = -((part < MR) & (part % HR // HD == 1)).astype(f)
    for j in range(4):
        sel[:, SEL_HEAD + j] = part // HR == j
        sel[:, SEL_MAX + j] = -(part == MR + j).astype(f)
    sel[:, SEL_MASK] = part == KR
    sel[:, SEL_MAXES] = (part >= MR) & (part < MR + 4)

    def packed_heads(w):
        w3 = np.repeat(w.reshape(4, 4, 1, HD, -1), 3, axis=2).reshape(4, MR, -1)
        return np.concatenate([w3, np.zeros((4, 128 - MR, w3.shape[-1]), f)], axis=1)

    def packed_w(w):
        return packed_heads(w).transpose(2, 0, 1).reshape(128, -1)

    def packed_b(b):
        return packed_heads(b.reshape(D, 1))[:, :, 0].T

    pair = (np.arange(NP)[:, None, None] * 2 + part[None, None, :] // I0)
    row = part[None, :, None] % E0
    spread = (row == pair).astype(f)
    up = lambda w: w.reshape(NP, 2 * I0, D).transpose(0, 2, 1)
    down = g["L0_ffn_ed_w"].reshape(NP, 2, D, I0).transpose(0, 1, 3, 2).reshape(NP, 2 * I0, D)
    routed = np.concatenate([up(g["L0_ffn_eg_w"]), up(g["L0_ffn_eu_w"]), spread, down], axis=2)
    shared = np.concatenate([g["L0_ffn_sg_w"].T, g["L0_ffn_su_w"].T, np.zeros((128, 128), f),
                             g["L0_ffn_sd_w"].T], axis=1)
    stream = np.concatenate([shared[None], routed], axis=0)

    qkv = np.stack([g["L1_attn_w_q"], g["L1_attn_w_k"], g["L1_attn_w_v"]], 1)
    qkv = qkv.reshape(D, 3, HP, 2 * KQ).transpose(2, 0, 1, 3).reshape(HP, D, -1)
    wo = g["L1_attn_w_o"].reshape(D, HP, 2 * KQ).transpose(2, 1, 0).reshape(128, -1)
    reset = lambda n: np.broadcast_to((np.arange(TT * n) % n != 0).astype(f), (128, TT * n))

    parts = {
        "xT": g["x"].reshape(T, D).T, "WqT": g["L0_attn_Wq"].T,
        "WkvT": np.concatenate([g["L0_attn_Wk"].T, g["L0_attn_Wv"].T], 1),
        "conv": np.concatenate([g["L0_attn_conv_w"], col(g["L0_attn_conv_b"])], 1),
        "blocks": blocks, "heads": heads_of, "ident": np.eye(128, dtype=f),
        "x_tok": tok(g["x"].reshape(T, D)), "WpT": g["L0_attn_Wp"].T,
        "ctxT": g["ctx_1024"].reshape(C, D).T,
        "KsT_w": g["L0_xattn_Wk_s"].T, "QsT_w": g["L0_xattn_Wq_s"].T, "Vs_w": g["L0_xattn_Wv_s"].T,
        "QcT_w": g["L0_xattn_Wq_c"].T, "KcT_w": g["L0_xattn_Wk_c"].T, "Vc_w": g["L0_xattn_Wv_c"].T,
        "gate_w": np.concatenate([g["L0_xattn_Wg"][:, :D].T, g["L0_xattn_Wg"][:, D:].T], 1),
        "cols": np.stack([g["L0_xattn_" + n] for n in ("bk_s", "bq_s", "bq_c", "bk_c", "bg")], 1),
        "gw": g["L0_ffn_gate_w"].T, "reset8": reset(G0), "reset64": reset(E0), "rw": g["L1_ffn_router_w"].T,
        "wo": wo, "causal": causal, "half": half,
        "Kr_w": packed_w(g["L1_xattn_Wk"]), "Qr_w": packed_w(g["L1_xattn_Wq"]),
        "V_w": g["L1_xattn_Wv"].T, "O_w": g["L1_xattn_Wo"].T,
        "qb": packed_b(g["L1_xattn_bq"]), "kb": packed_b(g["L1_xattn_bk"]), "sel": sel,
    }
    arrays = {"pack_" + n: np.ascontiguousarray(np.concatenate([parts[k] for k, _ in p], axis=1))
              for n, p in PACKS.items()}
    arrays["rows"] = np.concatenate([g[k] for k in (
        "L0_attn_bp", "L0_xattn_bv_s", "L0_xattn_bv_c", "L0_ffn_gate_bias", "L1_xattn_bv", "L1_xattn_bo")])[None]
    arrays["bproj"] = np.ascontiguousarray(g["L1_ffn_b_proj"])
    arrays["mask_in"] = np.ascontiguousarray(g["mask_BxS2_bk0"]).reshape(1, C)
    arrays["stream"] = np.ascontiguousarray(stream)
    experts = np.concatenate([
        g["L1_ffn_w_fc"],
        g["L1_ffn_w_proj"].reshape(E1, HC, 128, D).transpose(0, 2, 1, 3).reshape(E1, 128, -1),
        g["L1_ffn_b_fc"].reshape(E1, HC, 128).transpose(0, 2, 1)], axis=2)
    arrays["experts_w"] = np.ascontiguousarray(experts)
    arrays["heads_w"] = np.ascontiguousarray(qkv)

    nc = bacc.Bacc("TRN2", target_bir_lowering=False, num_devices=1)
    aps = {n: nc.dram_tensor(n, a.shape, mybir.dt.from_np(a.dtype), kind="ExternalInput").ap()
           for n, a in arrays.items()}
    out = nc.dram_tensor("out", (T, D), F32, kind="ExternalOutput").ap()
    build(nc, {n: aps["pack_" + n] for n in PACKS}, aps["rows"], aps["bproj"], aps["mask_in"], aps["stream"],
          aps["heads_w"], aps["experts_w"], out.rearrange("(t p) d -> p t d", p=128))
    r = run_bass_kernel_spmd(nc, [arrays], core_ids=[0])
    return r.results[0]["out"].reshape(NB, S, D)
```

```python
from contextlib import ExitStack

import numpy as np
import concourse.bass as bass
from concourse import mybir

F32 = mybir.dt.float32
F32R = mybir.dt.float32r
U8 = mybir.dt.uint8
ALU = mybir.AluOpType
ACT = mybir.ActivationFunctionType
AX = mybir.AxisListType.X

D = 128
NB = 2
S = 256
SC = 512
T = NB * S
C = NB * SC
TT = T // 128
HD = 8
NH = 16
E0, I0 = 64, 64
G0, TG0, K0 = 8, 4, 6
NP = E0 // 2
KQ = 64
HP = NH // 2
E1, H1, K1 = 8, 512, 2
HC = H1 // 128
NEG = -1.0e30

IDENT = [("ident", D)]
FRONT = [("xT", T), ("WqT", D), ("WkvT", 2 * D), ("conv", 4), ("blocks", D), ("heads", NH), ("x_tok", T), ("WpT", D)]
CROSS = [("ctxT", C), ("KsT_w", D), ("QsT_w", D), ("Vs_w", D), ("QcT_w", D), ("KcT_w", D), ("Vc_w", D),
         ("gate_w", 2 * D), ("cols", 5)]
ROUTE = [("gw", E0), ("reset8", TT * G0), ("reset64", TT * E0), ("rw", E1)]
HEADS = [("wo", NH * KQ), ("causal", 128), ("half", 2)]
MASKED = [("Kr_w", 4 * D), ("Qr_w", 4 * D), ("V_w", D), ("O_w", D), ("qb", 4), ("kb", 4), ("sel", 12)]
PACKS = {"ident": IDENT, "front": FRONT, "cross": CROSS, "route": ROUTE, "heads": HEADS, "masked": MASKED}
ROWS = [("bp", D), ("bvs", D), ("bvc", D), ("gbias", E0), ("bv", D), ("bo", D)]
SEL_LO_Q, SEL_LO_K, SEL_HEAD, SEL_MASK, SEL_MAX, SEL_MAXES = 0, 1, 2, 6, 7, 11
HR = 3 * HD
MR = 96
KR = 112
VW = 2 * HD + 1


def width(pack):
    return sum(n for _, n in pack)


def build(nc, packs, rows, bproj, maskin, pairs_w, pairs_down_w, heads_w, up_w, down_w, out):
    with ExitStack() as ctx:
        early = ExitStack()
        late = ExitStack()
        late4 = ExitStack()
        late5 = ExitStack()

        def sb(name, shape, dt=F32, stack=ctx):
            return stack.enter_context(nc.sbuf_tensor(name, shape, dt))

        def sem(name):
            return ctx.enter_context(nc.semaphore(name))

        psum = ctx.enter_context(nc.psum_tensor("psum", [128, 8, 512], F32))
        pk = {n: sb("pk_" + n, [128, width(p)]) for n, p in PACKS.items() if n not in ("front", "cross")}
        rowb = sb("rowb", [128, width(ROWS)])
        bpj = sb("bpj", [E1, D])
        maskb = sb("maskb", [128, C], U8)

        x_tok = sb("x_tok", [128, TT, D])
        res = sb("res", [128, TT, D])
        z = sb("z", [128, TT, D])
        stats = sb("stats", [128, TT, 6])
        mv = sb("mv", [128, TT, 2])
        vare = sb("vare", [128, TT])
        rstd = sb("rstd", [128, TT])
        mhalf = sb("mhalf", [128, TT])
        one1 = sb("one", [128, 1])
        xT = sb("xT_f32", [128, T])
        xh = sb("xh", [128, T], F32R)
        xl = sb("xl", [128, T], F32R)
        identr = sb("identr", [128, 128], F32R)
        causr = sb("causr", [128, 128], F32R)
        KX = sb("k4_packed", [128, 4, C], F32R)
        Vx = sb("v4_packed", [128, C // 128, NH, VW], F32R)
        raw = sb("pair_raw", [128, 4, 384])
        rawd = sb("pair_down_raw", [128, 4, 128])
        whi = sb("pair_hi", [128, 4, 384], F32R)
        wlo = sb("pair_lo", [128, 4, 256], F32R)
        gwh = sb("gwh", [128, E0], F32R)
        gwl = sb("gwl", [128, E0], F32R)
        rwh = sb("rwh", [128, E1], F32R)
        rwl = sb("rwl", [128, E1], F32R)
        sg = sb("silu_gate", [128, 2, T])
        h1 = sb("h_unweighted", [128, 2, T])
        hh = sb("h_weighted", [128, 2, T])
        score = sb("score", [128, TT, E0])
        gsc = sb("group_score", [128, TT, G0])
        m8 = sb("top8", [128, TT, 8])
        cnt = sb("count_above", [128, TT])
        gt = sb("above", [128, TT * E0])
        eq = sb("equal", [128, TT * E0])
        cum = sb("equal_so_far", [128, TT * E0])
        selg = sb("selected", [128, TT * E0])
        wsum = sb("weight_sum", [128, TT])
        comb = sb("comb", [128, TT, E0])
        combhl = sb("comb_hi_lo", [128, TT, 128])
        combT = sb("comb_T", [128, T], F32R)
        for n in ("front", "cross"):
            pk[n] = sb("pk_" + n, [128, width(PACKS[n])], stack=early)
        at = {}

        def place(n):
            o = 0
            for name, w in PACKS[n]:
                at[name] = pk[n][:, o:o + w]
                o += w

        for n in pk:
            place(n)
        o = 0
        for name, w in ROWS:
            at[name] = rowb[:, o:o + w]
            o += w
        ident = at["ident"]

        s_in = {n: sem("in_" + n) for n in [*PACKS, "rows", "bproj", "mask"]}
        s_y = sem("y_summed")
        s_res = sem("residual_biased")
        s_var = sem("variance")
        s_rstd = sem("rstd_powed")
        s_xn = sem("x_normed")
        s_xT = sem("x_transposed")
        s_xh = sem("x_hi")
        s_xl = sem("x_lo")
        s_out = sem("output_stored")
        s_dve = sem("dve_step")
        s_pool = sem("pool_step")
        s_act = sem("act_step")
        s_mh = sem("minus_half_set")

        block = ctx.enter_context(nc.Block())
        count = {"dve": 0, "pool": 0, "act": 0}

        def dstep(dve, ins):
            count["dve"] += 1
            ins.then_inc(s_dve, 1)
            dve.wait_ge(s_dve, count["dve"])

        def pstep(pool, ins):
            count["pool"] += 1
            ins.then_inc(s_pool, 1)
            pool.wait_ge(s_pool, count["pool"])

        def tiles(ap, n=TT):
            return ap.rearrange("p (t d) -> p t d", t=n)

        Y = tiles(psum[:, 7, :])

        def norm_vector(dve, n, residual):
            dve.wait_ge(s_y, n + 1)
            zz = Y
            if residual is not None:
                zz = z[:]
                dstep(dve, dve.tensor_tensor(zz, Y, residual, ALU.add))
            for i in range(TT):
                ins = dve.bn_stats(stats[:, i, :], zz[:, i, :])
            dstep(dve, ins)
            for i in range(TT):
                ins = dve.bn_aggr(mv[:, i, :], stats[:, i, :])
            dstep(dve, ins)
            dve.tensor_scalar(vare[:], mv[:, :, 1], 1e-5, None, ALU.add).then_inc(s_var, 1)
            dve.wait_ge(s_rstd, n + 1)
            for i in range(TT):
                ins = dve.tensor_scalar(x_tok[:, i, :], zz[:, i, :], mv[:, i, 0:1], rstd[:, i:i + 1],
                                        ALU.subtract, ALU.mult)
            ins.then_inc(s_xn, 1)

        def norm_pool(pool, n):
            pool.wait_ge(s_var, n + 1)
            if n == 0:
                pool.wait_ge(s_mh, 1)
            pool.tensor_tensor(rstd[:], vare[:], mhalf[:], ALU.pow).then_inc(s_rstd, 1)

        def norm_tensor(pe, n):
            pe.wait_ge(s_xn, n + 1)
            for i in range(TT):
                ins = pe.transpose(psum[:, 6, i * 128:i * 128 + 128], x_tok[:, i, :], ident)
            ins.then_inc(s_xT, 1)

        def norm_scalar(act, n):
            act.wait_ge(s_xT, n + 1)
            act.activation(xT[:] if n == 0 else xh[:], psum[:, 6, :], ACT.Copy).then_inc(s_xh, 1)

        def norm_lo(dve, n):
            dve.wait_ge(s_xh, n + 1)
            dve.tensor_tensor(xl[:], psum[:, 6, :], xh[:].bitcast(F32), ALU.subtract).then_inc(s_xl, 1)

        def three(pe, out_, wh, wl, ah, al, start=True, stop=True):
            pe.matmul(out_, wh, ah, start=start, stop=False)
            pe.matmul(out_, wl, ah, start=False, stop=False)
            return pe.matmul(out_, wh, al, start=False, stop=stop)

        kmin = sb("kmin", [128, TT, D], stack=early)
        kphi = sb("kphi", [128, TT, D], stack=early)
        qmin = sb("qmin", [128, T], stack=early)
        qphi = sb("qphi", [128, T], stack=early)
        v_one = sb("v_one", [128, TT, D + 1], stack=early)
        kvm = sb("kvm", [128, NB, D + NH], stack=early)
        rden = sb("rden", [128, TT, NH], stack=early)
        att = sb("att", [128, TT, D], stack=early)
        loc = sb("loc", [128, NB, S], stack=early)
        aT = sb("aT", [128, T], stack=early)
        KsT = sb("KsT", [128, C], stack=early)
        QsT = sb("QsT", [128, C], stack=early)
        Vs = sb("Vs", [128, C // 128, D], stack=early)

        s_q = sem("q_projected")
        s_kv = sem("kv_projected")
        s_km = sem("kq_below_zero")
        s_ke = sem("kq_exp")
        s_phi = sem("kq_features")
        s_v = sem("v_copied")
        s_vone = sem("v_ones_set")
        s_st = sem("state_summed")
        s_stm = sem("state_masked")
        s_num = sem("numerators")
        s_att = sem("attention")
        s_attT = sem("attention_transposed")
        s_aT = sem("attention_plus_local")
        s_cps = sem("context_projected")
        s_cev = sem("context_copied")
        s_cv = sem("context_values")
        s_cvd = sem("context_values_biased")

        num = psum[:, 1:3, :].rearrange("p a (i n) -> p (a i) n", i=2)
        state = psum[:, 3, :].rearrange("p (b n) -> p b n", b=NB)

        def context_kq(pe, k):
            w, h = (at["KsT_w"], at["QsT_w"])[k // 2], k % 2
            if k == 0:
                pe.wait_ge(s_in["cross"], 16)
            if k >= 2:
                pe.wait_ge(s_cev, k - 1)
            pe.matmul(psum[:, 4 + k % 2, :], w, at["ctxT"][:, h * 512:h * 512 + 512],
                      start=True, stop=True).then_inc(s_cps, 1)

        def stage0_tensor(pe):
            pe.wait_ge(s_in["ident"], 16)
            pe.wait_ge(s_in["front"], 16)
            for a in range(2):
                for i in range(TT):
                    ins = pe.matmul(psum[:, 1 + a, i * 128:i * 128 + 128], at["xT"][:, i * 128:i * 128 + 128],
                                    at["WkvT"][:, a * D:a * D + D], start=True, stop=True)
                ins.then_inc(s_kv, 1)
            pe.matmul(psum[:, 0, :], at["WqT"], at["xT"], start=True, stop=True).then_inc(s_q, 1)
            context_kq(pe, 0)
            context_kq(pe, 1)
            pe.wait_ge(s_phi, 1)
            pe.wait_ge(s_v, 1)
            pe.wait_ge(s_vone, 1)
            for b in range(NB):
                for i in range(2):
                    ins = pe.matmul(state[:, b, 0:D + 1], kphi[:, 2 * b + i, :], v_one[:, 2 * b + i, :],
                                    start=i == 0, stop=i == 1)
            ins.then_inc(s_st, 1)
            context_kq(pe, 2)
            context_kq(pe, 3)
            pe.wait_ge(s_stm, 1)
            pe.wait_ge(s_phi, 2)
            for i in range(TT):
                ins = pe.matmul(num[:, i, 0:D + NH], qphi[:, i * 128:i * 128 + 128], kvm[:, i // 2, :],
                                start=True, stop=True)
            ins.then_inc(s_num, 1)
            pe.wait_ge(s_cev, 4)
            for i in range(C // 128):
                ins = pe.matmul(psum[:, 4 + i // 4, i % 4 * 128:i % 4 * 128 + 128],
                                at["ctxT"][:, i * 128:i * 128 + 128], at["Vs_w"], start=True, stop=True)
            ins.then_inc(s_cv, 1)
            pe.wait_ge(s_att, 1)
            for i in range(TT):
                ins = pe.transpose(psum[:, 0, i * 128:i * 128 + 128], att[:, i, :], ident)
            ins.then_inc(s_attT, 1)
            pe.wait_ge(s_aT, 1)
            for i in range(TT):
                ins = pe.matmul(Y[:, i, :], aT[:, i * 128:i * 128 + 128], at["WpT"], start=True, stop=True)
            ins.then_inc(s_y, 1)
            kv4_tensor(pe, 0)
            norm_tensor(pe, 0)

        def stage0_vector(dve):
            dve.wait_ge(s_kv, 1)
            dve.tensor_scalar(kmin[:], tiles(psum[:, 1, :]), 0.0, None, ALU.min).then_inc(s_km, 1)
            dve.wait_ge(s_q, 1)
            dve.tensor_scalar(qmin[:], psum[:, 0, :], 0.0, None, ALU.min).then_inc(s_km, 1)
            dve.wait_ge(s_ke, 1)
            dve.scalar_tensor_tensor(kphi[:], tiles(psum[:, 1, :]), 0.0, kmin[:], ALU.max, ALU.add).then_inc(s_phi, 1)
            dve.wait_ge(s_ke, 2)
            dve.scalar_tensor_tensor(qphi[:], psum[:, 0, :], 0.0, qmin[:], ALU.max, ALU.add).then_inc(s_phi, 1)
            xs = at["xT"].rearrange("p (b s) -> p b s", b=NB)
            cw = at["conv"]
            dstep(dve, dve.tensor_scalar(loc[:], xs, cw[:, 1:2], cw[:, 3:4], ALU.mult, ALU.add))
            dstep(dve, dve.scalar_tensor_tensor(loc[:, :, 1:S], xs[:, :, 0:S - 1], cw[:, 0:1], loc[:, :, 1:S],
                                                ALU.mult, ALU.add))
            dstep(dve, dve.scalar_tensor_tensor(loc[:, :, 0:S - 1], xs[:, :, 1:S], cw[:, 2:3],
                                                loc[:, :, 0:S - 1], ALU.mult, ALU.add))
            dve.wait_ge(s_st, 1)
            dve.tensor_tensor(kvm[:, :, 0:D], state[:, :, 0:D],
                              at["blocks"].rearrange("p (o d) -> p o d", o=1).broadcast_to([128, NB, D]), ALU.mult)
            for b in range(NB):
                ins = dve.tensor_scalar(kvm[:, b, D:D + NH], at["heads"], state[:, b, D:D + 1], None, ALU.mult)
            ins.then_inc(s_stm, 1)
            dve.wait_ge(s_num, 1)
            dstep(dve, dve.tensor_scalar(rden[:], num[:, :, D:D + NH], 1e-6, None, ALU.max))
            dstep(dve, dve.reciprocal(rden[:], rden[:]))
            dve.tensor_tensor(att[:].rearrange("p t (h d) -> p t h d", h=NH),
                              num[:, :, 0:D].rearrange("p t (h d) -> p t h d", h=NH),
                              rden[:].rearrange("p t (h o) -> p t h o", o=1).broadcast_to([128, TT, NH, HD]),
                              ALU.mult).then_inc(s_att, 1)
            dve.wait_ge(s_attT, 1)
            dve.tensor_tensor(aT[:], psum[:, 0, :], loc[:].rearrange("p b s -> p (b s)"), ALU.add).then_inc(s_aT, 1)
            dve.wait_ge(s_cv, 1)
            dve.wait_ge(s_in["rows"], 16)
            dve.tensor_tensor(Vs[:], psum[:, 4:6, :].rearrange("p a (t d) -> p (a t) d", t=4),
                              at["bvs"].rearrange("p (o d) -> p o d", o=1).broadcast_to([128, 8, D]),
                              ALU.add).then_inc(s_cvd, 1)
            dve.wait_ge(s_res, 1)
            norm_vector(dve, 0, res[:])
            kv4_vector(dve, 0)

        def stage0_scalar(act):
            act.wait_ge(s_km, 1)
            act.activation(kmin[:], kmin[:], ACT.Exp).then_inc(s_ke, 1)
            act.wait_ge(s_km, 2)
            act.activation(qmin[:], qmin[:], ACT.Exp).then_inc(s_ke, 1)
            act.wait_ge(s_kv, 2)
            act.activation(v_one[:, :, 0:D], tiles(psum[:, 2, :]), ACT.Copy).then_inc(s_v, 1)
            for k in range(4):
                act.wait_ge(s_cps, k + 1)
                act.activation((KsT, QsT)[k // 2][:, k % 2 * 512:k % 2 * 512 + 512], psum[:, 4 + k % 2, :],
                               ACT.Identity, bias=at["cols"][:, k // 2:k // 2 + 1]).then_inc(s_cev, 1)
            kv4_scalar(act, 0)
            norm_scalar(act, 0)

        def stage0_pool(pool):
            pool.memset(mhalf[:], -0.5).then_inc(s_mh, 1)
            pool.memset(v_one[:, :, D:D + 1], 1.0).then_inc(s_vone, 1)
            pool.memset(Vx[:, :, :, HD:HD + 1].bitcast(F32), 1.0).then_inc(s_v4o, 1)
            pool.wait_ge(s_in["front"], 16)
            pool.wait_ge(s_in["rows"], 16)
            pool.tensor_tensor(res[:], tiles(at["x_tok"]),
                               at["bp"].rearrange("p (o d) -> p o d", o=1).broadcast_to([128, TT, D]),
                               ALU.add).then_inc(s_res, 1)
            norm_pool(pool, 0)

        P1 = sb("P1", [128, TT, SC], stack=early)
        vf = P1[:, 0:2, :].rearrange("p a (t h d) -> p (a t) h d", t=4, h=NH)
        kxf = sb("k4_biased", [128, 4, 512], stack=early)
        kxr = sb("k4_rounded", [128, 4, 512], F32R, stack=early)
        km = sb("mask4_added", [128, C], stack=early)
        kones = sb("mask4_rows", [128, C], stack=early)
        s_k4 = sem("k4_projected")
        s_k4a = sem("k4_copied")
        s_k4d = sem("k4_split")
        s_v4 = sem("v4_projected")
        s_v4c = sem("v4_biased")
        s_v4o = sem("v4_ones_set")
        s_kx = sem("kv4_ready")

        def kv4_tensor(pe, part):
            pe.wait_ge(s_in["masked"], 16)
            if not part:
                pe.wait_ge(s_cvd, 1)
            for n in range(4 * part, 4 * part + 4):
                if n % 4 >= 2:
                    pe.wait_ge(s_k4a, n - 1)
                pe.matmul(psum[:, (4, 0)[part] + n % 2, :], at["Kr_w"][:, n // 2 * D:n // 2 * D + D],
                          at["ctxT"][:, n % 2 * 512:n % 2 * 512 + 512], start=True, stop=True).then_inc(s_k4, 1)
            if not part:
                for i in range(C // 128):
                    ins = pe.matmul(psum[:, 1 + i // 4, i % 4 * 128:i % 4 * 128 + 128],
                                    at["ctxT"][:, i * 128:i * 128 + 128], at["V_w"], start=True, stop=True)
                ins.then_inc(s_v4, 1)

        def kv4_scalar(act, part):
            act.wait_ge(s_in["masked"], 16)
            for n in range(4 * part, 4 * part + 4):
                act.wait_ge(s_k4, n + 1)
                if part:
                    act.wait_ge(s_k4d, n - 3)
                bias = at["kb"][:, n // 2:n // 2 + 1]
                act.activation(kxf[:, n % 4, :], psum[:, (4, 0)[part] + n % 2, :], ACT.Identity, bias=bias)
                act.activation(kxr[:, n % 4, :], psum[:, (4, 0)[part] + n % 2, :], ACT.Identity,
                               bias=bias).then_inc(s_k4a, 1)

        def kv4_vector(dve, part):
            dve.wait_ge(s_in["masked"], 16)
            for n in range(4 * part, 4 * part + 4):
                dve.wait_ge(s_k4a, n + 1)
                dve.scalar_tensor_tensor(KX[:, n // 2, n % 2 * 512:n % 2 * 512 + 512], kxr[:, n % 4, :].bitcast(F32),
                                         at["sel"][:, SEL_LO_K:SEL_LO_K + 1], kxf[:, n % 4, :],
                                         ALU.mult, ALU.add).then_inc(s_k4d, 1)
            if part:
                dve.wait_ge(s_in["mask"], 16)
                m = slice(MR, 128)
                dstep(dve, dve.tensor_scalar(km[m, :], maskb[m, :], -NEG, NEG, ALU.mult, ALU.add))
                dstep(dve, dve.tensor_scalar(kones[m, :], km[m, :], at["sel"][m, SEL_MASK:SEL_MASK + 1],
                                             at["sel"][m, SEL_MAXES:SEL_MAXES + 1], ALU.mult, ALU.add))
                dve.wait_ge(s_k4d, 8)
                for t in range(4):
                    ins = dve.tensor_copy(KX[m, t, :], kones[m, :])
                ins.then_inc(s_kx, 1)
            else:
                dve.wait_ge(s_v4, 1)
                dve.wait_ge(s_v4o, 1)
                dstep(dve, dve.tensor_tensor(
                    vf, psum[:, 1:3, :].rearrange("p a (t h d) -> p (a t) h d", t=4, h=NH),
                    at["bv"].rearrange("p (o h d) -> p o h d", o=1, h=NH).broadcast_to([128, 8, NH, HD]), ALU.add))
                dstep(dve, dve.tensor_copy(Vx[:, :, :, 0:HD], vf))
                dve.tensor_tensor(Vx[:, :, :, HD + 1:VW], vf, Vx[:, :, :, 0:HD].bitcast(F32),
                                  ALU.subtract).then_inc(s_v4c, 1)

        QcT = sb("QcT", [128, T], stack=early)
        KcT = sb("KcT", [128, T], stack=early)
        Vc = sb("Vc", [128, TT, D], stack=early)
        P2 = sb("P2", [128, 8, S], stack=early)
        P1T = sb("P1T", [128, NB, 4, S], stack=early)
        P2T = sb("P2T", [128, NB, 2, SC], stack=early)
        mx1 = sb("mx1", [128, TT], stack=early)
        mx2 = sb("mx2", [128, 8], stack=early)
        sm1 = sb("sm1", [128, TT], stack=early)
        sm2 = sb("sm2", [128, 8], stack=early)
        c2s = sb("c2s", [128, T], stack=early)
        s2c = sb("s2c", [128, T], stack=early)
        gth = sb("gth", [128, T], stack=early)
        dif = loc[:].rearrange("p b s -> p (b s)")
        hbg = sb("hbg", [128, 1], stack=early)
        SCALE1 = 1.0 / float(np.sqrt(np.float32(D)))

        s_p1 = sem("x_projected")
        s_p1c = sem("x_qk_copied")
        s_p1v = sem("x_v_biased")
        s_s1 = sem("scores_by_token")
        s_s2 = sem("scores_by_context")
        s_m1 = sem("max_by_token")
        s_m2 = sem("max_by_context")
        s_e1 = sem("exp_by_token")
        s_e2 = sem("exp_by_context")
        s_n1 = sem("probs_by_token")
        s_n2 = sem("probs_by_context")
        s_t1 = sem("probs_by_token_T")
        s_t2 = sem("probs_by_context_T")
        s_t1c = sem("probs_by_token_T_copied")
        s_t2c = [sem(f"probs_by_context_T_copied_{b}") for b in range(NB)]
        s_o1 = sem("tokens_attended")
        s_o2 = sem("context_attended")
        s_o1c = sem("tokens_attended_copied")
        s_o2c = sem("context_attended_paired")
        s_g = sem("gate_summed")
        s_gt = sem("gate_tanh")
        s_mix = sem("gated")
        s_hbg = sem("half_gate_bias")
        BK2 = [0, 1, 2, 7]

        def s2_at(k):
            return psum[:, BK2[k // 2], k % 2 * S:k % 2 * S + S]

        def stage1_tensor(pe):
            pe.wait_ge(s_xh, 1)
            pe.matmul(psum[:, 0, :], at["QcT_w"], xT[:], start=True, stop=True).then_inc(s_p1, 1)
            pe.wait_ge(s_v4c, 1)
            pe.matmul(psum[:, 1, :], at["KcT_w"], xT[:], start=True, stop=True).then_inc(s_p1, 1)
            for i in range(TT):
                ins = pe.matmul(psum[:, 2, i * 128:i * 128 + 128], xT[:, i * 128:i * 128 + 128], at["Vc_w"],
                                start=True, stop=True)
            ins.then_inc(s_p1, 1)
            pe.wait_ge(s_p1c, 1)
            pe.wait_ge(s_cev, 4)
            pe.wait_ge(s_cvd, 1)
            for i in range(TT):
                pe.matmul(psum[:, 3 + i, :], QcT[:, i * 128:i * 128 + 128], KsT[:, i // 2 * SC:i // 2 * SC + SC],
                          start=True, stop=True).then_inc(s_s1, 1)
            pe.wait_ge(s_p1c, 2)
            pe.wait_ge(s_p1v, 1)
            for k in range(8):
                ins = pe.matmul(s2_at(k), QsT[:, k * 128:k * 128 + 128], KcT[:, k // 4 * S:k // 4 * S + S],
                                start=True, stop=True)
                if k % 2:
                    ins.then_inc(s_s2, 1)
            pe.wait_ge(s_e1, TT)
            for i in range(TT):
                pe.wait_ge(s_n1, i + 1)
                for j in range(4):
                    bk = 3 + 2 * (i // 2) + j // 2
                    o_ = j % 2 * S + i % 2 * 128
                    ins = pe.transpose(psum[:, bk, o_:o_ + 128], P1[:, i, j * 128:j * 128 + 128], ident)
                if i % 2:
                    ins.then_inc(s_t1, 1)
            pe.wait_ge(s_e2, 8)
            for k in range(8):
                pe.wait_ge(s_n2, k + 1)
                for j in range(2):
                    ins = pe.transpose(psum[:, BK2[k // 4 * 2 + j], k % 4 * 128:k % 4 * 128 + 128],
                                       P2[:, k, j * 128:j * 128 + 128], ident)
                if k % 4 == 3:
                    ins.then_inc(s_t2, 1)
            pe.wait_ge(s_t1c, 2)
            for b in range(NB):
                for j in range(4):
                    ins = pe.matmul(psum[:, 3, b * S:b * S + S], Vs[:, b * 4 + j, :], P1T[:, b, j, :],
                                    start=j == 0, stop=j == 3)
            ins.then_inc(s_o1, 1)
            for b in range(NB):
                pe.wait_ge(s_t2c[b], 1)
                for j in range(2):
                    ins = pe.matmul(psum[:, 4 + b, :], Vc[:, b * 2 + j, :], P2T[:, b, j, :],
                                    start=j == 0, stop=j == 1)
                ins.then_inc(s_o2, 1)
            pe.wait_ge(s_o1c, 1)
            pe.matmul(psum[:, 6, :], at["gate_w"][:, 0:D], c2s[:], start=True, stop=False)
            pe.wait_ge(s_o2c, 2)
            pe.matmul(psum[:, 6, :], at["gate_w"][:, D:2 * D], s2c[:], start=False, stop=True).then_inc(s_g, 1)
            kv4_tensor(pe, 1)
            pe.wait_ge(s_mix, 1)
            for i in range(TT):
                ins = pe.transpose(Y[:, i, :], gth[:, i * 128:i * 128 + 128], ident)
            ins.then_inc(s_y, 1)
            norm_tensor(pe, 1)

        def stage1_scalar(act):
            for k, dst in enumerate((QcT, KcT)):
                act.wait_ge(s_p1, k + 1)
                act.activation(dst[:], psum[:, k, :], ACT.Identity,
                               bias=at["cols"][:, 2 + k:3 + k]).then_inc(s_p1c, 1)
            for i in range(TT):
                act.wait_ge(s_m1, i + 1)
                act.activation(P1[:, i, :], psum[:, 3 + i, :], ACT.Exp, bias=mx1[:, i:i + 1], scale=SCALE1,
                               accum_out=sm1[:, i:i + 1]).then_inc(s_e1, 1)
            for k in range(8):
                act.wait_ge(s_m2, k // 2 + 1)
                act.activation(P2[:, k, :], s2_at(k), ACT.Exp, bias=mx2[:, k:k + 1], scale=SCALE1,
                               accum_out=sm2[:, k:k + 1]).then_inc(s_e2, 1)
            for b in range(NB):
                act.wait_ge(s_t1, b + 1)
                act.activation(P1T[:, b, :, :].rearrange("p (a j) s -> p a (j s)", a=2),
                               psum[:, 3 + 2 * b:5 + 2 * b, :], ACT.Copy).then_inc(s_t1c, 1)
            act.wait_ge(s_t2, 2)
            for j in range(2):
                ins = act.activation(P2T[:, 1, j, :], psum[:, BK2[2 + j], :], ACT.Copy)
            ins.then_inc(s_t2c[1], 1)
            stage2_early_scalar(act)
            act.wait_ge(s_o1, 1)
            act.activation(c2s[:], psum[:, 3, :], ACT.Copy).then_inc(s_o1c, 1)
            act.wait_ge(s_g, 1)
            act.wait_ge(s_hbg, 1)
            act.activation(gth[:], psum[:, 6, :], ACT.Tanh, bias=hbg[:, 0:1], scale=0.5).then_inc(s_gt, 1)
            kv4_scalar(act, 1)
            norm_scalar(act, 1)

        def stage1_vector(dve):
            dve.tensor_scalar(hbg[:], at["cols"][:, 4:5], 0.5, None, ALU.mult).then_inc(s_hbg, 1)
            dve.wait_ge(s_p1, 3)
            dve.tensor_tensor(Vc[:], tiles(psum[:, 2, :]),
                              at["bvc"].rearrange("p (o d) -> p o d", o=1).broadcast_to([128, TT, D]),
                              ALU.add).then_inc(s_p1v, 1)
            for i in range(TT):
                dve.wait_ge(s_s1, i + 1)
                dstep(dve, dve.tensor_reduce(mx1[:, i:i + 1], psum[:, 3 + i, :], AX, ALU.max))
                dve.tensor_scalar(mx1[:, i:i + 1], mx1[:, i:i + 1], -SCALE1, None, ALU.mult).then_inc(s_m1, 1)
            for k in range(4):
                dve.wait_ge(s_s2, k + 1)
                m = mx2[:, 2 * k:2 * k + 2]
                dstep(dve, dve.tensor_reduce(m, psum[:, BK2[k], :].rearrange("p (a s) -> p a s", a=2), AX, ALU.max))
                dve.tensor_scalar(m, m, -SCALE1, None, ALU.mult).then_inc(s_m2, 1)
            dve.wait_ge(s_e1, TT)
            dstep(dve, dve.reciprocal(sm1[:], sm1[:]))
            for i in range(TT):
                dve.tensor_scalar(P1[:, i, :], P1[:, i, :], sm1[:, i:i + 1], None, ALU.mult).then_inc(s_n1, 1)
            dve.wait_ge(s_e2, 8)
            dstep(dve, dve.reciprocal(sm2[:], sm2[:]))
            for k in range(8):
                dve.tensor_scalar(P2[:, k, :], P2[:, k, :], sm2[:, k:k + 1], 0.5, ALU.mult,
                                  ALU.mult).then_inc(s_n2, 1)
            dve.wait_ge(s_t2, 1)
            dve.tensor_copy(P2T[:, 0, :, :], psum[:, 0:2, :]).then_inc(s_t2c[0], 1)
            for b in range(NB):
                dve.wait_ge(s_o2, b + 1)
                dve.tensor_reduce(s2c[:, b * S:b * S + S], psum[:, 4 + b, :].rearrange("p (s o) -> p s o", o=2),
                                  AX, ALU.add).then_inc(s_o2c, 1)
            dve.wait_ge(s_o2c, 2)
            dve.wait_ge(s_o1c, 1)
            dstep(dve, dve.tensor_tensor(dif, c2s[:], s2c[:], ALU.subtract))
            dve.wait_ge(s_gt, 1)
            dstep(dve, dve.scalar_tensor_tensor(gth[:], gth[:], 1.0, dif, ALU.add, ALU.mult))
            dve.scalar_tensor_tensor(gth[:], gth[:], 0.5, s2c[:], ALU.mult, ALU.add).then_inc(s_mix, 1)
            norm_vector(dve, 1, x_tok[:])
            norm_lo(dve, 1)
            kv4_vector(dve, 1)

        def stage1_pool(pool):
            constants_pool(pool)
            norm_pool(pool, 1)

        early.close()

        Qrh = sb("q4_w_hi", [128, 4 * D], F32R, stack=late4)
        Qrl = sb("q4_w_lo", [128, 4 * D], F32R, stack=late4)
        xq = sg[:]
        yq = h1[:]
        rq = sb("q4_rounded", [128, 2, T], F32R, stack=late4)
        Qx = sb("q4_heads", [128, 4, 4, T], F32R, stack=late4)
        mxt = sb("max4", [128, TT, 128], stack=late4)
        VP = sb("v4_padded", [128, 2, C // 128, 4, 4 * VW], F32R, stack=late4)
        Pl = sb("exp4_lo", [128, 4, 512], F32R, stack=late4)
        OS = sb("attended4_T_raw", [128, T], stack=late4)
        rs4 = sb("sums4_inverse", [128, TT, 4], stack=late4)
        lo4 = sb("attended4_lo", [128, TT, 4, HD], stack=late4)
        att4 = sb("attended4", [128, TT, D], stack=late4)
        aT4 = sb("attended4_T", [128, T], stack=late4)

        s_gu = [sem(f"pair_gate_up_spread_loaded_{i}") for i in range(4)]
        s_dw = [sem(f"pair_down_loaded_{i}") for i in range(4)]
        s_const = sem("rounded_constants")
        s_whi = sem("pair_hi_made")
        s_wlo = sem("pair_lo_made")
        s_lg = sem("logits")
        s_th = sem("logits_tanh")
        s_pg = sem("pair_gate")
        s_pu = sem("pair_up")
        s_pc = sem("pair_weights_spread")
        s_silu = sem("pair_silu")
        s_h1 = sem("pair_h_unweighted")
        s_h = sem("pair_h")
        s_d = sem("pair_down")
        s_comb = sem("combine_weights")
        s_cT = sem("combine_weights_T")
        s_combT = sem("combine_weights_T_copied")
        LOOPS = (NP - 4) // 4

        def bc(ap, n):
            return ap.rearrange("p (a o) -> p a o", o=1).broadcast_to([128, ap.shape[1], n])

        def top_k(dve, v, n, k, reset):
            f = selg[:, 0:TT * n].rearrange("p (t e) -> p t e", t=TT)
            g_, e_, c_ = (a[:, 0:TT * n].rearrange("p (t e) -> p t e", t=TT) for a in (gt, eq, cum))
            for i in range(TT):
                ins = dve.max(m8[:, i, :], v[:, i, :])
            dstep(dve, ins)
            thr = m8[:, :, k - 1:k].broadcast_to([128, TT, n])
            dve.tensor_tensor(g_, v, thr, ALU.is_gt)
            dstep(dve, dve.tensor_tensor(e_, v, thr, ALU.is_equal))
            dve.tensor_tensor_scan(cum[:, 0:TT * n], reset, eq[:, 0:TT * n], 0.0, ALU.mult, ALU.add)
            dstep(dve, dve.tensor_reduce(cnt[:], g_, AX, ALU.add))
            dstep(dve, dve.tensor_scalar(cnt[:], cnt[:], -1.0, float(k), ALU.mult, ALU.add))
            dstep(dve, dve.tensor_tensor(c_, c_, bc(cnt[:], n), ALU.is_le))
            dstep(dve, dve.tensor_tensor(e_, e_, c_, ALU.mult))
            dstep(dve, dve.tensor_tensor(f, e_, g_, ALU.add))
            return f

        def normalised(dve, v, chosen, n, eps):
            c_ = comb[:].rearrange("p t e -> p (t e)")[:, 0:TT * n].rearrange("p (t e) -> p t e", t=TT)
            dstep(dve, dve.tensor_tensor(c_, v, chosen, ALU.mult))
            dstep(dve, dve.tensor_reduce(wsum[:], c_, AX, ALU.add))
            if eps:
                dstep(dve, dve.tensor_scalar(wsum[:], wsum[:], eps, None, ALU.add))
            dstep(dve, dve.reciprocal(wsum[:], wsum[:]))
            dstep(dve, dve.tensor_tensor(c_, c_, bc(wsum[:], n), ALU.mult))
            return c_

        def load_pair(sp, p, slot):
            sp.dma_start(raw[:, slot, :], pairs_w[p + 1, :, :]).then_inc(s_gu[slot], 16)

        def load_pair_down(sp, p, slot):
            sp.dma_start(rawd[:, slot, :], pairs_down_w[p + 1, :, :]).then_inc(s_dw[slot], 16)

        def stage2_sync(sp):
            for p in range(-1, 3):
                load_pair(sp, p, p % 4)
                load_pair_down(sp, p, p % 4)
            for p in range(3, 5):
                sp.wait_ge(s_wlo, p - 2)
                load_pair(sp, p, p % 4)

            def step(i, j):
                sp.wait_ge(s_d, i + 1)
                load_pair_down(sp, i + 3, (j + 3) % 4)
                if not isinstance(i, int) or i + 5 < NP:
                    sp.wait_ge(s_wlo, i + 3)
                    load_pair(sp, i + 5, (j + 5) % 4)

            with sp.Fori(0, LOOPS - 1) as it:
                for j in range(4):
                    step(it * 4 + j, j)
            for i in range(4 * (LOOPS - 1), NP - 3):
                step(i, i % 4)

        def constants_pool(pool):
            pool.wait_ge(s_in["route"], 16)
            pstep(pool, pool.tensor_copy(gwh[:], at["gw"]))
            pool.tensor_tensor(gwl[:], at["gw"], gwh[:].bitcast(F32), ALU.subtract)
            pstep(pool, pool.tensor_copy(rwh[:], at["rw"]))
            pool.tensor_tensor(rwl[:], at["rw"], rwh[:].bitcast(F32), ALU.subtract)
            pool.tensor_copy(identr[:], ident)
            pool.wait_ge(s_in["heads"], 16)
            pool.tensor_copy(causr[:], at["causal"]).then_inc(s_const, 1)

        def pair_lo(pool, p, slot):
            pool.wait_ge(s_whi, p + 2)
            pool.tensor_tensor(wlo[:, slot, :], raw[:, slot, 0:256], whi[:, slot, 0:256].bitcast(F32),
                               ALU.subtract).then_inc(s_wlo, 1)

        def stage2_pool(pool):
            for p in range(-1, 1):
                pair_lo(pool, p, p % 4)
            with pool.Fori(0, LOOPS) as it:
                for j in range(4):
                    pair_lo(pool, it * 4 + j + 1, (j + 1) % 4)
            for p in range(NP - 3, NP):
                pair_lo(pool, p, p % 4)
            norm_pool(pool, 2)

        def pair_hi(act, q, slot, turn):
            act.wait_ge(s_gu[slot], turn * 16 + 16)
            act.activation(whi[:, slot, :], raw[:, slot, :], ACT.Copy).then_inc(s_whi, 1)

        def pair_silu(act, p, par):
            act.wait_ge(s_pg, p + 2)
            act.wait_ge(s_h1, p)
            act.activation(sg[:, par, :], psum[:, par, :], ACT.Silu).then_inc(s_silu, 1)

        def stage2_early_scalar(act):
            pair_hi(act, -1, 3, 0)
            pair_hi(act, 0, 0, 0)
            pair_hi(act, 1, 1, 0)

        def stage2_scalar(act):
            act.wait_ge(s_lg, 1)
            act.activation(score[:], psum[:, 5, 0:TT * E0].rearrange("p (t e) -> p t e", t=TT), ACT.Tanh,
                           scale=0.5).then_inc(s_th, 1)
            act.wait_ge(s_pg, 1)
            act.activation(sg[:, 1, :], psum[:, 1, :], ACT.Silu).then_inc(s_silu, 1)
            pair_hi(act, 2, 2, 0)
            pair_silu(act, 0, 0)
            act.wait_ge(s_cT, 1)
            act.activation(combT[:], psum[:, 6, :], ACT.Copy).then_inc(s_combT, 1)
            act.wait_ge(s_pu, 1)
            with act.Fori(0, LOOPS) as it:
                for j in range(4):
                    act.wait_ge(s_pc, it * 4 + j + 1)
                    pair_hi(act, None, (j + 3) % 4, it + 1)
                    pair_silu(act, it * 4 + j + 1, (j + 1) % 2)
            act.wait_ge(s_pc, NP - 4)
            pair_hi(act, NP - 1, 3, NP // 4)
            for p in range(NP - 3, NP):
                pair_silu(act, p, p % 2)
            norm_scalar(act, 2)

        def pair_h1(dve, p, par):
            dve.wait_ge(s_silu, p + 2)
            dve.wait_ge(s_pu, p + 2)
            dve.tensor_tensor(h1[:, par, :], psum[:, 2 + par, :], sg[:, par, :], ALU.mult).then_inc(s_h1, 1)

        def pair_h(dve, p, par):
            dve.wait_ge(s_pc, p + 1)
            dve.wait_ge(s_h1, p + 2)
            dve.wait_ge(s_d, p)
            dve.tensor_tensor(hh[:, par, :], psum[:, 4 + par, :], h1[:, par, :], ALU.mult).then_inc(s_h, 1)

        def stage2_vector(dve):
            dve.wait_ge(s_th, 1)
            dve.wait_ge(s_in["route"], 16)
            dstep(dve, dve.tensor_scalar(score[:], score[:], 0.5, 0.5, ALU.mult, ALU.add))
            dstep(dve, dve.tensor_tensor(score[:], score[:],
                                         at["gbias"].rearrange("p (o e) -> p o e", o=1).broadcast_to([128, TT, E0]),
                                         ALU.add))
            by_group = score[:].rearrange("p t (g e) -> p (t g) e", g=G0)
            dstep(dve, dve.tensor_reduce(gsc[:].rearrange("p t g -> p (t g)"), by_group, AX, ALU.max))
            top_k(dve, gsc[:], G0, TG0, at["reset8"])
            dstep(dve, dve.tensor_tensor(by_group, by_group, bc(selg[:, 0:TT * G0], E0 // G0), ALU.mult))
            chosen = top_k(dve, score[:], E0, K0, at["reset64"])
            normalised(dve, score[:], chosen, E0, 1e-8)
            dstep(dve, dve.tensor_copy(combhl[:, :, 0:E0].bitcast(F32R), comb[:]))
            dve.tensor_tensor(combhl[:, :, E0:2 * E0], comb[:], combhl[:, :, 0:E0], ALU.subtract).then_inc(s_comb, 1)
            pair_h1(dve, -1, 1)
            dve.wait_ge(s_h1, 1)
            dve.tensor_copy(hh[:, 1, :], h1[:, 1, :]).then_inc(s_h, 1)
            pair_h1(dve, 0, 0)
            pair_h(dve, 0, 0)
            with dve.Fori(0, LOOPS) as it:
                for j in range(4):
                    pair_h1(dve, it * 4 + j + 1, (j + 1) % 2)
                    pair_h(dve, it * 4 + j + 1, (j + 1) % 2)
            for p in range(NP - 3, NP):
                pair_h1(dve, p, p % 2)
                pair_h(dve, p, p % 2)
            norm_vector(dve, 2, x_tok[:])
            norm_lo(dve, 2)

        def pair_gate_up(pe, p, slot, par):
            pe.wait_ge(s_wlo, p + 2)
            if not isinstance(p, int) or p > 0:
                pe.wait_ge(s_h1, p)
            three(pe, psum[:, par, :], whi[:, slot, 0:128], wlo[:, slot, 0:128], xh[:], xl[:]).then_inc(s_pg, 1)
            three(pe, psum[:, 2 + par, :], whi[:, slot, 128:256], wlo[:, slot, 128:256], xh[:], xl[:]).then_inc(s_pu, 1)

        def pair_spread(pe, p, slot, par):
            if not isinstance(p, int) or p > 1:
                pe.wait_ge(s_h, p)
            pe.matmul(psum[:, 4 + par, :], whi[:, slot, 256:384], combT[:], start=True, stop=True).then_inc(s_pc, 1)

        def pair_down(pe, p, slot, par, turn, first=False, last=False, done=s_d):
            pe.wait_ge(s_dw[slot], turn * 16 + 16)
            pe.wait_ge(s_h, p + 2)
            for i in range(TT):
                ins = pe.matmul(Y[:, i, :], hh[:, par, i * 128:i * 128 + 128], rawd[:, slot, :],
                                start=first and i == 0, stop=last, skip_group_check=True)
            ins.then_inc(done, 1)

        def stage2_tensor(pe):
            pe.wait_ge(s_xh, 2)
            pe.wait_ge(s_const, 1)
            pe.wait_ge(s_xl, 1)
            for i in range(TT):
                t = slice(i * 128, i * 128 + 128)
                ins = three(pe, psum[:, 5, i * E0:i * E0 + E0], xh[:, t], xl[:, t], gwh[:], gwl[:])
            ins.then_inc(s_lg, 1)
            pair_gate_up(pe, -1, 3, 1)
            pair_gate_up(pe, 0, 0, 0)
            pe.wait_ge(s_comb, 1)
            for i in range(TT):
                ins = pe.transpose(psum[:, 6, i * 128:i * 128 + 128], combhl[:, i, :], ident)
            ins.then_inc(s_cT, 1)
            pair_gate_up(pe, 1, 1, 1)
            pe.wait_ge(s_combT, 1)
            pair_spread(pe, 0, 0, 0)
            pair_down(pe, -1, 3, 1, 0, first=True)
            pair_spread(pe, 1, 1, 1)
            with pe.Fori(0, LOOPS) as it:
                for j in range(4):
                    pair_gate_up(pe, it * 4 + j + 2, (j + 2) % 4, j % 2)
                    pair_down(pe, it * 4 + j, j, j % 2, it + j // 3)
                    pair_spread(pe, it * 4 + j + 2, (j + 2) % 4, j % 2)
            for p in range(NP - 4, NP):
                if p + 2 < NP:
                    pair_gate_up(pe, p + 2, (p + 2) % 4, p % 2)
                end = p == NP - 1
                pair_down(pe, p, p % 4, p % 2, (p + 1) // 4, last=end, done=s_y if end else s_d)
                if p + 2 < NP:
                    pair_spread(pe, p + 2, (p + 2) % 4, p % 2)
            norm_tensor(pe, 2)

        wsr = sb("head_w_raw", [128, 2, 384], stack=late)
        wqk = sb("head_qk_w_hi_lo", [128, 2, 256], F32R, stack=late)
        wv = sb("head_v_w_hi_lo", [128, 2, 2, 128], F32R, stack=late)
        QH = sb("q_hi", [128, 2, T], F32R, stack=late)
        QL = sb("q_lo", [128, 2, T], F32R, stack=late)
        KH = sb("k_hi", [128, 2, NB, 2, S], F32R, stack=late)
        KL = sb("k_lo", [128, 2, NB, 2, S], F32R, stack=late)
        Vv = hh[:].rearrange("p a (t d) -> p a t d", t=TT)
        PL = sg[:].rearrange("p a (b m) -> p (a b) m", b=2)
        PTs = raw[:].rearrange("p a w -> p (a w)").rearrange("p (a w) -> p a w", a=3)
        PE_ = sb("probs_early", [128, 4, 128], stack=late)
        nmx = sb("minus_max", [128, 8], stack=late)
        sums = sb("prob_sums", [128, 2, 8], stack=late)
        rsum = sb("prob_sums_inverse", [128, 8], stack=late)
        On = sb("attended_normed", [128, 8, KQ], stack=late)
        OTs = sb("attended_T", [128, T], stack=late)
        SCALE3 = 1.0 / float(np.sqrt(KQ))

        s_wsr = [sem(f"head_w_loaded_{i}") for i in range(2)]
        s_wsh = sem("head_w_hi_made")
        s_ws = sem("head_w_made")
        s_jq = sem("head_q")
        s_jk = sem("head_k")
        s_jv = sem("head_v")
        s_qh = sem("head_q_hi")
        s_kh = sem("head_k_hi")
        s_ql = sem("head_q_lo")
        s_kl = sem("head_k_lo")
        s_vv = sem("head_v_copied")
        s_S = sem("head_scores")
        s_mx = sem("head_max")
        s_nm = sem("head_minus_max")
        s_ex = sem("head_exp")
        s_pt = sem("head_probs_T")
        s_pta = sem("head_probs_T_copied_act")
        s_ptd = sem("head_probs_T_copied_dve")
        s_pv = sem("head_attended")
        s_rs = sem("head_sums_inverted")
        s_on = sem("head_normed")
        s_otp = sem("head_attended_T")
        s_ot = sem("head_attended_T_copied")
        heads_o = at["wo"].rearrange("p (n w) -> p n w", n=HP)
        TILE_OF = (1, 3, 0, 2)
        sc_late = lambda b: psum[:, 3 + b, :].rearrange("p (h m) -> p h m", h=2)
        sc_early = psum[:, 5, :].rearrange("p (b h m) -> p b h m", b=NB, h=2)

        def stage3_load(sp, n, slot):
            sp.dma_start(wsr[:, slot, :], heads_w[n, :, :]).then_inc(s_wsr[slot], 16)

        def stage3_sync(sp):
            sp.wait_ge(s_xn, 2)
            stage3_load(sp, 0, 0)
            stage3_load(sp, 1, 1)
            with sp.Fori(0, HP // 2 - 1) as it:
                for j in range(2):
                    sp.wait_ge(s_ws, it * 2 + j + 1)
                    stage3_load(sp, it * 2 + j + 2, j)

        def head_split(pool, n, par, turn):
            pool.wait_ge(s_wsr[par], turn * 16 + 16)
            one = lambda w: one1[:].broadcast_to([128, w])
            pool.tensor_tensor(wqk[:, 0, :], wsr[:, par, 0:256], one(256), ALU.mult)
            pool.tensor_tensor(wv[:, par, 0, :], wsr[:, par, 256:384], one(128), ALU.mult).then_inc(s_wsh, 1)
            pool.wait_ge(s_wsh, n + 1)
            pool.tensor_tensor(wqk[:, 1, :], wsr[:, par, 0:256], wqk[:, 0, :].bitcast(F32), ALU.subtract)
            pool.tensor_tensor(wv[:, par, 1, :], wsr[:, par, 256:384], wv[:, par, 0, :].bitcast(F32),
                               ALU.subtract).then_inc(s_ws, 1)

        def stage3_pool(pool):
            pstep(pool, pool.memset(one1[:], 1.0))
            head_split(pool, 0, 0, 0)
            pool.wait_ge(s_jk, 1)
            head_split(pool, 1, 1, 0)
            with pool.Fori(0, HP // 2 - 1) as it:
                for j in range(2):
                    n = it * 2 + j + 2
                    pool.wait_ge(s_jk, n)
                    pool.wait_ge(s_jv, n - 1)
                    head_split(pool, n, j, it + 1)
            stage4_early_pool(pool)
            norm_pool(pool, 3)

        def head_project_qk(pe, n):
            pe.wait_ge(s_ws, n + 1)
            three(pe, psum[:, 0, :], wqk[:, 0, 0:128], wqk[:, 1, 0:128], xh[:], xl[:]).then_inc(s_jq, 1)
            three(pe, psum[:, 1, :], wqk[:, 0, 128:256], wqk[:, 1, 128:256], xh[:], xl[:]).then_inc(s_jk, 1)

        def head_project_v(pe, par):
            for i in range(TT):
                t = slice(i * 128, i * 128 + 128)
                ins = three(pe, psum[:, 2, t], xh[:, t], xl[:, t], wv[:, par, 0, :], wv[:, par, 1, :])
            ins.then_inc(s_jv, 1)

        def head_scores(pe, n, par):
            pe.wait_ge(s_ql, n + 1)
            pe.wait_ge(s_kl, n + 1)
            for b in range(NB):
                q = slice(b * S + 128, b * S + 256)
                o_ = sc_late(b)
                three(pe, o_, QH[:, par, q], QL[:, par, q], KH[:, par, b, :, :], KL[:, par, b, :, :], stop=False)
                pe.matmul(o_[:, :, 128:256], identr[:],
                          causr[:].rearrange("p (o m) -> p o m", o=1).broadcast_to([128, 2, 128]),
                          start=False, stop=True)
                q = slice(b * S, b * S + 128)
                o_ = sc_early[:, b, :, :]
                three(pe, o_, QH[:, par, q], QL[:, par, q], KH[:, par, b, :, 0:128],
                      KL[:, par, b, :, 0:128], stop=False)
                ins = pe.matmul(o_, identr[:],
                                causr[:].rearrange("p (o m) -> p o m", o=1).broadcast_to([128, 2, 128]),
                                start=False, stop=True)
            ins.then_inc(s_S, 1)

        def head_turn(pe, n):
            pe.wait_ge(s_ex, n + 1)
            for b in range(NB):
                for h in range(2):
                    k = 2 * b + h
                    pe.transpose(psum[:, b, h * S:h * S + 128], PE_[:, k, :], ident)
                    pe.transpose(psum[:, b, h * S + 128:h * S + 256], PL[:, k, 0:128], ident)
            for k in range(4):
                ins = pe.transpose(psum[:, 2, k * 128:k * 128 + 128], PL[:, k, 128:256], ident)
            ins.then_inc(s_pt, 1)

        def head_attend(pe, n, par):
            pe.wait_ge(s_pta, n + 1)
            pe.wait_ge(s_ptd, n + 1)
            for late in (1, 0):
                for b in range(NB):
                    for h in range(2):
                        k = 2 * b + h
                        o_ = psum[:, 6, (k + 4 * (1 - late)) * KQ:(k + 4 * (1 - late)) * KQ + KQ]
                        c = h * S + 128 * late
                        v = slice(h * KQ, h * KQ + KQ)
                        ins = pe.matmul(o_, PTs[:, b, c:c + 128], Vv[:, par, 2 * b, v], start=True, stop=not late)
                        if late:
                            ins = pe.matmul(o_, PTs[:, 2, k * 128:k * 128 + 128], Vv[:, par, 2 * b + 1, v],
                                            start=False, stop=True)
            ins.then_inc(s_pv, 1)

        def head_turn_output(pe, n):
            pe.wait_ge(s_on, n + 1)
            for k in range(4):
                c = TILE_OF[k] * 128
                ins = pe.transpose(psum[:, 6, c:c + 128], On[:, 2 * k:2 * k + 2, :].rearrange("p a d -> p (a d)"), ident)
            ins.then_inc(s_otp, 1)

        def head_output(pe, n, last=False):
            pe.wait_ge(s_ot, n + 1)
            for i in range(TT):
                ins = pe.matmul(Y[:, i, :], OTs[:, i * 128:i * 128 + 128], heads_o[:, n, :],
                                start=False, stop=last, skip_group_check=True)
            if last:
                ins.then_inc(s_y, 1)

        def stage3_tensor(pe):
            pe.wait_ge(s_xh, 3)
            pe.matmul(psum[:, 7, :], ident, x_tok[:].rearrange("p t d -> p (t d)"), start=True, stop=False,
                      skip_group_check=True)
            pe.wait_ge(s_xl, 2)
            head_project_qk(pe, 0)
            head_project_v(pe, 0)
            head_scores(pe, 0, 0)
            head_project_qk(pe, 1)
            pe.wait_ge(s_vv, 1)
            head_project_v(pe, 1)
            pe.wait_ge(s_ql, 2)
            pe.wait_ge(s_kl, 2)
            head_project_qk(pe, 2)

            def step(n, par, first=False, scores=True, qk=True, v=True):
                if v:
                    pe.wait_ge(s_ql, n + 3)
                    pe.wait_ge(s_kl, n + 3)
                if scores:
                    pe.wait_ge(s_vv, n + 2)
                head_turn(pe, n)
                if scores:
                    head_scores(pe, n + 1, 1 - par)
                if qk:
                    pe.wait_ge(s_pta, n + 1)
                    pe.wait_ge(s_ptd, n + 1)
                    head_project_qk(pe, n + 3)
                head_attend(pe, n, par)
                if v:
                    head_project_v(pe, par)
                if not first:
                    head_output(pe, n - 1)
                head_turn_output(pe, n)

            step(0, 0, first=True)
            with pe.Fori(0, (HP - 4) // 2) as it:
                for j in range(2):
                    step(it * 2 + j + 1, 1 - j)
            step(HP - 3, 1, qk=False)
            step(HP - 2, 0, qk=False, v=False)
            step(HP - 1, 1, scores=False, qk=False, v=False)
            head_output(pe, HP - 1, last=True)
            norm_tensor(pe, 3)

        def head_hi(act, n, par):
            act.wait_ge(s_jq, n + 1)
            act.activation(QH[:, par, :], psum[:, 0, :], ACT.Copy).then_inc(s_qh, 1)
            act.wait_ge(s_jk, n + 1)
            for h in range(2):
                ins = act.activation(KH[:, par, :, h, :], psum[:, 1, :].rearrange("p (b m) -> p b m", b=NB), ACT.Copy,
                                     scale=at["half"][:, h:h + 1])
            ins.then_inc(s_kh, 1)

        def head_exps(act, n, par):
            act.wait_ge(s_nm, n + 1)
            for k in range(4):
                act.activation(PL[:, k, :], sc_late(k // 2)[:, k % 2, :], ACT.Exp, bias=nmx[:, k:k + 1],
                               scale=SCALE3, accum_out=sums[:, par, k:k + 1])
            for k in range(4):
                ins = act.activation(PE_[:, k, :], sc_early[:, k // 2, k % 2, :], ACT.Exp,
                                     bias=nmx[:, 4 + k:5 + k], scale=SCALE3, accum_out=sums[:, par, 4 + k:5 + k])
            ins.then_inc(s_ex, 1)

        def stage3_scalar(act):
            head_hi(act, 0, 0)
            head_exps(act, 0, 0)
            head_hi(act, 1, 1)
            head_hi(act, 2, 0)

            def step(n, par, scores=True, qk=True):
                act.wait_ge(s_pt, n + 1)
                act.activation(PTs[:, 0, :], psum[:, 0, :], ACT.Copy).then_inc(s_pta, 1)
                if qk:
                    head_hi(act, n + 3, 1 - par)
                if scores:
                    head_exps(act, n + 1, 1 - par)
                act.wait_ge(s_otp, n + 1)
                act.activation(OTs[:], psum[:, 6, :], ACT.Copy).then_inc(s_ot, 1)

            step(0, 0)
            with act.Fori(0, (HP - 4) // 2) as it:
                for j in range(2):
                    step(it * 2 + j + 1, 1 - j)
            step(HP - 3, 1, qk=False)
            step(HP - 2, 0, qk=False)
            step(HP - 1, 1, scores=False, qk=False)
            norm_scalar(act, 3)

        def head_lo(dve, n, par):
            dve.wait_ge(s_qh, n + 1)
            dve.tensor_tensor(QL[:, par, :], psum[:, 0, :], QH[:, par, :].bitcast(F32), ALU.subtract).then_inc(s_ql, 1)
            dve.wait_ge(s_kh, n + 1)
            for h in range(2):
                ins = dve.scalar_tensor_tensor(KL[:, par, :, h, :], psum[:, 1, :].rearrange("p (b m) -> p b m", b=NB),
                                               at["half"][:, h:h + 1], KH[:, par, :, h, :].bitcast(F32),
                                               ALU.mult, ALU.subtract)
            ins.then_inc(s_kl, 1)

        def head_v(dve, n, par):
            dve.wait_ge(s_jv, n + 1)
            dve.tensor_copy(Vv[:, par, :, :], tiles(psum[:, 2, :])).then_inc(s_vv, 1)

        def head_max(dve, n):
            dve.wait_ge(s_S, n + 1)
            dve.tensor_reduce(nmx[:, 0:4], psum[:, 3:5, :].rearrange("p a (h m) -> p (a h) m", h=2), AX, ALU.max)
            dve.tensor_reduce(nmx[:, 4:8], sc_early.rearrange("p b h m -> p (b h) m"), AX, ALU.max).then_inc(s_mx, 1)
            dve.wait_ge(s_mx, n + 1)
            dve.tensor_scalar(nmx[:], nmx[:], -SCALE3, None, ALU.mult).then_inc(s_nm, 1)

        def stage3_vector(dve):
            head_lo(dve, 0, 0)
            head_v(dve, 0, 0)
            head_max(dve, 0)
            head_lo(dve, 1, 1)
            head_v(dve, 1, 1)
            head_lo(dve, 2, 0)

            def step(n, par, scores=True, qk=True, v=True):
                dve.wait_ge(s_pt, n + 1)
                dve.tensor_copy(PTs[:, 1:3, :], psum[:, 1:3, :]).then_inc(s_ptd, 1)
                dve.reciprocal(rsum[:], sums[:, par, :]).then_inc(s_rs, 1)
                if scores:
                    head_max(dve, n + 1)
                if qk:
                    head_lo(dve, n + 3, 1 - par)
                dve.wait_ge(s_pv, n + 1)
                dve.wait_ge(s_rs, n + 1)
                dve.tensor_tensor(On[:], psum[:, 6, :].rearrange("p (k d) -> p k d", d=KQ), bc(rsum[:], KQ),
                                  ALU.mult).then_inc(s_on, 1)
                if v:
                    head_v(dve, n + 2, par)

            step(0, 0)
            with dve.Fori(0, (HP - 4) // 2) as it:
                for j in range(2):
                    step(it * 2 + j + 1, 1 - j)
            step(HP - 3, 1, qk=False)
            step(HP - 2, 0, qk=False, v=False)
            step(HP - 1, 1, scores=False, qk=False, v=False)
            norm_vector(dve, 3, None)
            norm_lo(dve, 3)

        SCALE4 = 1.0 / float(np.sqrt(np.float32(HD)))
        UNITS = 64
        AHEAD = 18
        LAG = 3
        QBANK = (7, 4, 5, 6)

        s_qw = sem("q4_w_split")
        s_mz = sem("max4_cleared")
        s_qp = sem("q4_projected")
        s_qe = sem("q4_copied")
        s_qy = sem("q4_split_made")
        s_qx = sem("q4_heads_made")
        s_xs = sem("scores4_by_query")
        s_xm = sem("max4_taken")
        s_xt = sem("max4_T")
        s_xqa = sem("max4_in_operand_act")
        s_xqd = sem("max4_in_operand_dve")
        s_ST = sem("scores4_by_key")
        s_xe = sem("exp4_and_hi")
        s_lod = sem("exp4_lo_by_dve")
        s_lop = sem("exp4_lo_by_pool")
        s_vp = sem("v4_padded_made")
        s_xp = sem("attended4_summed")
        s_xc = sem("attended4_copied")
        s_xr = sem("attended4_by_tokens")
        s_xo = sem("attended4_normed")
        s_x4t = sem("attended4_turned")
        s_x4c = sem("attended4_turned_copied")
        O4 = tiles(psum[:, 7, :])[:, :, 0:4 * VW].rearrange("p t (h d) -> p t h d", h=4)
        unit = lambda ap: ap.rearrange("p a w -> p (a w)").rearrange("p (u w) -> p u w", w=512)
        Pf = [unit(raw[:])[:, i, :] for i in range(3)] + [unit(rawd[:])[:, 0, :]]
        Ph = [unit(whi[:])[:, i, :] for i in range(3)] + [unit(wlo[:])[:, 0, :]]

        def q4_heads(eng, t, j):
            return eng.tensor_scalar(Qx[:, t, j, :], yq[:, t % 2, :], at["sel"][:, SEL_HEAD + j:SEL_HEAD + j + 1],
                                     at["sel"][:, SEL_MASK:SEL_MASK + 1], ALU.mult, ALU.add)

        def exp4_lo(eng, n, done):
            eng.wait_ge(s_xe, n + 1)
            eng.tensor_tensor(Pl[:, n % 4, :], Pf[n % 4], Ph[n % 4].bitcast(F32),
                              ALU.subtract).then_inc(done, 1)

        def v4_pad(pool, t):
            for j in range(4):
                ins = pool.tensor_tensor(VP[:, t % 2, :, j, j * VW:j * VW + VW], Vx[:, :, 4 * t + j, :].bitcast(F32),
                                         one1[:].rearrange("p (o q) -> p o q", o=1).broadcast_to([128, C // 128, VW]),
                                         ALU.mult)
            ins.then_inc(s_vp, 1)

        def stage4_early_pool(pool):
            pstep(pool, pool.tensor_copy(Qrh[:], at["Qr_w"]))
            pool.tensor_tensor(Qrl[:], at["Qr_w"], Qrh[:].bitcast(F32), ALU.subtract).then_inc(s_qw, 1)
            pool.memset(mxt[:], 0.0).then_inc(s_mz, 1)
            pstep(pool, pool.memset(VP[:].bitcast(F32), 0.0))
            v4_pad(pool, 0)
            v4_pad(pool, 1)

        def stage4_pool(pool):
            pool.wait_ge(s_qy, 2)
            for j in range(4):
                ins = q4_heads(pool, 1, j)
            ins.then_inc(s_qx, 1)
            for n in range(3, UNITS, 4):
                exp4_lo(pool, n, s_lop)
                if n < 16:
                    t = 2 + n // 8
                    pool.wait_ge(s_qy, t + 1)
                    q4_heads(pool, t, n // 4 % 2 * 2)
                    ins = q4_heads(pool, t, n // 4 % 2 * 2 + 1)
                    if n // 4 % 2:
                        ins.then_inc(s_qx, 1)
                if n in (19, 35):
                    t = 2 + n // 35
                    pool.wait_ge(s_xp, 16 * (t - 1))
                    v4_pad(pool, t)
                if n == 23:
                    pool.tensor_tensor(res[:], x_tok[:],
                                       at["bo"].rearrange("p (o d) -> p o d", o=1).broadcast_to([128, TT, D]),
                                       ALU.add).then_inc(s_res, 1)
            norm_pool(pool, 4)

        def q4_project(pe, t):
            w = slice(t * D, t * D + D)
            three(pe, psum[:, QBANK[t], :], Qrh[:, w], Qrl[:, w], xh[:], xl[:]).then_inc(s_qp, 1)

        def q4_scores(pe, w):
            t, j, u = w // 16, w // 4 % 4, w % 4
            if w % 16 == 0:
                pe.wait_ge(s_qx, t + 1)
            if w >= 4:
                pe.wait_ge(s_xm, (w - 4) // 2 + 1)
            pe.matmul(psum[:, u, :], Qx[:, t, j, u * 128:u * 128 + 128], KX[:, t, u // 2 * SC:u // 2 * SC + SC],
                      start=True, stop=True).then_inc(s_xs, 1)

        def q4_turn(pe, t):
            pe.wait_ge(s_xm, 8 * (t + 1))
            if t >= 2:
                pe.wait_ge(s_xo, t - 1)
            for i in range(TT):
                ins = pe.transpose(psum[:, 7, i * 128:i * 128 + 128], mxt[:, i, :], ident)
            ins.then_inc(s_xt, 1)

        def k4_scores(pe, n):
            t, j, b = n // 16, n // 4 % 4, n // 2 % 2
            if n % 16 == 0:
                pe.wait_ge(s_xqa, t + 1)
                pe.wait_ge(s_xqd, t + 1)
            if n >= 2:
                pe.wait_ge(s_xe, n - 1)
            for a in range(2):
                k = b * SC + (n % 2 * 2 + a) * 128
                ins = pe.matmul(psum[:, 4 + n % 2, a * S:a * S + S], KX[:, t, k:k + 128],
                                Qx[:, t, j, b * S:b * S + S], start=True, stop=True)
            ins.then_inc(s_ST, 1)

        def v4_attend(pe, n):
            t, j, b = n // 16, n // 4 % 4, n // 2 % 2
            if n % 4 == 3:
                pe.wait_ge(s_lop, n // 4 + 1)
            else:
                pe.wait_ge(s_lod, n // 4 * 3 + n % 4 + 1)
            if n % 16 == 0:
                pe.wait_ge(s_vp, t + 1)
                if t:
                    pe.wait_ge(s_xc, t)
            for a in range(2):
                for p in (Ph[n % 4], Pl[:, n % 4, :]):
                    ins = pe.matmul(psum[0:4 * VW, 6, b * S:b * S + S], VP[:, t % 2, 4 * b + n % 2 * 2 + a, j, :],
                                    p[:, a * S:a * S + S], start=n % 16 == 0 and a == 0 and p is Ph[n % 4],
                                    stop=n % 16 == 15 and a == 1 and p is not Ph[n % 4],
                                    skip_group_check=True)
            ins.then_inc(s_xp, 1)

        def v4_turn(pe, t):
            pe.wait_ge(s_xc, t + 1)
            for i in range(TT):
                ins = pe.transpose(psum[:, 7, i * 128:i * 128 + 4 * VW], OS[0:4 * VW, i * 128:i * 128 + 128],
                                   ident[0:4 * VW, 0:4 * VW])
            ins.then_inc(s_xr, 1)

        def stage4_tensor(pe):
            pe.wait_ge(s_xh, 4)
            pe.wait_ge(s_xl, 3)
            pe.wait_ge(s_qw, 1)
            pe.wait_ge(s_kx, 1)
            pe.wait_ge(s_mz, 1)
            for t in range(4):
                q4_project(pe, t)
            for w in range(AHEAD):
                q4_scores(pe, w)
            q4_turn(pe, 0)
            pe.wait_ge(s_qe, 4)
            for n in range(UNITS + LAG):
                if n < UNITS - AHEAD:
                    q4_scores(pe, n + AHEAD)
                if n < UNITS:
                    k4_scores(pe, n)
                if n >= LAG:
                    v4_attend(pe, n - LAG)
                if n % 16 == 5 and n > 16:
                    v4_turn(pe, n // 16 - 1)
                if n % 16 == 14 and n + 2 < UNITS:
                    q4_turn(pe, n // 16 + 1)
            v4_turn(pe, 3)
            pe.wait_ge(s_xo, 4)
            for i in range(TT):
                ins = pe.transpose(psum[:, 0, i * 128:i * 128 + 128], att4[:, i, :], ident)
            ins.then_inc(s_x4t, 1)
            pe.wait_ge(s_x4c, 1)
            for i in range(TT):
                ins = pe.matmul(Y[:, i, :], aT4[:, i * 128:i * 128 + 128], at["O_w"], start=True, stop=True)
            ins.then_inc(s_y, 1)
            norm_tensor(pe, 4)

        def stage4_scalar(act):
            act.wait_ge(s_in["masked"], 16)

            def q_copy(t):
                act.wait_ge(s_qp, t + 1)
                if t >= 2:
                    act.wait_ge(s_qy, t - 1)
                b = at["qb"][:, t:t + 1]
                act.activation(xq[:, t % 2, :], psum[:, QBANK[t], :], ACT.Identity, bias=b)
                act.activation(rq[:, t % 2, :], psum[:, QBANK[t], :], ACT.Identity, bias=b).then_inc(s_qe, 1)

            def put_max(t):
                act.wait_ge(s_xt, t + 1)
                act.wait_ge(s_qx, t + 1)
                act.wait_ge(s_xqd, t + 1)
                for j in range(2):
                    ins = act.activation(Qx[MR:128, t, j, :], psum[MR:128, 7, :], ACT.Identity,
                                         scale=at["sel"][MR:128, SEL_MAX + j:SEL_MAX + j + 1],
                                         bias=at["sel"][MR:128, SEL_MASK:SEL_MASK + 1])
                ins.then_inc(s_xqa, 1)

            def o_copy(t):
                act.wait_ge(s_xp, 16 * t + 16)
                act.activation(OS[0:4 * VW, :], psum[0:4 * VW, 6, :], ACT.Copy).then_inc(s_xc, 1)

            for t in range(4):
                q_copy(t)
            put_max(0)
            for n in range(UNITS):
                act.wait_ge(s_ST, n + 1)
                if n >= 4:
                    act.wait_ge(s_xp, n - 3)
                act.activation(Pf[n % 4], psum[:, 4 + n % 2, :], ACT.Exp, scale=SCALE4)
                act.activation(Ph[n % 4], psum[:, 4 + n % 2, :], ACT.Exp, scale=SCALE4).then_inc(s_xe, 1)
                if n % 16 == 2 and n > 16:
                    o_copy(n // 16 - 1)
                if n % 16 == 15 and n + 1 < UNITS:
                    put_max(n // 16 + 1)
            o_copy(3)
            act.wait_ge(s_x4t, 1)
            act.activation(aT4[:], psum[:, 0, :], ACT.Copy).then_inc(s_x4c, 1)
            norm_scalar(act, 4)

        def stage4_vector(dve):
            dve.wait_ge(s_mz, 1)

            def q_split(t):
                dve.wait_ge(s_qe, t + 1)
                if t > 2:
                    dve.wait_ge(s_qx, t - 1)
                dve.scalar_tensor_tensor(yq[:, t % 2, :], rq[:, t % 2, :].bitcast(F32),
                                         at["sel"][:, SEL_LO_Q:SEL_LO_Q + 1],
                                         xq[:, t % 2, :], ALU.mult, ALU.add).then_inc(s_qy, 1)

            def maxima(m):
                t, j, b = m // 8, m // 2 % 4, m % 2
                dve.wait_ge(s_xs, 2 * m + 2)
                if t and m % 8 == 0:
                    dve.wait_ge(s_xt, t)
                dve.tensor_reduce(mxt[:, 2 * b:2 * b + 2, MR + j], psum[:, 2 * b:2 * b + 2, :], AX,
                                  ALU.max).then_inc(s_xm, 1)

            def put_max(t):
                dve.wait_ge(s_xt, t + 1)
                dve.wait_ge(s_qx, t + 1)
                for j in range(2, 4):
                    ins = dve.tensor_scalar(Qx[MR:128, t, j, :], psum[MR:128, 7, :],
                                            at["sel"][MR:128, SEL_MAX + j:SEL_MAX + j + 1],
                                            at["sel"][MR:128, SEL_MASK:SEL_MASK + 1], ALU.mult, ALU.add)
                ins.then_inc(s_xqd, 1)

            def norm_heads(t):
                dve.wait_ge(s_xr, t + 1)
                dstep(dve, dve.reciprocal(rs4[:], O4[:, :, :, HD]))
                a = att4[:, :, t * 32:t * 32 + 32].rearrange("p t (h d) -> p t h d", h=4)
                r = rs4[:].rearrange("p t (h o) -> p t h o", o=1).broadcast_to([128, TT, 4, HD])
                dve.tensor_tensor(lo4[:], O4[:, :, :, HD + 1:VW], r, ALU.mult)
                dstep(dve, dve.tensor_tensor(a, O4[:, :, :, 0:HD], r, ALU.mult))
                dve.tensor_tensor(a, a, lo4[:], ALU.add).then_inc(s_xo, 1)

            q_split(0)
            dve.wait_ge(s_qy, 1)
            for j in range(4):
                ins = q4_heads(dve, 0, j)
            ins.then_inc(s_qx, 1)
            q_split(1)
            maxima(0)
            q_split(2)
            for m in range(1, 8):
                maxima(m)
            put_max(0)
            maxima(8)
            for n in range(UNITS):
                if n % 2 and n + AHEAD < UNITS:
                    maxima((n + AHEAD) // 2)
                if n % 4 < 3:
                    exp4_lo(dve, n, s_lod)
                if n == 7:
                    q_split(3)
                if n % 16 == 6 and n > 16:
                    norm_heads(n // 16 - 1)
                if n % 16 == 15 and n + 1 < UNITS:
                    put_max(n // 16 + 1)
            norm_heads(3)
            dve.wait_ge(s_res, 2)
            norm_vector(dve, 4, res[:])
            norm_lo(dve, 4)
        late.close()
        upr = sb("expert_up_raw", [128, 2, H1 + HC], stack=late5)
        dnr = sb("expert_down_raw", [128, 2, HC * D], stack=late5)
        fcb = sb("expert_up_bias", [128, 2, HC], stack=late5)
        fch = whi[:].rearrange("p a w -> p (a w)")[:, 0:2 * H1].rearrange("p (a w) -> p a w", a=2)
        fcl = wlo[:].rearrange("p a w -> p (a w)").rearrange("p (a w) -> p a w", a=2)
        hT = sb("expert_hidden", [128, 2, HC, T], stack=late5)
        acc = sb("experts_summed", [128, TT, D], stack=late5)
        p5 = sb("probs5", [128, TT, E1], stack=late5)
        mx5 = sb("max5", [128, TT], stack=late5)
        cT5 = sb("combine5_T", [E1, T], stack=late5)

        s_up = [sem(f"expert_up_loaded_{i}") for i in range(2)]
        s_dn = [sem(f"expert_down_loaded_{i}") for i in range(2)]
        s_fb = sem("expert_up_bias_copied")
        s_fh = sem("expert_up_hi_made")
        s_fl = sem("expert_up_lo_made")
        s_l5 = sem("logits5")
        s_d5 = sem("logits5_less_max")
        s_e5 = sem("exp5")
        s_c5 = sem("combine5")
        s_c5t = sem("combine5_turned")
        s_c5c = sem("combine5_turned_copied")
        s_fc = sem("expert_hidden_chunk_summed")
        s_ge = sem("expert_hidden_chunk_gelu")
        s_pj = sem("expert_output")
        s_ac = sem("expert_added")

        def load_up(sp, e, slot):
            sp.dma_start(upr[:, slot, :], up_w[e, :, :]).then_inc(s_up[slot], 16)

        def load_down(sp, e, slot):
            sp.dma_start(dnr[:, slot, :], down_w[e, :, :]).then_inc(s_dn[slot], 16)

        def stage5_sync(sp):
            sp.wait_ge(s_xn, 4)
            for e in range(2):
                load_up(sp, e, e)
                load_down(sp, e, e)
            with sp.Fori(0, E1 // 2 - 1) as it:
                for j in range(2):
                    sp.wait_ge(s_fb, it * 2 + j + 1)
                    load_up(sp, it * 2 + j + 2, j)
                    sp.wait_ge(s_pj, it * 2 + j + 1)
                    load_down(sp, it * 2 + j + 2, j)

        def expert_split(pool, e, par, turn):
            pool.wait_ge(s_up[par], turn * 16 + 16)
            pool.tensor_tensor(fch[:, par, :], upr[:, par, 0:H1], one1[:].broadcast_to([128, H1]),
                               ALU.mult).then_inc(s_fh, 1)
            pool.wait_ge(s_fh, e + 1)
            pool.tensor_tensor(fcl[:, par, :], upr[:, par, 0:H1], fch[:, par, :].bitcast(F32),
                               ALU.subtract).then_inc(s_fl, 1)
            pool.tensor_tensor(fcb[:, par, :], upr[:, par, H1:H1 + HC], one1[:].broadcast_to([128, HC]),
                               ALU.mult).then_inc(s_fb, 1)

        def stage5_pool(pool):
            expert_split(pool, 0, 0, 0)
            expert_split(pool, 1, 1, 0)
            with pool.Fori(0, E1 // 2 - 1) as it:
                for j in range(2):
                    pool.wait_ge(s_ge, it * 8 + j * 4 + 4)
                    expert_split(pool, it * 2 + j + 2, j, it + 1)
            norm_pool(pool, 5)

        def expert_up(pe, e, par, first=False):
            pe.wait_ge(s_fl, e + 1)
            for c in range(HC):
                if not first:
                    pe.wait_ge(s_ge, (e - 1) * 4 + c + 1)
                w = slice(c * 128, c * 128 + 128)
                three(pe, psum[:, c, :], fch[:, par, w], fcl[:, par, w], xh[:], xl[:]).then_inc(s_fc, 1)

        def expert_down(pe, e, par, turn):
            pe.wait_ge(s_dn[par], turn * 16 + 16)
            pe.wait_ge(s_ge, e * 4 + 4)
            pe.wait_ge(s_ac, e + 1)
            for i in range(TT):
                for c in range(HC):
                    ins = pe.matmul(psum[:, 4 + par, i * 128:i * 128 + 128], hT[:, par, c, i * 128:i * 128 + 128],
                                    dnr[:, par, c * D:c * D + D], start=c == 0, stop=c == HC - 1)
            ins.then_inc(s_pj, 1)

        def stage5_tensor(pe):
            pe.wait_ge(s_xh, 5)
            pe.wait_ge(s_xl, 4)
            for i in range(TT):
                t = slice(i * 128, i * 128 + 128)
                ins = three(pe, psum[:, 5, i * E1:i * E1 + E1], xh[:, t], xl[:, t], rwh[:], rwl[:])
            ins.then_inc(s_l5, 1)
            expert_up(pe, 0, 0, first=True)
            pe.wait_ge(s_c5, 1)
            for i in range(TT):
                ins = pe.transpose(psum[0:E1, 5, i * 128:i * 128 + 128], comb5[:, i, :], ident)
            ins.then_inc(s_c5t, 1)
            pe.wait_ge(s_c5c, 1)
            pe.wait_ge(s_in["bproj"], 16)
            for i in range(TT):
                ins = pe.matmul(Y[:, i, :], cT5[:, i * 128:i * 128 + 128], bpj[:], start=True, stop=True)
            ins.then_inc(s_y, 1)
            with pe.Fori(0, E1 // 2 - 1) as it:
                for j in range(2):
                    expert_up(pe, it * 2 + j + 1, 1 - j)
                    expert_down(pe, it * 2 + j, j, it)
            expert_up(pe, E1 - 1, 1)
            expert_down(pe, E1 - 2, 0, E1 // 2 - 1)
            expert_down(pe, E1 - 1, 1, E1 // 2 - 1)

        def expert_gelu(act, e, par):
            act.wait_ge(s_fb, e + 1)
            for c in range(HC):
                act.wait_ge(s_fc, e * 4 + c + 1)
                act.activation(hT[:, par, c, :], psum[:, c, :], ACT.Gelu_apprx_tanh,
                               bias=fcb[:, par, c:c + 1]).then_inc(s_ge, 1)

        def stage5_scalar(act):
            act.wait_ge(s_d5, 1)
            act.activation(p5[:], p5[:], ACT.Exp).then_inc(s_e5, 1)
            expert_gelu(act, 0, 0)
            act.wait_ge(s_c5t, 1)
            act.activation(cT5[:], psum[0:E1, 5, :], ACT.Copy).then_inc(s_c5c, 1)
            with act.Fori(0, E1 // 2 - 1) as it:
                for j in range(2):
                    expert_gelu(act, it * 2 + j + 1, 1 - j)
            expert_gelu(act, E1 - 1, 1)

        def expert_add(dve, e, par):
            dve.wait_ge(s_ac, e + 1)
            dve.wait_ge(s_pj, e + 1)
            for i in range(TT):
                ins = dve.scalar_tensor_tensor(acc[:, i, :], psum[:, 4 + par, i * 128:i * 128 + 128],
                                               comb5e[:, i, e, :], acc[:, i, :], ALU.mult, ALU.add)
            ins.then_inc(s_ac, 1)

        comb5 = comb[:].rearrange("p t e -> p (t e)")[:, 0:TT * E1].rearrange("p (t e) -> p t e", t=TT)
        comb5e = comb[:].rearrange("p t e -> p (t e)")[:, 0:TT * E1].rearrange("p (t e o) -> p t e o", t=TT, o=1)

        def stage5_vector(dve):
            lg = psum[:, 5, 0:TT * E1].rearrange("p (t e) -> p t e", t=TT)
            dve.wait_ge(s_l5, 1)
            dstep(dve, dve.tensor_reduce(mx5[:], lg, AX, ALU.max))
            dve.tensor_tensor(p5[:], lg, bc(mx5[:], E1), ALU.subtract).then_inc(s_d5, 1)
            dve.tensor_copy(acc[:], x_tok[:]).then_inc(s_ac, 1)
            dve.wait_ge(s_e5, 1)
            dstep(dve, dve.tensor_reduce(mx5[:], p5[:], AX, ALU.add))
            dstep(dve, dve.reciprocal(mx5[:], mx5[:]))
            dstep(dve, dve.tensor_tensor(p5[:], p5[:], bc(mx5[:], E1), ALU.mult))
            chosen = top_k(dve, p5[:], E1, K1, at["reset8"])
            normalised(dve, p5[:], chosen, E1, 0.0)
            dve.sem_inc(s_c5, 1)
            with dve.Fori(0, E1 // 2) as it:
                for j in range(2):
                    expert_add(dve, it * 2 + j, j)
            dve.wait_ge(s_ac, E1 + 1)
            norm_vector(dve, 5, acc[:])

        late5.close()

        late4.close()


        @block.sync
        def _(sp):
            sp.dma_start(pk["ident"][:], packs["ident"]).then_inc(s_in["ident"], 16)
            sp.dma_start(pk["front"][:], packs["front"]).then_inc(s_in["front"], 16)
            sp.dma_start(rowb[:], rows.broadcast_to([128, width(ROWS)])).then_inc(s_in["rows"], 16)
            for n in ("cross", "route"):
                sp.dma_start(pk[n][:], packs[n]).then_inc(s_in[n], 16)
            sp.dma_start(maskb[MR:128, :], maskin.broadcast_to([128 - MR, C])).then_inc(s_in["mask"], 16)
            sp.dma_start(bpj[:], bproj).then_inc(s_in["bproj"], 16)
            for n in ("masked", "heads"):
                sp.dma_start(pk[n][:], packs[n]).then_inc(s_in[n], 16)
            stage2_sync(sp)
            stage3_sync(sp)
            stage5_sync(sp)
            sp.wait_ge(s_xn, 6)
            sp.dma_start(out, x_tok[:]).then_inc(s_out, 16)
            sp.wait_ge(s_out, 16)

        @block.tensor
        def _(pe):
            stage0_tensor(pe)
            stage1_tensor(pe)
            stage2_tensor(pe)
            stage3_tensor(pe)
            stage4_tensor(pe)
            stage5_tensor(pe)

        @block.vector
        def _(dve):
            stage0_vector(dve)
            stage1_vector(dve)
            stage2_vector(dve)
            stage3_vector(dve)
            stage4_vector(dve)
            stage5_vector(dve)

        @block.scalar
        def _(act):
            stage0_scalar(act)
            stage1_scalar(act)
            stage2_scalar(act)
            stage3_scalar(act)
            stage4_scalar(act)
            stage5_scalar(act)

        @block.gpsimd
        def _(pool):
            stage0_pool(pool)
            stage1_pool(pool)
            stage2_pool(pool)
            stage3_pool(pool)
            stage4_pool(pool)
            stage5_pool(pool)


def kernel(**inputs):
    import concourse.bacc as bacc
    from concourse.bass_utils import run_bass_kernel_spmd

    g = {k: np.asarray(v) for k, v in inputs.items()}
    f = np.float32

    def col(v):
        return v.reshape(-1, 1)

    def tok(v):
        return v.reshape(-1, 128, v.shape[-1]).transpose(1, 0, 2).reshape(128, -1)

    part = np.arange(128)
    heads_of = (part[:, None] // HD == np.arange(NH)[None, :]).astype(f)
    blocks = (part[:, None] // HD == part[None, :] // HD).astype(f)
    causal = np.where(part[None, :] > part[:, None], f(NEG), f(0))
    half = np.stack([part < 64, part >= 64], 1).astype(f)
    sel = np.zeros((128, 12), f)
    sel[:, SEL_LO_Q] = -((part < MR) & (part % HR // HD == 2)).astype(f)
    sel[:, SEL_LO_K] = -((part < MR) & (part % HR // HD == 1)).astype(f)
    for j in range(4):
        sel[:, SEL_HEAD + j] = part // HR == j
        sel[:, SEL_MAX + j] = -(part == MR + j).astype(f)
    sel[:, SEL_MASK] = part == KR
    sel[:, SEL_MAXES] = (part >= MR) & (part < MR + 4)

    def packed_heads(w):
        w3 = np.repeat(w.reshape(4, 4, 1, HD, -1), 3, axis=2).reshape(4, MR, -1)
        return np.concatenate([w3, np.zeros((4, 128 - MR, w3.shape[-1]), f)], axis=1)

    def packed_w(w):
        return packed_heads(w).transpose(2, 0, 1).reshape(128, -1)

    def packed_b(b):
        return packed_heads(b.reshape(D, 1))[:, :, 0].T

    pair = (np.arange(NP)[:, None, None] * 2 + part[None, None, :] // I0)
    row = part[None, :, None] % E0
    spread = (row == pair).astype(f)
    up = lambda w: w.reshape(NP, 2 * I0, D).transpose(0, 2, 1)
    down = g["L0_ffn_ed_w"].reshape(NP, 2, D, I0).transpose(0, 1, 3, 2).reshape(NP, 2 * I0, D)
    routed = np.concatenate([up(g["L0_ffn_eg_w"]), up(g["L0_ffn_eu_w"]), spread], axis=2)
    shared = np.concatenate([g["L0_ffn_sg_w"].T, g["L0_ffn_su_w"].T, np.zeros((128, 128), f)], axis=1)

    qkv = np.stack([g["L1_attn_w_q"], g["L1_attn_w_k"], g["L1_attn_w_v"]], 1)
    qkv = qkv.reshape(D, 3, HP, 2 * KQ).transpose(2, 0, 1, 3).reshape(HP, D, -1)
    wo = g["L1_attn_w_o"].reshape(D, HP, 2 * KQ).transpose(2, 1, 0).reshape(128, -1)
    reset = lambda n: np.broadcast_to((np.arange(TT * n) % n != 0).astype(f), (128, TT * n))

    parts = {
        "xT": g["x"].reshape(T, D).T, "WqT": g["L0_attn_Wq"].T,
        "WkvT": np.concatenate([g["L0_attn_Wk"].T, g["L0_attn_Wv"].T], 1),
        "conv": np.concatenate([g["L0_attn_conv_w"], col(g["L0_attn_conv_b"])], 1),
        "blocks": blocks, "heads": heads_of, "ident": np.eye(128, dtype=f),
        "x_tok": tok(g["x"].reshape(T, D)), "WpT": g["L0_attn_Wp"].T,
        "ctxT": g["ctx_1024"].reshape(C, D).T,
        "KsT_w": g["L0_xattn_Wk_s"].T, "QsT_w": g["L0_xattn_Wq_s"].T, "Vs_w": g["L0_xattn_Wv_s"].T,
        "QcT_w": g["L0_xattn_Wq_c"].T, "KcT_w": g["L0_xattn_Wk_c"].T, "Vc_w": g["L0_xattn_Wv_c"].T,
        "gate_w": np.concatenate([g["L0_xattn_Wg"][:, :D].T, g["L0_xattn_Wg"][:, D:].T], 1),
        "cols": np.stack([g["L0_xattn_" + n] for n in ("bk_s", "bq_s", "bq_c", "bk_c", "bg")], 1),
        "gw": g["L0_ffn_gate_w"].T, "reset8": reset(G0), "reset64": reset(E0), "rw": g["L1_ffn_router_w"].T,
        "wo": wo, "causal": causal, "half": half,
        "Kr_w": packed_w(g["L1_xattn_Wk"]), "Qr_w": packed_w(g["L1_xattn_Wq"]),
        "V_w": g["L1_xattn_Wv"].T, "O_w": g["L1_xattn_Wo"].T,
        "qb": packed_b(g["L1_xattn_bq"]), "kb": packed_b(g["L1_xattn_bk"]), "sel": sel,
    }
    arrays = {"pack_" + n: np.ascontiguousarray(np.concatenate([parts[k] for k, _ in p], axis=1))
              for n, p in PACKS.items()}
    arrays["rows"] = np.concatenate([g[k] for k in (
        "L0_attn_bp", "L0_xattn_bv_s", "L0_xattn_bv_c", "L0_ffn_gate_bias", "L1_xattn_bv", "L1_xattn_bo")])[None]
    arrays["bproj"] = np.ascontiguousarray(g["L1_ffn_b_proj"])
    arrays["mask_in"] = np.ascontiguousarray(g["mask_BxS2_bk0"]).reshape(1, C)
    arrays["pairs_w"] = np.concatenate([shared[None], routed], axis=0)
    arrays["pairs_down_w"] = np.concatenate([g["L0_ffn_sd_w"].T[None], down], axis=0)
    arrays["up_w"] = np.concatenate([g["L1_ffn_w_fc"], g["L1_ffn_b_fc"].reshape(E1, HC, 128).transpose(0, 2, 1)], axis=2)
    arrays["down_w"] = np.ascontiguousarray(
        g["L1_ffn_w_proj"].reshape(E1, HC, 128, D).transpose(0, 2, 1, 3).reshape(E1, 128, -1))
    arrays["heads_w"] = np.ascontiguousarray(qkv)

    nc = bacc.Bacc("TRN2", target_bir_lowering=False, num_devices=1)
    aps = {n: nc.dram_tensor(n, a.shape, mybir.dt.from_np(a.dtype), kind="ExternalInput").ap()
           for n, a in arrays.items()}
    out = nc.dram_tensor("out", (T, D), F32, kind="ExternalOutput").ap()
    build(nc, {n: aps["pack_" + n] for n in PACKS}, aps["rows"], aps["bproj"], aps["mask_in"],
          aps["pairs_w"], aps["pairs_down_w"], aps["heads_w"], aps["up_w"], aps["down_w"], out.rearrange("(t p) d -> p t d", p=128))
    r = run_bass_kernel_spmd(nc, [arrays], core_ids=[0])
    return r.results[0]["out"].reshape(NB, S, D)
```

```python
from contextlib import ExitStack

import numpy as np
import concourse.bass as bass
from concourse import mybir

F32 = mybir.dt.float32
F32R = mybir.dt.float32r
U8 = mybir.dt.uint8
ALU = mybir.AluOpType
ACT = mybir.ActivationFunctionType
AX = mybir.AxisListType.X

D = 128
NB = 2
S = 256
SC = 512
T = NB * S
C = NB * SC
TT = T // 128
HD = 8
NH = 16
E0, I0 = 64, 64
G0, TG0, K0 = 8, 4, 6
NP = E0 // 2
KQ = 64
HP = NH // 2
E1, H1, K1 = 8, 512, 2
HC = H1 // 128
NEG = -1.0e30

IDENT = [("ident", D)]
FRONT = [("xT", T), ("WkvT", 2 * D), ("WqT", D)]
LOCAL = [("conv", 4), ("blocks", D), ("heads", NH), ("x_tok", T), ("WpT", D)]
CROSS = [("ctxT", C), ("KsT_w", D), ("QsT_w", D), ("Vs_w", D), ("QcT_w", D), ("KcT_w", D), ("Vc_w", D),
         ("gate_w", 2 * D), ("cols", 5)]
ROUTE = [("gw", E0), ("reset8", TT * G0), ("reset64", TT * E0), ("rw", E1)]
HEADS = [("wo", NH * KQ), ("causal", 128), ("half", 2)]
MASKED = [("Kr_w", 4 * D), ("Qr_w", 4 * D), ("V_w", D), ("O_w", D), ("qb", 4), ("kb", 4), ("sel", 12)]
PACKS = {"ident": IDENT, "front": FRONT, "local": LOCAL, "cross": CROSS, "route": ROUTE, "heads": HEADS, "masked": MASKED}
ROWS = [("bp", D), ("bvs", D), ("bvc", D), ("gbias", E0), ("bv", D), ("bo", D)]
SEL_LO_Q, SEL_LO_K, SEL_HEAD, SEL_MASK, SEL_MAX, SEL_MAXES = 0, 1, 2, 6, 7, 11
HR = 3 * HD
MR = 96
KR = 112
VW = 2 * HD + 1


def width(pack):
    return sum(n for _, n in pack)


def build(nc, packs, rows, bproj, maskin, pairs_w, heads_w, up_w, down_w, out):
    with ExitStack() as ctx:
        early = ExitStack()
        early_last = ExitStack()
        hidden = ExitStack()
        late = ExitStack()
        late4 = ExitStack()
        late5 = ExitStack()

        def sb(name, shape, dt=F32, stack=ctx):
            return stack.enter_context(nc.sbuf_tensor(name, shape, dt))

        def sem(name):
            return ctx.enter_context(nc.semaphore(name))

        psum = ctx.enter_context(nc.psum_tensor("psum", [128, 8, 512], F32))
        pk = {n: sb("pk_" + n, [128, width(p)]) for n, p in PACKS.items() if n not in ("front", "local", "cross")}
        rowb = sb("rowb", [128, width(ROWS)])
        bpj = sb("bpj", [E1, D])
        maskb = sb("maskb", [128, C], U8)

        x_tok = sb("x_tok", [128, TT, D])
        res = sb("res", [128, TT, D])
        stats = sb("stats", [128, TT, 6])
        mv = sb("mv", [128, TT, 2])
        vare = sb("vare", [128, TT])
        rstd = sb("rstd", [128, TT])
        mhalf = sb("minus_half", [128, TT])
        one1 = sb("one", [128, 1])
        unused = sb("table_load_output", [128, 1])
        xT = sb("xT_f32", [128, T])
        xh = sb("xh", [128, T], F32R)
        xl = sb("xl", [128, T], F32R)
        identr = sb("identr", [128, 128], F32R)
        causr = sb("causr", [128, 128], F32R)
        KX = sb("k4_packed", [128, 4, C], F32R)
        Vx = sb("v4_packed", [128, C // 128, NH, VW], F32R)
        raw = sb("pair_raw", [128, 4, 512])
        whi = sb("pair_hi", [128, 4, 512], F32R)
        wlo = sb("pair_lo", [128, 4, 384], F32R)
        gwh = sb("gwh", [128, E0], F32R)
        gwl = sb("gwl", [128, E0], F32R)
        rwh = sb("rwh", [128, E1], F32R)
        rwl = sb("rwl", [128, E1], F32R)
        moeT = xT
        sg = sb("silu_gate", [128, 2, T])
        h1 = sb("h_unweighted", [128, 2, T])
        hh = sb("h_weighted", [128, 2, T])
        score = sb("score", [128, TT, E0])
        gsc = sb("group_score", [128, TT, G0])
        m8 = sb("top8", [128, TT, 8])
        cnt = sb("count_above", [128, TT])
        gt = sb("above", [128, TT * E0])
        eq = sb("equal", [128, TT * E0])
        cum = sb("equal_so_far", [128, TT * E0])
        selg = sb("selected", [128, TT * E0])
        wsum = sb("weight_sum", [128, TT])
        comb = sb("comb", [128, TT, E0])
        combhl = sb("comb_hi_lo", [128, TT, 128])
        combT = sb("comb_T", [128, T], F32R)
        for n in ("front", "local", "cross"):
            pk[n] = sb("pk_" + n, [128, width(PACKS[n])], stack=early)
        at = {}

        def place(n):
            o = 0
            for name, w in PACKS[n]:
                at[name] = pk[n][:, o:o + w]
                o += w

        for n in pk:
            place(n)
        o = 0
        for name, w in ROWS:
            at[name] = rowb[:, o:o + w]
            o += w
        ident = at["ident"]

        s_in = {n: sem("in_" + n) for n in [*PACKS, "rows", "bproj", "mask"]}
        s_y = sem("y_summed")
        s_res = sem("residual_biased")
        s_var = sem("variance")
        s_rstd = sem("rstd_powed")
        s_xn = sem("x_tile_normed")
        s_xT = sem("x_transposed")
        s_xh = sem("x_hi")
        s_xl = sem("x_lo")
        s_xf = sem("x_T_whole")
        s_out = sem("output_stored")
        s_dve = sem("dve_step")
        s_pool = sem("pool_step")
        s_mh = sem("minus_half_set")

        block = ctx.enter_context(nc.Block())
        count = {"dve": 0, "pool": 0}

        def dstep(dve, ins):
            count["dve"] += 1
            ins.then_inc(s_dve, 1)
            dve.wait_ge(s_dve, count["dve"])

        def pstep(pool, ins):
            count["pool"] += 1
            ins.then_inc(s_pool, 1)
            pool.wait_ge(s_pool, count["pool"])

        def tiles(ap, n=TT):
            return ap.rearrange("p (t d) -> p t d", t=n)

        Y = tiles(psum[:, 7, :])

        def norm_vector(dve, n, zz=Y):
            dve.wait_ge(s_y, n + 1)
            for i in range(TT):
                ins = dve.bn_stats(stats[:, i, :], zz[:, i, :])
            dstep(dve, ins)
            for i in range(TT):
                ins = dve.bn_aggr(mv[:, i, :], stats[:, i, :])
            dstep(dve, ins)
            dve.tensor_scalar(vare[:], mv[:, :, 1], 1e-5, None, ALU.add).then_inc(s_var, 1)
            dve.wait_ge(s_rstd, n + 1)
            for i in range(TT):
                dve.tensor_scalar(x_tok[:, i, :], zz[:, i, :], mv[:, i, 0:1], rstd[:, i:i + 1],
                                  ALU.subtract, ALU.mult).then_inc(s_xn, 1)

        def norm_pool(pool, n):
            pool.wait_ge(s_var, n + 1)
            if n == 0:
                pool.wait_ge(s_mh, 1)
            pool.tensor_tensor(rstd[:], vare[:], mhalf[:], ALU.pow).then_inc(s_rstd, 1)

        def norm_tensor(pe, n):
            for i in range(TT):
                pe.wait_ge(s_xn, n * TT + i + 1)
                ins = pe.transpose(psum[:, 6, i * 128:i * 128 + 128], x_tok[:, i, :], ident)
            ins.then_inc(s_xT, 1)

        def norm_scalar(act, n):
            act.wait_ge(s_xT, n + 1)
            act.activation(xT[:] if n == 0 else xh[:], psum[:, 6, :], ACT.Copy).then_inc(s_xh, 1)

        def load_table(act, func):
            act.activation(unused[:], one1[:], func)

        def norm_lo(dve, n):
            dve.wait_ge(s_xh, n + 1)
            dve.tensor_tensor(xl[:], psum[:, 6, :], xh[:].bitcast(F32), ALU.subtract).then_inc(s_xl, 1)

        def residual_first(pe, r):
            pe.matmul(psum[:, 7, :], ident, r.rearrange("p t d -> p (t d)"), start=True, stop=False,
                      skip_group_check=True)

        def three(pe, out_, wh, wl, ah, al, start=True, stop=True, skip=False):
            pe.matmul(out_, wh, ah, start=start, stop=False, skip_group_check=skip)
            pe.matmul(out_, wl, ah, start=False, stop=False, skip_group_check=skip)
            return pe.matmul(out_, wh, al, start=False, stop=stop, skip_group_check=skip)

        def three_early(pe, n, out_, wh, wl):
            pe.wait_ge(s_xh, n + 1)
            pe.matmul(out_, wh, xh[:], start=True, stop=False)
            pe.matmul(out_, wl, xh[:], start=False, stop=False)
            pe.wait_ge(s_xl, n)
            return pe.matmul(out_, wh, xl[:], start=False, stop=True)

        kmin = sb("kmin", [128, TT, D], stack=early)
        kphi = sb("kphi", [128, TT, D], stack=early)
        qmin = sb("qmin", [128, T], stack=early)
        qphi = sb("qphi", [128, T], stack=early)
        v_one = sb("v_one", [128, TT, D + 1], stack=early)
        kvm = sb("kvm", [128, NB, D + NH], stack=early)
        rden = sb("rden", [128, TT, NH], stack=early)
        att = sb("att", [128, TT, D], stack=early)
        loc = sb("loc", [128, NB, S], stack=early)
        aT = sb("aT", [128, T], stack=early)
        KsT = sb("KsT", [128, C], stack=early)
        QsT = sb("QsT", [128, C], stack=early)
        Vs = sb("Vs", [128, C // 128, D], stack=early)

        s_q = sem("q_projected")
        s_kv = sem("kv_projected")
        s_km = sem("kq_below_zero")
        s_ke = sem("kq_exp")
        s_phi = sem("kq_features")
        s_v = sem("v_copied")
        s_vone = sem("v_ones_set")
        s_st = sem("state_summed")
        s_stm = sem("state_masked")
        s_num = sem("numerators")
        s_att = sem("attention")
        s_attT = sem("attention_transposed")
        s_aT = sem("attention_plus_local")
        s_cps = sem("context_projected")
        s_cev = sem("context_copied")
        s_cv = sem("context_values")
        s_cvd = sem("context_values_biased")

        num = psum[:, 1:3, :].rearrange("p a (i n) -> p (a i) n", i=2)
        state = psum[:, 3, :].rearrange("p (b n) -> p b n", b=NB)

        def context_kq(pe, k):
            w, h = (at["KsT_w"], at["QsT_w"])[k // 2], k % 2
            if k == 0:
                pe.wait_ge(s_in["cross"], 16)
            if k >= 2:
                pe.wait_ge(s_cev, k - 1)
            pe.matmul(psum[:, 4 + k % 2, :], w, at["ctxT"][:, h * 512:h * 512 + 512],
                      start=True, stop=True).then_inc(s_cps, 1)

        def stage0_tensor(pe):
            pe.wait_ge(s_in["front"], 16)
            for a in range(2):
                for i in range(TT):
                    ins = pe.matmul(psum[:, 1 + a, i * 128:i * 128 + 128], at["xT"][:, i * 128:i * 128 + 128],
                                    at["WkvT"][:, a * D:a * D + D], start=True, stop=True)
                ins.then_inc(s_kv, 1)
            pe.matmul(psum[:, 0, :], at["WqT"], at["xT"], start=True, stop=True).then_inc(s_q, 1)
            pe.wait_ge(s_phi, 1)
            pe.wait_ge(s_v, 1)
            pe.wait_ge(s_vone, 1)
            for b in range(NB):
                for i in range(2):
                    ins = pe.matmul(state[:, b, 0:D + 1], kphi[:, 2 * b + i, :], v_one[:, 2 * b + i, :],
                                    start=i == 0, stop=i == 1)
            ins.then_inc(s_st, 1)
            context_kq(pe, 0)
            pe.wait_ge(s_stm, 1)
            pe.wait_ge(s_phi, 2)
            for i in range(TT):
                ins = pe.matmul(num[:, i, 0:D + NH], qphi[:, i * 128:i * 128 + 128], kvm[:, i // 2, :],
                                start=True, stop=True)
            ins.then_inc(s_num, 1)
            context_kq(pe, 1)
            pe.wait_ge(s_att, 1)
            for i in range(TT):
                ins = pe.transpose(psum[:, 0, i * 128:i * 128 + 128], att[:, i, :], ident)
            ins.then_inc(s_attT, 1)
            pe.wait_ge(s_res, 1)
            residual_first(pe, res[:])
            pe.wait_ge(s_aT, 1)
            for i in range(TT):
                ins = pe.matmul(Y[:, i, :], aT[:, i * 128:i * 128 + 128], at["WpT"], start=False, stop=True,
                                skip_group_check=True)
            ins.then_inc(s_y, 1)
            context_kq(pe, 2)
            context_kq(pe, 3)
            pe.wait_ge(s_in["masked"], 16)
            pe.wait_ge(s_ir, 1)
            pe.wait_ge(s_mk, 1)
            k4_tensor(pe, 0, 6)
            k4_tensor(pe, 1, 3)
            pe.wait_ge(s_cev, 4)
            for i in range(C // 128):
                ins = pe.matmul(psum[:, 4 + i // 4, i % 4 * 128:i % 4 * 128 + 128],
                                at["ctxT"][:, i * 128:i * 128 + 128], at["Vs_w"], start=True, stop=True)
            ins.then_inc(s_cv, 1)
            pe.wait_ge(s_k4a, 1)
            norm_tensor(pe, 0)

        def mask_rows(dve):
            sel = at["sel"]
            dve.wait_ge(s_in["mask"], 16)
            dve.wait_ge(s_in["masked"], 16)
            dstep(dve, dve.tensor_scalar(km[:], maskb[:], -NEG, NEG, ALU.mult, ALU.add))
            dve.tensor_scalar(kones[:], km[:], sel[:, SEL_MASK:SEL_MASK + 1], sel[:, SEL_MAXES:SEL_MAXES + 1],
                              ALU.mult, ALU.add).then_inc(s_mk, 1)

        def stage0_vector(dve):
            dve.wait_ge(s_kv, 1)
            dve.tensor_scalar(kmin[:], tiles(psum[:, 1, :]), 0.0, None, ALU.min).then_inc(s_km, 1)
            dve.wait_ge(s_ke, 1)
            dve.scalar_tensor_tensor(kphi[:], tiles(psum[:, 1, :]), 0.0, kmin[:], ALU.max, ALU.add).then_inc(s_phi, 1)
            dve.wait_ge(s_q, 1)
            dve.tensor_scalar(qmin[:], psum[:, 0, :], 0.0, None, ALU.min).then_inc(s_km, 1)
            dve.wait_ge(s_ke, 2)
            dve.scalar_tensor_tensor(qphi[:], psum[:, 0, :], 0.0, qmin[:], ALU.max, ALU.add).then_inc(s_phi, 1)
            xs = at["xT"].rearrange("p (b s) -> p b s", b=NB)
            cw = at["conv"]
            dve.wait_ge(s_in["local"], 16)
            dstep(dve, dve.tensor_scalar(loc[:], xs, cw[:, 1:2], cw[:, 3:4], ALU.mult, ALU.add))
            dstep(dve, dve.scalar_tensor_tensor(loc[:, :, 1:S], xs[:, :, 0:S - 1], cw[:, 0:1], loc[:, :, 1:S],
                                                ALU.mult, ALU.add))
            dstep(dve, dve.scalar_tensor_tensor(loc[:, :, 0:S - 1], xs[:, :, 1:S], cw[:, 2:3],
                                                loc[:, :, 0:S - 1], ALU.mult, ALU.add))
            dve.wait_ge(s_st, 1)
            dve.tensor_tensor(kvm[:, :, 0:D], state[:, :, 0:D],
                              at["blocks"].rearrange("p (o d) -> p o d", o=1).broadcast_to([128, NB, D]), ALU.mult)
            for b in range(NB):
                ins = dve.tensor_scalar(kvm[:, b, D:D + NH], at["heads"], state[:, b, D:D + 1], None, ALU.mult)
            ins.then_inc(s_stm, 1)
            mask_rows(dve)
            dve.wait_ge(s_num, 1)
            dstep(dve, dve.tensor_scalar(rden[:], num[:, :, D:D + NH], 1e-6, None, ALU.max))
            dstep(dve, dve.reciprocal(rden[:], rden[:]))
            dve.tensor_tensor(att[:].rearrange("p t (h d) -> p t h d", h=NH),
                              num[:, :, 0:D].rearrange("p t (h d) -> p t h d", h=NH),
                              rden[:].rearrange("p t (h o) -> p t h o", o=1).broadcast_to([128, TT, NH, HD]),
                              ALU.mult).then_inc(s_att, 1)
            dve.wait_ge(s_attT, 1)
            dve.tensor_tensor(aT[:], psum[:, 0, :], loc[:].rearrange("p b s -> p (b s)"), ALU.add).then_inc(s_aT, 1)
            norm_vector(dve, 0)
            dve.wait_ge(s_cv, 1)
            dve.wait_ge(s_in["rows"], 16)
            dve.tensor_tensor(Vs[:], psum[:, 4:6, :].rearrange("p a (t d) -> p (a t) d", t=4),
                              at["bvs"].rearrange("p (o d) -> p o d", o=1).broadcast_to([128, 8, D]),
                              ALU.add).then_inc(s_cvd, 1)

        def stage0_scalar(act):
            act.wait_ge(s_km, 1)
            act.activation(kmin[:], kmin[:], ACT.Exp).then_inc(s_ke, 1)
            act.wait_ge(s_kv, 2)
            act.activation(v_one[:, :, 0:D], tiles(psum[:, 2, :]), ACT.Copy).then_inc(s_v, 1)
            act.wait_ge(s_km, 2)
            act.activation(qmin[:], qmin[:], ACT.Exp).then_inc(s_ke, 1)
            for k in range(4):
                act.wait_ge(s_cps, k + 1)
                act.activation((KsT, QsT)[k // 2][:, k % 2 * 512:k % 2 * 512 + 512], psum[:, 4 + k % 2, :],
                               ACT.Identity, bias=at["cols"][:, k // 2:k // 2 + 1]).then_inc(s_cev, 1)
            act.wait_ge(s_in["masked"], 16)
            for n in range(2):
                k4_scalar(act, n, (6, 3)[n])
            norm_scalar(act, 0)

        def stage0_pool(pool):
            pool.memset(mhalf[:], -0.5).then_inc(s_mh, 1)
            pool.memset(v_one[:, :, D:D + 1], 1.0).then_inc(s_vone, 1)
            pool.memset(Vx[:, :, :, HD:HD + 1].bitcast(F32), 1.0)
            pstep(pool, pool.memset(one1[:], 1.0))
            pool.wait_ge(s_in["ident"], 16)
            pool.tensor_tensor(identr[:], ident, one1[:].broadcast_to([128, 128]), ALU.mult).then_inc(s_ir, 1)
            pool.wait_ge(s_in["local"], 16)
            pool.wait_ge(s_in["rows"], 16)
            pool.tensor_tensor(res[:], tiles(at["x_tok"]),
                               at["bp"].rearrange("p (o d) -> p o d", o=1).broadcast_to([128, TT, D]),
                               ALU.add).then_inc(s_res, 1)
            pool.wait_ge(s_in["masked"], 16)
            norm_pool(pool, 0)
            for n in range(2):
                k4_pool(pool, n, 0)
                k4_pool(pool, n, 1)

        P1 = sb("P1", [128, TT, SC], stack=early)
        vf = P1[:, 0:2, :].rearrange("p a (t h d) -> p (a t) h d", t=4, h=NH)
        kxf = sb("k4_biased", [128, 4, 512], stack=early)
        kxr = sb("k4_rounded", [128, 4, 512], F32R, stack=early)
        km = sb("mask4_added", [128, C], stack=early)
        kones = sb("mask4_rows", [128, C], F32R, stack=early)
        s_ir = sem("identity_rounded")
        s_mk = sem("mask4_rows_made")
        s_k4 = sem("k4_projected")
        s_k4a = sem("k4_copied")
        s_k4d = sem("k4_split")
        s_v4 = sem("v4_projected")
        s_v4a = sem("v4_copied")

        def k4_tensor(pe, n, bank):
            if n >= 6:
                pe.wait_ge(s_k4a, n - 1)
            c = slice(n % 2 * 512, n % 2 * 512 + 512)
            pe.matmul(psum[:, bank, :], at["Kr_w"][:, n // 2 * D:n // 2 * D + D], at["ctxT"][:, c],
                      start=True, stop=False)
            pe.matmul(psum[:, bank, :], identr[:], kones[:, c], start=False, stop=True).then_inc(s_k4, 1)

        def k4_scalar(act, n, bank):
            act.wait_ge(s_k4, n + 1)
            if n >= 4:
                act.wait_ge(s_k4d, n - 3)
            bias = at["kb"][:, n // 2:n // 2 + 1]
            act.activation(kxf[:, n % 4, :], psum[:, bank, :], ACT.Identity, bias=bias)
            act.activation(kxr[:, n % 4, :], psum[:, bank, :], ACT.Identity, bias=bias).then_inc(s_k4a, 1)

        def k4_pool(pool, n, part):
            if part == 0:
                pool.wait_ge(s_k4a, n + 1)
                pstep(pool, pool.tensor_tensor(
                    kxr[:, n % 4, :].bitcast(F32), kxr[:, n % 4, :].bitcast(F32),
                    at["sel"][:, SEL_LO_K:SEL_LO_K + 1].broadcast_to([128, 512]), ALU.mult))
            else:
                pool.tensor_tensor(KX[:, n // 2, n % 2 * 512:n % 2 * 512 + 512], kxr[:, n % 4, :].bitcast(F32),
                                   kxf[:, n % 4, :], ALU.add).then_inc(s_k4d, 1)

        def v4_tensor(pe):
            for i in range(C // 128):
                ins = pe.matmul(psum[:, (4, 6)[i // 4], i % 4 * 128:i % 4 * 128 + 128],
                                at["ctxT"][:, i * 128:i * 128 + 128], at["V_w"], start=True, stop=True)
                if i % 4 == 3:
                    ins.then_inc(s_v4, 1)

        def v4_scalar(act):
            for a in range(2):
                act.wait_ge(s_v4, a + 1)
                act.activation(vf[:, 4 * a:4 * a + 4, :, :],
                               psum[:, (4, 6)[a], :].rearrange("p (t h d) -> p t h d", t=4, h=NH),
                               ACT.Copy).then_inc(s_v4a, 1)

        def v4_pool(pool, part):
            if part == 0:
                pool.wait_ge(s_v4a, 2)
                pstep(pool, pool.tensor_tensor(
                    vf, vf, at["bv"].rearrange("p (o h d) -> p o h d", o=1, h=NH).broadcast_to([128, 8, NH, HD]), ALU.add))
            elif part == 1:
                pstep(pool, pool.tensor_tensor(
                    Vx[:, :, :, 0:HD], vf,
                    one1[:].rearrange("p (a b c) -> p a b c", a=1, b=1).broadcast_to([128, 8, NH, HD]), ALU.mult))
            else:
                pstep(pool, pool.tensor_tensor(Vx[:, :, :, HD + 1:VW], vf, Vx[:, :, :, 0:HD].bitcast(F32), ALU.subtract))

        QcT = sb("QcT", [128, T], stack=early)
        KcT = sb("KcT", [128, T], stack=early)
        Vc = sb("Vc", [128, TT, D], stack=early)
        P1T = sb("P1T", [128, NB, 4, S], stack=early)
        P2T = sb("P2T", [128, NB, 2, S], stack=early)
        mx1 = sb("mx1", [128, TT], stack=early)
        mx2 = sb("mx2", [128, 8], stack=early)
        sm1 = sb("sm1", [128, TT], stack=early)
        sm2 = sb("sm2", [128, 8], stack=early)
        c2s = sb("c2s", [128, T], stack=early)
        s2c = sb("s2c", [128, T], stack=early)
        gth = sb("gth", [128, T], stack=early)
        dif = loc[:].rearrange("p b s -> p (b s)")
        hbg = sb("hbg", [128, 1], stack=early)
        P2 = sb("P2", [128, 8, S], stack=early_last)
        SCALE1 = 1.0 / float(np.sqrt(np.float32(D)))

        s_p1 = sem("x_projected")
        s_p1c = sem("x_qk_copied")
        s_p1v = sem("x_v_biased")
        s_s1 = sem("scores_by_token")
        s_s2 = sem("scores_by_context")
        s_m1 = sem("max_by_token")
        s_m2 = sem("max_by_context")
        s_e1 = sem("exp_by_token")
        s_e2 = sem("exp_by_context")
        s_n1 = sem("probs_by_token")
        s_n2 = sem("probs_by_context")
        s_t1 = sem("probs_by_token_T")
        s_t2 = sem("probs_by_context_T")
        s_t1c = sem("probs_by_token_T_copied")
        s_t2c = sem("probs_by_context_T_paired")
        s_o1 = sem("tokens_attended")
        s_o2 = sem("context_attended")
        s_o1c = sem("tokens_attended_copied")
        s_o2c = sem("context_attended_copied")
        s_g = sem("gate_summed")
        s_gt = sem("gate_tanh")
        s_mix = sem("gated")
        s_hbg = sem("half_gate_bias")
        BK2 = [0, 1, 7, 2]

        def s2_at(k):
            return psum[:, BK2[k // 2], k % 2 * S:k % 2 * S + S]

        def stage1_tensor(pe):
            pe.wait_ge(s_xh, 1)
            pe.matmul(psum[:, 0, :], at["QcT_w"], xT[:], start=True, stop=True).then_inc(s_p1, 1)
            pe.matmul(psum[:, 1, :], at["KcT_w"], xT[:], start=True, stop=True).then_inc(s_p1, 1)
            pe.wait_ge(s_p1c, 1)
            pe.wait_ge(s_cev, 4)
            pe.wait_ge(s_cvd, 1)
            for i in range(TT):
                pe.matmul(psum[:, 3 + i, :], QcT[:, i * 128:i * 128 + 128], KsT[:, i // 2 * SC:i // 2 * SC + SC],
                          start=True, stop=True).then_inc(s_s1, 1)
            for i in range(TT):
                ins = pe.matmul(psum[:, 2, i * 128:i * 128 + 128], xT[:, i * 128:i * 128 + 128], at["Vc_w"],
                                start=True, stop=True)
            ins.then_inc(s_p1, 1)
            pe.wait_ge(s_p1c, 2)
            for k in range(8):
                if k == 6:
                    pe.wait_ge(s_p1v, 1)
                ins = pe.matmul(s2_at(k), QsT[:, k * 128:k * 128 + 128], KcT[:, k // 4 * S:k // 4 * S + S],
                                start=True, stop=True)
                if k % 2:
                    ins.then_inc(s_s2, 1)
            pe.wait_ge(s_e1, TT)
            for i in range(TT):
                pe.wait_ge(s_n1, i + 1)
                for j in range(4):
                    bk = 3 + 2 * (i // 2) + j // 2
                    o_ = j % 2 * S + i % 2 * 128
                    ins = pe.transpose(psum[:, bk, o_:o_ + 128], P1[:, i, j * 128:j * 128 + 128], ident)
                if i % 2:
                    ins.then_inc(s_t1, 1)
            pe.wait_ge(s_e2, 8)
            for k in range(8):
                pe.wait_ge(s_n2, k + 1)
                for j in range(2):
                    ins = pe.transpose(psum[:, BK2[k // 4 * 2 + j], k % 4 * 128:k % 4 * 128 + 128],
                                       P2[:, k, j * 128:j * 128 + 128], ident)
                if k % 4 == 3:
                    ins.then_inc(s_t2, 1)
            pe.wait_ge(s_t1c, 2)
            for b in range(NB):
                for j in range(4):
                    ins = pe.matmul(psum[:, 3, b * S:b * S + S], Vs[:, b * 4 + j, :], P1T[:, b, j, :],
                                    start=j == 0, stop=j == 3)
            ins.then_inc(s_o1, 1)
            for b in range(NB):
                pe.wait_ge(s_t2c, b + 1)
                for j in range(2):
                    ins = pe.matmul(psum[:, 4, b * S:b * S + S], Vc[:, b * 2 + j, :], P2T[:, b, j, :],
                                    start=j == 0, stop=j == 1)
            ins.then_inc(s_o2, 1)
            residual_first(pe, x_tok[:])
            pe.wait_ge(s_o1c, 1)
            pe.matmul(psum[:, 6, :], at["gate_w"][:, 0:D], c2s[:], start=True, stop=False)
            pe.wait_ge(s_o2c, 1)
            pe.matmul(psum[:, 6, :], at["gate_w"][:, D:2 * D], s2c[:], start=False, stop=True).then_inc(s_g, 1)
            k4_tensor(pe, 2, 0)
            k4_tensor(pe, 3, 1)
            pe.wait_ge(s_mix, 1)
            for i in range(TT):
                ins = pe.matmul(Y[:, i, :], gth[:, i * 128:i * 128 + 128], ident, start=False, stop=True,
                                skip_group_check=True)
            ins.then_inc(s_y, 1)
            norm_tensor(pe, 1)

        def stage1_scalar(act):
            for k, dst in enumerate((QcT, KcT)):
                act.wait_ge(s_p1, k + 1)
                act.activation(dst[:], psum[:, k, :], ACT.Identity,
                               bias=at["cols"][:, 2 + k:3 + k]).then_inc(s_p1c, 1)
            for i in range(TT):
                act.wait_ge(s_m1, i + 1)
                act.activation(P1[:, i, :], psum[:, 3 + i, :], ACT.Exp, bias=mx1[:, i:i + 1], scale=SCALE1,
                               accum_out=sm1[:, i:i + 1]).then_inc(s_e1, 1)
            for k in range(8):
                act.wait_ge(s_m2, k // 2 + 1)
                act.activation(P2[:, k, :], s2_at(k), ACT.Exp, bias=mx2[:, k:k + 1], scale=SCALE1,
                               accum_out=sm2[:, k:k + 1]).then_inc(s_e2, 1)
            for b in range(NB):
                act.wait_ge(s_t1, b + 1)
                act.activation(P1T[:, b, :, :].rearrange("p (a j) s -> p a (j s)", a=2),
                               psum[:, 3 + 2 * b:5 + 2 * b, :], ACT.Copy).then_inc(s_t1c, 1)
            stage2_early_scalar(act)
            act.wait_ge(s_o1, 1)
            act.activation(c2s[:], psum[:, 3, :], ACT.Copy).then_inc(s_o1c, 1)
            act.wait_ge(s_o2, 1)
            act.activation(s2c[:], psum[:, 4, :], ACT.Copy).then_inc(s_o2c, 1)
            act.wait_ge(s_g, 1)
            act.wait_ge(s_hbg, 1)
            act.activation(gth[:], psum[:, 6, :], ACT.Tanh, bias=hbg[:, 0:1], scale=0.5).then_inc(s_gt, 1)
            for n in range(2, 4):
                k4_scalar(act, n, n - 2)
            norm_scalar(act, 1)

        def stage1_vector(dve):
            dve.tensor_scalar(hbg[:], at["cols"][:, 4:5], 0.5, None, ALU.mult).then_inc(s_hbg, 1)
            for i in range(TT):
                dve.wait_ge(s_s1, i + 1)
                dstep(dve, dve.tensor_reduce(mx1[:, i:i + 1], psum[:, 3 + i, :], AX, ALU.max))
                dve.tensor_scalar(mx1[:, i:i + 1], mx1[:, i:i + 1], -SCALE1, None, ALU.mult).then_inc(s_m1, 1)
            dve.wait_ge(s_p1, 3)
            dve.tensor_tensor(Vc[:], tiles(psum[:, 2, :]),
                              at["bvc"].rearrange("p (o d) -> p o d", o=1).broadcast_to([128, TT, D]),
                              ALU.add).then_inc(s_p1v, 1)
            for k in range(4):
                dve.wait_ge(s_s2, k + 1)
                m = mx2[:, 2 * k:2 * k + 2]
                dstep(dve, dve.tensor_reduce(m, psum[:, BK2[k], :].rearrange("p (a s) -> p a s", a=2), AX, ALU.max))
                dve.tensor_scalar(m, m, -SCALE1, None, ALU.mult).then_inc(s_m2, 1)
            dve.wait_ge(s_e1, TT)
            dstep(dve, dve.reciprocal(sm1[:], sm1[:]))
            for i in range(TT):
                dve.tensor_scalar(P1[:, i, :], P1[:, i, :], sm1[:, i:i + 1], None, ALU.mult).then_inc(s_n1, 1)
            dve.wait_ge(s_e2, 8)
            dstep(dve, dve.reciprocal(sm2[:], sm2[:]))
            for k in range(8):
                dve.tensor_scalar(P2[:, k, :], P2[:, k, :], sm2[:, k:k + 1], 0.5, ALU.mult,
                                  ALU.mult).then_inc(s_n2, 1)
            for b in range(NB):
                dve.wait_ge(s_t2, b + 1)
                for j in range(2):
                    ins = dve.tensor_reduce(P2T[:, b, j, :], psum[:, BK2[2 * b + j], :].rearrange("p (s o) -> p s o", o=2),
                                            AX, ALU.add)
                ins.then_inc(s_t2c, 1)
            dve.wait_ge(s_o2c, 1)
            dve.wait_ge(s_o1c, 1)
            dstep(dve, dve.tensor_tensor(dif, c2s[:], s2c[:], ALU.subtract))
            dve.wait_ge(s_gt, 1)
            dstep(dve, dve.scalar_tensor_tensor(gth[:], gth[:], 1.0, dif, ALU.add, ALU.mult))
            dve.scalar_tensor_tensor(gth[:], gth[:], 0.5, s2c[:], ALU.mult, ALU.add).then_inc(s_mix, 1)
            norm_vector(dve, 1)
            norm_lo(dve, 1)

        def stage1_pool(pool):
            constants_pool(pool)
            norm_pool(pool, 1)

        early_last.close()
        hhi = sb("h_hi", [128, 2, T], F32R, stack=hidden)
        hlo = sb("h_lo", [128, 2, T], F32R, stack=hidden)
        hidden.close()
        early.close()

        Qrh = sb("q4_w_hi", [128, 4 * D], F32R, stack=late4)
        Qrl = sb("q4_w_lo", [128, 4 * D], F32R, stack=late4)
        xq = sg[:]
        yq = h1[:]
        rq = sb("q4_rounded", [128, 2, T], F32R, stack=late4)
        Qx = sb("q4_heads", [128, 4, 4, T], F32R, stack=late4)
        mxt = sb("max4", [128, TT, 128], stack=late4)
        VP = sb("v4_padded", [128, 2, C // 128, 4, 4 * VW], F32R, stack=late4)
        Pl = sb("exp4_lo", [128, 4, 512], F32R, stack=late4)
        OS = sb("attended4_T_raw", [128, T], stack=late4)
        rs4 = sb("sums4_inverse", [128, TT, 4], stack=late4)
        lo4 = sb("attended4_lo", [128, TT, 4, HD], stack=late4)
        att4 = sb("attended4", [128, TT, D], stack=late4)
        aT4 = sb("attended4_T", [128, T], stack=late4)

        s_gu = [sem(f"pair_loaded_{i}") for i in range(4)]
        s_hhi = sem("pair_h_hi")
        s_hlo = sem("pair_h_lo")
        s_const = sem("rounded_constants")
        s_whi = sem("pair_hi_made")
        s_wlo = sem("pair_lo_made")
        s_lg = sem("logits")
        s_th = sem("logits_tanh")
        s_pg = sem("pair_gate")
        s_pu = sem("pair_up")
        s_pc = sem("pair_weights_spread")
        s_silu = sem("pair_silu")
        s_h1 = sem("pair_h_unweighted")
        s_h = sem("pair_h")
        s_d = sem("pair_down")
        s_c2 = sem("combine_weights")
        s_mT = sem("experts_sum_T_copied")
        s_comb = sem("combine_weights_split")
        s_cT = sem("combine_weights_T")
        s_combT = sem("combine_weights_T_copied")
        LOOPS = (NP - 4) // 4

        def bc(ap, n):
            return ap.rearrange("p (a o) -> p a o", o=1).broadcast_to([128, ap.shape[1], n])

        def top_k(dve, v, n, k, reset):
            f = selg[:, 0:TT * n].rearrange("p (t e) -> p t e", t=TT)
            g_, e_, c_ = (a[:, 0:TT * n].rearrange("p (t e) -> p t e", t=TT) for a in (gt, eq, cum))
            for i in range(TT):
                ins = dve.max(m8[:, i, :], v[:, i, :])
            dstep(dve, ins)
            thr = m8[:, :, k - 1:k].broadcast_to([128, TT, n])
            dve.tensor_tensor(g_, v, thr, ALU.is_gt)
            dstep(dve, dve.tensor_tensor(e_, v, thr, ALU.is_equal))
            dve.tensor_tensor_scan(cum[:, 0:TT * n], reset, eq[:, 0:TT * n], 0.0, ALU.mult, ALU.add)
            dstep(dve, dve.tensor_reduce(cnt[:], g_, AX, ALU.add))
            dstep(dve, dve.tensor_scalar(cnt[:], cnt[:], -1.0, float(k), ALU.mult, ALU.add))
            dstep(dve, dve.tensor_tensor(c_, c_, bc(cnt[:], n), ALU.is_le))
            dstep(dve, dve.tensor_tensor(e_, e_, c_, ALU.mult))
            dstep(dve, dve.tensor_tensor(f, e_, g_, ALU.add))
            return f

        def normalised(dve, v, chosen, n, eps, done):
            c_ = comb[:].rearrange("p t e -> p (t e)")[:, 0:TT * n].rearrange("p (t e) -> p t e", t=TT)
            dstep(dve, dve.tensor_tensor(c_, v, chosen, ALU.mult))
            dstep(dve, dve.tensor_reduce(wsum[:], c_, AX, ALU.add))
            if eps:
                dstep(dve, dve.tensor_scalar(wsum[:], wsum[:], eps, None, ALU.add))
            dstep(dve, dve.reciprocal(wsum[:], wsum[:]))
            dve.tensor_tensor(c_, c_, bc(wsum[:], n), ALU.mult).then_inc(done, 1)

        def load_pair(sp, p, slot):
            sp.dma_start(raw[:, slot, :], pairs_w[p + 1, :, :]).then_inc(s_gu[slot], 16)

        def stage2_sync(sp):
            for p in range(-1, 3):
                load_pair(sp, p, p % 4)
            with sp.Fori(0, LOOPS) as it:
                for j in range(4):
                    sp.wait_ge(s_wlo, it * 4 + j + 1)
                    load_pair(sp, it * 4 + j + 3, (j + 3) % 4)
            sp.wait_ge(s_wlo, NP - 3)
            load_pair(sp, NP - 1, (NP - 1) % 4)

        def constants_pool(pool):
            pool.wait_ge(s_in["route"], 16)
            pstep(pool, pool.tensor_copy(gwh[:], at["gw"]))
            pool.tensor_tensor(gwl[:], at["gw"], gwh[:].bitcast(F32), ALU.subtract)
            pstep(pool, pool.tensor_copy(rwh[:], at["rw"]))
            pool.tensor_tensor(rwl[:], at["rw"], rwh[:].bitcast(F32), ALU.subtract)
            pool.wait_ge(s_in["heads"], 16)
            pool.tensor_copy(causr[:], at["causal"]).then_inc(s_const, 1)

        def pair_lo(pool, p, slot):
            pool.wait_ge(s_whi, p + 2)
            pool.tensor_tensor(wlo[:, slot, :], raw[:, slot, 0:384], whi[:, slot, 0:384].bitcast(F32),
                               ALU.subtract).then_inc(s_wlo, 1)

        def stage2_pool(pool):
            for p in range(-1, 2):
                if p < 1:
                    k4_pool(pool, p + 3, 0)
                    k4_pool(pool, p + 3, 1)
                pair_lo(pool, p, p % 4)
            pair_lo(pool, 2, 2)
            for part in range(3):
                v4_pool(pool, part)
            k4_pool(pool, 4, 0)
            k4_pool(pool, 4, 1)
            for p in range(3, 11):
                pair_lo(pool, p, p % 4)
                if p < 9:
                    k4_pool(pool, 5 + (p - 3) // 2, (p - 3) % 2)
            with pool.Fori(0, LOOPS - 3) as it:
                for j in range(4):
                    pair_lo(pool, it * 4 + j + 11, (j + 3) % 4)
            for p in range(4 * LOOPS - 1, NP):
                pair_lo(pool, p, p % 4)
            norm_pool(pool, 2)

        def pair_h_hi(act, p, par):
            act.wait_ge(s_h, p + 2)
            act.activation(hhi[:, par, :], hh[:, par, :], ACT.Copy).then_inc(s_hhi, 1)

        def pair_hi(act, slot, turn):
            act.wait_ge(s_gu[slot], turn * 16 + 16)
            act.activation(whi[:, slot, :], raw[:, slot, :], ACT.Copy).then_inc(s_whi, 1)

        def pair_silu(act, p, par):
            act.wait_ge(s_pg, p + 2)
            act.wait_ge(s_h1, p)
            act.activation(sg[:, par, :], psum[:, par, :], ACT.Silu).then_inc(s_silu, 1)

        def stage2_early_scalar(act):
            for p in range(-1, 2):
                pair_hi(act, p % 4, 0)

        def stage2_scalar(act):
            act.wait_ge(s_lg, 1)
            act.activation(score[:], psum[:, 5, 0:TT * E0].rearrange("p (t e) -> p t e", t=TT), ACT.Tanh,
                           scale=0.5).then_inc(s_th, 1)
            act.wait_ge(s_pg, 1)
            act.activation(sg[:, 1, :], psum[:, 1, :], ACT.Silu).then_inc(s_silu, 1)
            pair_hi(act, 2, 0)
            pair_silu(act, 0, 0)
            v4_scalar(act)
            for n in range(4, 8):
                k4_scalar(act, n, (4, 6)[n % 2])
            act.wait_ge(s_cT, 1)
            act.activation(combT[:], psum[:, 6, :], ACT.Copy).then_inc(s_combT, 1)
            pair_h_hi(act, -1, 1)
            with act.Fori(0, LOOPS) as it:
                for j in range(4):
                    pair_silu(act, it * 4 + j + 1, (j + 1) % 2)
                    pair_h_hi(act, it * 4 + j, j % 2)
                    act.wait_ge(s_d, it * 4 + j + 1)
                    pair_hi(act, (j + 3) % 4, it + 1)
            for p in range(NP - 3, NP):
                pair_silu(act, p, p % 2)
                pair_h_hi(act, p - 1, (p - 1) % 2)
                if p + 2 < NP:
                    act.wait_ge(s_d, p)
                    pair_hi(act, (p + 2) % 4, (p + 3) // 4)
            pair_h_hi(act, NP - 1, (NP - 1) % 2)
            act.wait_ge(s_d, NP + 1)
            act.activation(moeT[:], psum[:, 6, :], ACT.Copy).then_inc(s_mT, 1)
            norm_scalar(act, 2)
            act.wait_ge(s_xl, 2)
            act.activation(xT[:], psum[:, 6, :], ACT.Copy).then_inc(s_xf, 1)

        def pair_h1(dve, p, par):
            dve.wait_ge(s_silu, p + 2)
            dve.wait_ge(s_pu, p + 2)
            dve.tensor_tensor(h1[:, par, :], psum[:, 2 + par, :], sg[:, par, :], ALU.mult).then_inc(s_h1, 1)

        def pair_h(dve, p, par):
            dve.wait_ge(s_pc, p + 1)
            dve.wait_ge(s_h1, p + 2)
            if not isinstance(p, int) or p > 0:
                dve.wait_ge(s_hhi, p)
            dve.tensor_tensor(hh[:, par, :], psum[:, 4 + par, :], h1[:, par, :], ALU.mult).then_inc(s_h, 1)

        def pair_h_lo(dve, p, par):
            dve.wait_ge(s_hhi, p + 2)
            dve.tensor_tensor(hlo[:, par, :], hh[:, par, :], hhi[:, par, :].bitcast(F32), ALU.subtract).then_inc(s_hlo, 1)

        def stage2_vector(dve):
            dve.wait_ge(s_th, 1)
            dve.wait_ge(s_in["route"], 16)
            dstep(dve, dve.tensor_scalar(score[:], score[:], 0.5, 0.5, ALU.mult, ALU.add))
            dstep(dve, dve.tensor_tensor(score[:], score[:],
                                         at["gbias"].rearrange("p (o e) -> p o e", o=1).broadcast_to([128, TT, E0]),
                                         ALU.add))
            by_group = score[:].rearrange("p t (g e) -> p (t g) e", g=G0)
            dstep(dve, dve.tensor_reduce(gsc[:].rearrange("p t g -> p (t g)"), by_group, AX, ALU.max))
            top_k(dve, gsc[:], G0, TG0, at["reset8"])
            dstep(dve, dve.tensor_tensor(by_group, by_group, bc(selg[:, 0:TT * G0], E0 // G0), ALU.mult))
            chosen = top_k(dve, score[:], E0, K0, at["reset64"])
            normalised(dve, score[:], chosen, E0, 1e-8, s_c2)
            dve.wait_ge(s_c2, 1)
            dstep(dve, dve.tensor_copy(combhl[:, :, 0:E0].bitcast(F32R), comb[:]))
            dve.tensor_tensor(combhl[:, :, E0:2 * E0], comb[:], combhl[:, :, 0:E0], ALU.subtract).then_inc(s_comb, 1)
            pair_h1(dve, -1, 1)
            dve.wait_ge(s_h1, 1)
            dve.tensor_copy(hh[:, 1, :], h1[:, 1, :]).then_inc(s_h, 1)
            pair_h1(dve, 0, 0)
            pair_h_lo(dve, -1, 1)
            pair_h(dve, 0, 0)
            with dve.Fori(0, LOOPS) as it:
                for j in range(4):
                    pair_h1(dve, it * 4 + j + 1, (j + 1) % 2)
                    pair_h_lo(dve, it * 4 + j, j % 2)
                    pair_h(dve, it * 4 + j + 1, (j + 1) % 2)
            for p in range(NP - 3, NP):
                pair_h1(dve, p, p % 2)
                pair_h_lo(dve, p - 1, (p - 1) % 2)
                pair_h(dve, p, p % 2)
            pair_h_lo(dve, NP - 1, (NP - 1) % 2)
            norm_vector(dve, 2)
            norm_lo(dve, 2)

        def pair_gate_up(pe, p, slot, par):
            pe.wait_ge(s_wlo, p + 2)
            if not isinstance(p, int) or p > 0:
                pe.wait_ge(s_h1, p)
            three(pe, psum[:, par, :], whi[:, slot, 0:128], wlo[:, slot, 0:128], xh[:], xl[:]).then_inc(s_pg, 1)
            three(pe, psum[:, 2 + par, :], whi[:, slot, 128:256], wlo[:, slot, 128:256], xh[:], xl[:]).then_inc(s_pu, 1)

        def pair_spread(pe, p, slot, par):
            if not isinstance(p, int) or p > 1:
                pe.wait_ge(s_h, p)
            pe.matmul(psum[:, 4 + par, :], whi[:, slot, 384:512], combT[:], start=True, stop=True).then_inc(s_pc, 1)

        def pair_down(pe, p, slot, par, first=False, last=False):
            pe.wait_ge(s_hlo, p + 2)
            three(pe, psum[:, 6, :], whi[:, slot, 256:384], wlo[:, slot, 256:384], hhi[:, par, :], hlo[:, par, :],
                  start=first, stop=last, skip=True).then_inc(s_d, 1)

        def stage2_tensor(pe):
            pe.wait_ge(s_xh, 2)
            pe.wait_ge(s_const, 1)
            for i in range(TT):
                t, o_ = slice(i * 128, i * 128 + 128), psum[:, 5, i * E0:i * E0 + E0]
                pe.matmul(o_, xh[:, t], gwh[:], start=True, stop=False)
                pe.matmul(o_, xh[:, t], gwl[:], start=False, stop=False)
                pe.wait_ge(s_xl, 1)
                ins = pe.matmul(o_, xl[:, t], gwh[:], start=False, stop=True)
            ins.then_inc(s_lg, 1)
            pair_gate_up(pe, -1, 3, 1)
            pair_gate_up(pe, 0, 0, 0)
            v4_tensor(pe)
            pe.wait_ge(s_v4a, 1)
            k4_tensor(pe, 4, 4)
            pe.wait_ge(s_v4a, 2)
            k4_tensor(pe, 5, 6)
            k4_tensor(pe, 6, 4)
            k4_tensor(pe, 7, 6)
            residual_first(pe, x_tok[:])
            pe.wait_ge(s_k4a, 8)
            pe.wait_ge(s_comb, 1)
            for i in range(TT):
                ins = pe.transpose(psum[:, 6, i * 128:i * 128 + 128], combhl[:, i, :], ident)
            ins.then_inc(s_cT, 1)
            pair_gate_up(pe, 1, 1, 1)
            pe.wait_ge(s_combT, 1)
            pair_spread(pe, 0, 0, 0)
            pair_down(pe, -1, 3, 1, first=True)
            pair_spread(pe, 1, 1, 1)
            with pe.Fori(0, LOOPS) as it:
                for j in range(4):
                    pair_gate_up(pe, it * 4 + j + 2, (j + 2) % 4, j % 2)
                    pair_down(pe, it * 4 + j, j, j % 2)
                    pair_spread(pe, it * 4 + j + 2, (j + 2) % 4, j % 2)
            for p in range(NP - 4, NP):
                if p + 2 < NP:
                    pair_gate_up(pe, p + 2, (p + 2) % 4, p % 2)
                pair_down(pe, p, p % 4, p % 2, last=p == NP - 1)
                if p + 2 < NP:
                    pair_spread(pe, p + 2, (p + 2) % 4, p % 2)
            pe.wait_ge(s_mT, 1)
            for i in range(TT):
                ins = pe.matmul(Y[:, i, :], moeT[:, i * 128:i * 128 + 128], ident, start=False, stop=True,
                                skip_group_check=True)
            ins.then_inc(s_y, 1)
            norm_tensor(pe, 2)

        wsr = sb("head_w_raw", [128, 2, 384], stack=late)
        wqk = sb("head_qk_w_hi_lo", [128, 2, 256], F32R, stack=late)
        QH = sb("q_hi", [128, 2, T], F32R, stack=late)
        QL = sb("q_lo", [128, 2, T], F32R, stack=late)
        KH = sb("k_hi", [128, 2, NB, 2, S], F32R, stack=late)
        KL = sb("k_lo", [128, 2, NB, 2, S], F32R, stack=late)
        Vv = hh[:].rearrange("p a (t d) -> p a t d", t=TT)
        PL = sg[:].rearrange("p a (b m) -> p (a b) m", b=2)
        PTs = raw[:, 0:3, :]
        PE_ = sb("probs_early", [128, 4, 128], stack=late)
        nmx = sb("minus_max", [128, 8], stack=late)
        sums = sb("prob_sums", [128, 2, 8], stack=late)
        rsum = sb("prob_sums_inverse", [128, 8], stack=late)
        On = sb("attended_normed", [128, 8, KQ], stack=late)
        OTs = sb("attended_T", [128, T], stack=late)
        SCALE3 = 1.0 / float(np.sqrt(KQ))

        s_wsr = [sem(f"head_w_loaded_{i}") for i in range(2)]
        s_wsh = sem("head_w_hi_made")
        s_ws = sem("head_w_made")
        s_jq = sem("head_q")
        s_jk = sem("head_k")
        s_jv = sem("head_v")
        s_qh = sem("head_q_hi")
        s_kh = sem("head_k_hi")
        s_ql = sem("head_q_lo")
        s_kl = sem("head_k_lo")
        s_vv = sem("head_v_copied")
        s_S = sem("head_scores")
        s_mx = sem("head_max")
        s_nm = sem("head_minus_max")
        s_ex = sem("head_exp")
        s_pt = sem("head_probs_T")
        s_pta = sem("head_probs_T_copied_act")
        s_ptd = sem("head_probs_T_copied_dve")
        s_pv = sem("head_attended")
        s_rs = sem("head_sums_inverted")
        s_on = sem("head_normed")
        s_otp = sem("head_attended_T")
        s_ot = sem("head_attended_T_copied")
        heads_o = at["wo"].rearrange("p (n w) -> p n w", n=HP)
        TILE_OF = (1, 3, 0, 2)
        sc_late = lambda b: psum[:, 3 + b, :].rearrange("p (h m) -> p h m", h=2)
        sc_early = psum[:, 5, :].rearrange("p (b h m) -> p b h m", b=NB, h=2)

        def stage3_load(sp, n, slot):
            sp.dma_start(wsr[:, slot, :], heads_w[n, :, :]).then_inc(s_wsr[slot], 16)

        def stage3_sync(sp):
            sp.wait_ge(s_xn, 2 * TT)
            sp.wait_ge(s_k4d, 8)
            stage3_load(sp, 0, 0)
            stage3_load(sp, 1, 1)
            with sp.Fori(0, HP // 2 - 1) as it:
                for j in range(2):
                    sp.wait_ge(s_jv, it * 2 + j + 1)
                    stage3_load(sp, it * 2 + j + 2, j)

        def head_split(pool, n, par, turn):
            pool.wait_ge(s_wsr[par], turn * 16 + 16)
            pool.tensor_tensor(wqk[:, 0, :], wsr[:, par, 0:256], one1[:].broadcast_to([128, 256]),
                               ALU.mult).then_inc(s_wsh, 1)
            pool.wait_ge(s_wsh, n + 1)
            pool.tensor_tensor(wqk[:, 1, :], wsr[:, par, 0:256], wqk[:, 0, :].bitcast(F32), ALU.subtract).then_inc(s_ws, 1)

        def stage3_pool(pool):
            head_split(pool, 0, 0, 0)
            pool.wait_ge(s_jk, 1)
            head_split(pool, 1, 1, 0)
            with pool.Fori(0, HP // 2 - 1) as it:
                for j in range(2):
                    n = it * 2 + j + 2
                    pool.wait_ge(s_jk, n)
                    head_split(pool, n, j, it + 1)
            stage4_early_pool(pool)
            norm_pool(pool, 3)

        def head_project_qk(pe, n):
            pe.wait_ge(s_ws, n + 1)
            three(pe, psum[:, 0, :], wqk[:, 0, 0:128], wqk[:, 1, 0:128], xh[:], xl[:]).then_inc(s_jq, 1)
            three(pe, psum[:, 1, :], wqk[:, 0, 128:256], wqk[:, 1, 128:256], xh[:], xl[:]).then_inc(s_jk, 1)

        def head_project_v(pe, par):
            for i in range(TT):
                t = slice(i * 128, i * 128 + 128)
                ins = pe.matmul(psum[:, 2, t], xT[:, t], wsr[:, par, 256:384], start=True, stop=True)
            ins.then_inc(s_jv, 1)

        def head_scores(pe, n, par):
            pe.wait_ge(s_ql, n + 1)
            pe.wait_ge(s_kl, n + 1)
            for b in range(NB):
                q = slice(b * S + 128, b * S + 256)
                o_ = sc_late(b)
                three(pe, o_, QH[:, par, q], QL[:, par, q], KH[:, par, b, :, :], KL[:, par, b, :, :], stop=False)
                pe.matmul(o_[:, :, 128:256], identr[:],
                          causr[:].rearrange("p (o m) -> p o m", o=1).broadcast_to([128, 2, 128]),
                          start=False, stop=True)
                q = slice(b * S, b * S + 128)
                o_ = sc_early[:, b, :, :]
                three(pe, o_, QH[:, par, q], QL[:, par, q], KH[:, par, b, :, 0:128],
                      KL[:, par, b, :, 0:128], stop=False)
                ins = pe.matmul(o_, identr[:],
                                causr[:].rearrange("p (o m) -> p o m", o=1).broadcast_to([128, 2, 128]),
                                start=False, stop=True)
            ins.then_inc(s_S, 1)

        def head_turn(pe, n):
            pe.wait_ge(s_ex, n + 1)
            for b in range(NB):
                for h in range(2):
                    k = 2 * b + h
                    pe.transpose(psum[:, b, h * S:h * S + 128], PE_[:, k, :], ident)
                    pe.transpose(psum[:, b, h * S + 128:h * S + 256], PL[:, k, 0:128], ident)
            for k in range(4):
                ins = pe.transpose(psum[:, 2, k * 128:k * 128 + 128], PL[:, k, 128:256], ident)
            ins.then_inc(s_pt, 1)

        def head_attend(pe, n, par):
            pe.wait_ge(s_pta, n + 1)
            pe.wait_ge(s_ptd, n + 1)
            for late in (1, 0):
                for b in range(NB):
                    for h in range(2):
                        k = 2 * b + h
                        o_ = psum[:, 6, (k + 4 * (1 - late)) * KQ:(k + 4 * (1 - late)) * KQ + KQ]
                        c = h * S + 128 * late
                        v = slice(h * KQ, h * KQ + KQ)
                        ins = pe.matmul(o_, PTs[:, b, c:c + 128], Vv[:, par, 2 * b, v], start=True, stop=not late)
                        if late:
                            ins = pe.matmul(o_, PTs[:, 2, k * 128:k * 128 + 128], Vv[:, par, 2 * b + 1, v],
                                            start=False, stop=True)
            ins.then_inc(s_pv, 1)

        def head_turn_output(pe, n):
            pe.wait_ge(s_on, n + 1)
            for k in range(4):
                c = TILE_OF[k] * 128
                ins = pe.transpose(psum[:, 6, c:c + 128], On[:, 2 * k:2 * k + 2, :].rearrange("p a d -> p (a d)"), ident)
            ins.then_inc(s_otp, 1)

        def head_output(pe, n, last=False):
            pe.wait_ge(s_ot, n + 1)
            for i in range(TT):
                ins = pe.matmul(Y[:, i, :], OTs[:, i * 128:i * 128 + 128], heads_o[:, n, :],
                                start=False, stop=last, skip_group_check=True)
            if last:
                ins.then_inc(s_y, 1)

        def stage3_tensor(pe):
            pe.wait_ge(s_ws, 1)
            three_early(pe, 2, psum[:, 0, :], wqk[:, 0, 0:128], wqk[:, 1, 0:128]).then_inc(s_jq, 1)
            three(pe, psum[:, 1, :], wqk[:, 0, 128:256], wqk[:, 1, 128:256], xh[:], xl[:]).then_inc(s_jk, 1)
            pe.wait_ge(s_xf, 1)
            head_project_v(pe, 0)
            residual_first(pe, x_tok[:])
            head_scores(pe, 0, 0)
            head_project_qk(pe, 1)
            pe.wait_ge(s_vv, 1)
            head_project_v(pe, 1)
            pe.wait_ge(s_ql, 2)
            pe.wait_ge(s_kl, 2)
            head_project_qk(pe, 2)

            def step(n, par, first=False, scores=True, qk=True, v=True):
                if v:
                    pe.wait_ge(s_ql, n + 3)
                    pe.wait_ge(s_kl, n + 3)
                if scores:
                    pe.wait_ge(s_vv, n + 2)
                head_turn(pe, n)
                if scores:
                    head_scores(pe, n + 1, 1 - par)
                if qk:
                    pe.wait_ge(s_pta, n + 1)
                    pe.wait_ge(s_ptd, n + 1)
                    head_project_qk(pe, n + 3)
                head_attend(pe, n, par)
                if v:
                    head_project_v(pe, par)
                if not first:
                    head_output(pe, n - 1)
                head_turn_output(pe, n)

            step(0, 0, first=True)
            with pe.Fori(0, (HP - 4) // 2) as it:
                for j in range(2):
                    step(it * 2 + j + 1, 1 - j)
            step(HP - 3, 1, qk=False)
            step(HP - 2, 0, qk=False, v=False)
            step(HP - 1, 1, scores=False, qk=False, v=False)
            head_output(pe, HP - 1, last=True)
            norm_tensor(pe, 3)

        def head_hi(act, n, par):
            act.wait_ge(s_jq, n + 1)
            act.activation(QH[:, par, :], psum[:, 0, :], ACT.Copy).then_inc(s_qh, 1)
            act.wait_ge(s_jk, n + 1)
            for h in range(2):
                ins = act.activation(KH[:, par, :, h, :], psum[:, 1, :].rearrange("p (b m) -> p b m", b=NB), ACT.Copy,
                                     scale=at["half"][:, h:h + 1])
            ins.then_inc(s_kh, 1)

        def head_exps(act, n, par):
            act.wait_ge(s_nm, n + 1)
            for k in range(4):
                act.activation(PL[:, k, :], sc_late(k // 2)[:, k % 2, :], ACT.Exp, bias=nmx[:, k:k + 1],
                               scale=SCALE3, accum_out=sums[:, par, k:k + 1])
            for k in range(4):
                ins = act.activation(PE_[:, k, :], sc_early[:, k // 2, k % 2, :], ACT.Exp,
                                     bias=nmx[:, 4 + k:5 + k], scale=SCALE3, accum_out=sums[:, par, 4 + k:5 + k])
            ins.then_inc(s_ex, 1)

        def stage3_scalar(act):
            load_table(act, ACT.Exp)
            head_hi(act, 0, 0)
            head_hi(act, 1, 1)
            head_exps(act, 0, 0)
            head_hi(act, 2, 0)

            def step(n, par, scores=True, qk=True):
                act.wait_ge(s_pt, n + 1)
                act.activation(PTs[:, 0, :], psum[:, 0, :], ACT.Copy).then_inc(s_pta, 1)
                if qk:
                    head_hi(act, n + 3, 1 - par)
                if scores:
                    head_exps(act, n + 1, 1 - par)
                act.wait_ge(s_otp, n + 1)
                act.activation(OTs[:], psum[:, 6, :], ACT.Copy).then_inc(s_ot, 1)

            step(0, 0)
            with act.Fori(0, (HP - 4) // 2) as it:
                for j in range(2):
                    step(it * 2 + j + 1, 1 - j)
            step(HP - 3, 1, qk=False)
            step(HP - 2, 0, qk=False)
            step(HP - 1, 1, scores=False, qk=False)
            norm_scalar(act, 3)

        def head_lo(dve, n, par):
            dve.wait_ge(s_qh, n + 1)
            dve.tensor_tensor(QL[:, par, :], psum[:, 0, :], QH[:, par, :].bitcast(F32), ALU.subtract).then_inc(s_ql, 1)
            dve.wait_ge(s_kh, n + 1)
            for h in range(2):
                ins = dve.scalar_tensor_tensor(KL[:, par, :, h, :], psum[:, 1, :].rearrange("p (b m) -> p b m", b=NB),
                                               at["half"][:, h:h + 1], KH[:, par, :, h, :].bitcast(F32),
                                               ALU.mult, ALU.subtract)
            ins.then_inc(s_kl, 1)

        def head_v(dve, n, par):
            dve.wait_ge(s_jv, n + 1)
            dve.tensor_copy(Vv[:, par, :, :], tiles(psum[:, 2, :])).then_inc(s_vv, 1)

        def head_max(dve, n):
            dve.wait_ge(s_S, n + 1)
            dve.tensor_reduce(nmx[:, 0:4], psum[:, 3:5, :].rearrange("p a (h m) -> p (a h) m", h=2), AX, ALU.max)
            dve.tensor_reduce(nmx[:, 4:8], sc_early.rearrange("p b h m -> p (b h) m"), AX, ALU.max).then_inc(s_mx, 1)
            dve.wait_ge(s_mx, n + 1)
            dve.tensor_scalar(nmx[:], nmx[:], -SCALE3, None, ALU.mult).then_inc(s_nm, 1)

        def stage3_vector(dve):
            head_lo(dve, 0, 0)
            head_v(dve, 0, 0)
            head_max(dve, 0)
            head_lo(dve, 1, 1)
            head_v(dve, 1, 1)
            head_lo(dve, 2, 0)

            def step(n, par, scores=True, qk=True, v=True):
                dve.wait_ge(s_pt, n + 1)
                dve.tensor_copy(PTs[:, 1:3, :], psum[:, 1:3, :]).then_inc(s_ptd, 1)
                dve.reciprocal(rsum[:], sums[:, par, :]).then_inc(s_rs, 1)
                if scores:
                    head_max(dve, n + 1)
                if qk:
                    head_lo(dve, n + 3, 1 - par)
                dve.wait_ge(s_pv, n + 1)
                dve.wait_ge(s_rs, n + 1)
                dve.tensor_tensor(On[:], psum[:, 6, :].rearrange("p (k d) -> p k d", d=KQ), bc(rsum[:], KQ),
                                  ALU.mult).then_inc(s_on, 1)
                if v:
                    head_v(dve, n + 2, par)

            step(0, 0)
            with dve.Fori(0, (HP - 4) // 2) as it:
                for j in range(2):
                    step(it * 2 + j + 1, 1 - j)
            step(HP - 3, 1, qk=False)
            step(HP - 2, 0, qk=False, v=False)
            step(HP - 1, 1, scores=False, qk=False, v=False)
            norm_vector(dve, 3)
            norm_lo(dve, 3)

        SCALE4 = 1.0 / float(np.sqrt(np.float32(HD)))
        UNITS = 64
        AHEAD = 20
        LAG = 3
        QBANK = (7, 4, 5, 6)

        s_qw = sem("q4_w_split")
        s_mz = sem("max4_cleared")
        s_qp = sem("q4_projected")
        s_qe = sem("q4_copied")
        s_qy = sem("q4_split_made")
        s_qx = sem("q4_heads_made")
        s_q0 = sem("q4_heads_of_group_0_made")
        s_xs = sem("scores4_by_query")
        s_xm = sem("max4_taken")
        s_xt = sem("max4_T")
        s_xq = sem("max4_in_operand")
        s_ST = sem("scores4_by_key")
        s_xe = sem("exp4_and_hi")
        s_lod = sem("exp4_lo_by_dve")
        s_lop = sem("exp4_lo_by_pool")
        s_vp = sem("v4_padded_made")
        s_xp = sem("attended4_summed")
        s_xc = sem("attended4_copied")
        s_xr = sem("attended4_by_tokens")
        s_xo = sem("attended4_normed")
        s_x4t = sem("attended4_turned")
        s_x4c = sem("attended4_turned_copied")
        O4 = tiles(psum[:, 7, :])[:, :, 0:4 * VW].rearrange("p t (h d) -> p t h d", h=4)
        Pf = [raw[:, i, :] for i in range(4)]
        Ph = [whi[:, i, :] for i in range(4)]

        def q4_heads(eng, t, j):
            return eng.tensor_scalar(Qx[:, t, j, :], yq[:, t % 2, :], at["sel"][:, SEL_HEAD + j:SEL_HEAD + j + 1],
                                     at["sel"][:, SEL_MASK:SEL_MASK + 1], ALU.mult, ALU.add)

        def first_heads(eng, first):
            eng.wait_ge(s_qy, 1)
            for j in (first, first + 1):
                if first:
                    ins = eng.activation(Qx[:, 0, j, :], yq[:, 0, :], ACT.Identity,
                                         scale=at["sel"][:, SEL_HEAD + j:SEL_HEAD + j + 1],
                                         bias=at["sel"][:, SEL_MASK:SEL_MASK + 1])
                else:
                    ins = q4_heads(eng, 0, j)
            ins.then_inc(s_q0, 1)

        def exp4_lo(eng, n, done):
            eng.wait_ge(s_xe, n + 1)
            eng.tensor_tensor(Pl[:, n % 4, :], Pf[n % 4], Ph[n % 4].bitcast(F32),
                              ALU.subtract).then_inc(done, 1)

        def v4_pad(pool, t):
            for j in range(4):
                ins = pool.tensor_tensor(VP[:, t % 2, :, j, j * VW:j * VW + VW], Vx[:, :, 4 * t + j, :].bitcast(F32),
                                         one1[:].rearrange("p (o q) -> p o q", o=1).broadcast_to([128, C // 128, VW]),
                                         ALU.mult)
            ins.then_inc(s_vp, 1)

        def stage4_early_pool(pool):
            pstep(pool, pool.tensor_copy(Qrh[:], at["Qr_w"]))
            pool.tensor_tensor(Qrl[:], at["Qr_w"], Qrh[:].bitcast(F32), ALU.subtract).then_inc(s_qw, 1)
            pool.memset(mxt[:], 0.0).then_inc(s_mz, 1)
            pstep(pool, pool.memset(VP[:].bitcast(F32), 0.0))
            v4_pad(pool, 0)
            v4_pad(pool, 1)

        def stage4_pool(pool):
            pool.wait_ge(s_qy, 2)
            for j in range(4):
                ins = q4_heads(pool, 1, j)
            ins.then_inc(s_qx, 1)
            for n in range(1, UNITS, 2):
                exp4_lo(pool, n, s_lop)
                if n < 16:
                    t, j = 2 + n // 8, n // 2 % 4
                    pool.wait_ge(s_qy, t + 1)
                    ins = q4_heads(pool, t, j)
                    if j == 3:
                        ins.then_inc(s_qx, 1)
                if n in (21, 37):
                    t = 2 + n // 37
                    pool.wait_ge(s_xp, 16 * (t - 1))
                    v4_pad(pool, t)
                if n == 25:
                    pool.tensor_tensor(res[:], x_tok[:],
                                       at["bo"].rearrange("p (o d) -> p o d", o=1).broadcast_to([128, TT, D]),
                                       ALU.add).then_inc(s_res, 1)
            norm_pool(pool, 4)

        def q4_project(pe, t):
            w = slice(t * D, t * D + D)
            three(pe, psum[:, QBANK[t], :], Qrh[:, w], Qrl[:, w], xh[:], xl[:]).then_inc(s_qp, 1)

        def q4_scores(pe, w):
            t, j, u = w // 16, w // 4 % 4, w % 4
            if w == 0:
                pe.wait_ge(s_q0, 2)
            elif w % 16 == 0:
                pe.wait_ge(s_qx, t)
            if w >= 4:
                pe.wait_ge(s_xm, (w - 4) // 2 + 1)
            pe.matmul(psum[:, u, :], Qx[:, t, j, u * 128:u * 128 + 128], KX[:, t, u // 2 * SC:u // 2 * SC + SC],
                      start=True, stop=True).then_inc(s_xs, 1)

        def q4_turn(pe, t):
            pe.wait_ge(s_xm, 8 * (t + 1))
            if t >= 2:
                pe.wait_ge(s_xo, t - 1)
            for i in range(TT):
                ins = pe.transpose(psum[:, 7, i * 128:i * 128 + 128], mxt[:, i, :], ident)
            ins.then_inc(s_xt, 1)

        def k4_scores(pe, n):
            t, j, b = n // 16, n // 4 % 4, n // 2 % 2
            if n % 16 == 0:
                pe.wait_ge(s_xq, t + 1)
            if n >= 2:
                pe.wait_ge(s_xe, n - 1)
            for a in range(2):
                k = b * SC + (n % 2 * 2 + a) * 128
                ins = pe.matmul(psum[:, 4 + n % 2, a * S:a * S + S], KX[:, t, k:k + 128],
                                Qx[:, t, j, b * S:b * S + S], start=True, stop=True)
            ins.then_inc(s_ST, 1)

        def v4_attend(pe, n):
            t, j, b = n // 16, n // 4 % 4, n // 2 % 2
            pe.wait_ge(s_lop if n % 2 else s_lod, n // 2 + 1)
            if n % 16 == 0:
                pe.wait_ge(s_vp, t + 1)
                if t:
                    pe.wait_ge(s_xc, t)
            for a in range(2):
                for p in (Ph[n % 4], Pl[:, n % 4, :]):
                    ins = pe.matmul(psum[0:4 * VW, 6, b * S:b * S + S], VP[:, t % 2, 4 * b + n % 2 * 2 + a, j, :],
                                    p[:, a * S:a * S + S], start=n % 16 == 0 and a == 0 and p is Ph[n % 4],
                                    stop=n % 16 == 15 and a == 1 and p is not Ph[n % 4],
                                    skip_group_check=True)
            ins.then_inc(s_xp, 1)

        def v4_turn(pe, t):
            pe.wait_ge(s_xc, t + 1)
            for i in range(TT):
                ins = pe.transpose(psum[:, 7, i * 128:i * 128 + 4 * VW], OS[0:4 * VW, i * 128:i * 128 + 128],
                                   ident[0:4 * VW, 0:4 * VW])
            ins.then_inc(s_xr, 1)

        def stage4_tensor(pe):
            pe.wait_ge(s_qw, 1)
            pe.wait_ge(s_k4d, 8)
            pe.wait_ge(s_mz, 1)
            three_early(pe, 3, psum[:, QBANK[0], :], Qrh[:, 0:D], Qrl[:, 0:D]).then_inc(s_qp, 1)
            for t in range(1, 4):
                q4_project(pe, t)
            for w in range(16):
                q4_scores(pe, w)
            q4_turn(pe, 0)
            for w in range(16, AHEAD):
                q4_scores(pe, w)
            pe.wait_ge(s_qe, 4)
            for n in range(UNITS + LAG):
                if n < UNITS - AHEAD:
                    q4_scores(pe, n + AHEAD)
                if n < UNITS:
                    k4_scores(pe, n)
                if n >= LAG:
                    v4_attend(pe, n - LAG)
                if n % 16 == 5 and n > 16:
                    v4_turn(pe, n // 16 - 1)
                if n % 16 == 12 and n + 4 < UNITS:
                    q4_turn(pe, n // 16 + 1)
            v4_turn(pe, 3)
            pe.wait_ge(s_xo, 4)
            for i in range(TT):
                ins = pe.transpose(psum[:, 0, i * 128:i * 128 + 128], att4[:, i, :], ident)
            ins.then_inc(s_x4t, 1)
            pe.wait_ge(s_res, 2)
            residual_first(pe, res[:])
            pe.wait_ge(s_x4c, 1)
            for i in range(TT):
                ins = pe.matmul(Y[:, i, :], aT4[:, i * 128:i * 128 + 128], at["O_w"], start=False, stop=True,
                                skip_group_check=True)
            ins.then_inc(s_y, 1)
            norm_tensor(pe, 4)

        def stage4_scalar(act):
            act.wait_ge(s_in["masked"], 16)

            def q_copy(t):
                act.wait_ge(s_qp, t + 1)
                if t >= 2:
                    act.wait_ge(s_qy, t - 1)
                b = at["qb"][:, t:t + 1]
                act.activation(xq[:, t % 2, :], psum[:, QBANK[t], :], ACT.Identity, bias=b)
                act.activation(rq[:, t % 2, :], psum[:, QBANK[t], :], ACT.Identity, bias=b).then_inc(s_qe, 1)

            def o_copy(t):
                act.wait_ge(s_xp, 16 * t + 16)
                act.activation(OS[0:4 * VW, :], psum[0:4 * VW, 6, :], ACT.Copy).then_inc(s_xc, 1)

            for t in range(4):
                q_copy(t)
                if t == 0:
                    first_heads(act, 2)
            for n in range(UNITS):
                act.wait_ge(s_ST, n + 1)
                if n >= 4:
                    act.wait_ge(s_xp, n - 3)
                act.activation(Pf[n % 4], psum[:, 4 + n % 2, :], ACT.Exp, scale=SCALE4)
                act.activation(Ph[n % 4], psum[:, 4 + n % 2, :], ACT.Exp, scale=SCALE4).then_inc(s_xe, 1)
                if n % 16 == 2 and n > 16:
                    o_copy(n // 16 - 1)
            o_copy(3)
            act.wait_ge(s_x4t, 1)
            act.activation(aT4[:], psum[:, 0, :], ACT.Copy).then_inc(s_x4c, 1)
            norm_scalar(act, 4)

        def stage4_vector(dve):
            dve.wait_ge(s_mz, 1)

            def q_split(t):
                dve.wait_ge(s_qe, t + 1)
                if t > 2:
                    dve.wait_ge(s_qx, t - 2)
                dve.scalar_tensor_tensor(yq[:, t % 2, :], rq[:, t % 2, :].bitcast(F32),
                                         at["sel"][:, SEL_LO_Q:SEL_LO_Q + 1],
                                         xq[:, t % 2, :], ALU.mult, ALU.add).then_inc(s_qy, 1)

            def maxima(m):
                t, j, b = m // 8, m // 2 % 4, m % 2
                dve.wait_ge(s_xs, 2 * m + 2)
                if t and m % 8 == 0:
                    dve.wait_ge(s_xt, t)
                dve.tensor_reduce(mxt[:, 2 * b:2 * b + 2, MR + j], psum[:, 2 * b:2 * b + 2, :], AX,
                                  ALU.max).then_inc(s_xm, 1)

            def put_max(t):
                dve.wait_ge(s_xt, t + 1)
                if t:
                    dve.wait_ge(s_qx, t)
                for j in range(4):
                    ins = dve.tensor_scalar(Qx[MR:128, t, j, :], psum[MR:128, 7, :],
                                            at["sel"][MR:128, SEL_MAX + j:SEL_MAX + j + 1],
                                            at["sel"][MR:128, SEL_MASK:SEL_MASK + 1], ALU.mult, ALU.add)
                ins.then_inc(s_xq, 1)

            def norm_heads(t):
                dve.wait_ge(s_xr, t + 1)
                dstep(dve, dve.reciprocal(rs4[:], O4[:, :, :, HD]))
                a = att4[:, :, t * 32:t * 32 + 32].rearrange("p t (h d) -> p t h d", h=4)
                r = rs4[:].rearrange("p t (h o) -> p t h o", o=1).broadcast_to([128, TT, 4, HD])
                dve.tensor_tensor(lo4[:], O4[:, :, :, HD + 1:VW], r, ALU.mult)
                dstep(dve, dve.tensor_tensor(a, O4[:, :, :, 0:HD], r, ALU.mult))
                dve.tensor_tensor(a, a, lo4[:], ALU.add).then_inc(s_xo, 1)

            q_split(0)
            first_heads(dve, 0)
            maxima(0)
            q_split(1)
            for m in range(1, 8):
                maxima(m)
            put_max(0)
            q_split(2)
            maxima(8)
            maxima(9)
            for n in range(UNITS):
                if n % 2 and n + AHEAD < UNITS:
                    maxima((n + AHEAD) // 2)
                if n % 2 == 0:
                    exp4_lo(dve, n, s_lod)
                if n == 3:
                    q_split(3)
                if n % 16 == 6 and n > 16:
                    norm_heads(n // 16 - 1)
                if n % 16 == 13 and n + 3 < UNITS:
                    put_max(n // 16 + 1)
            norm_heads(3)
            norm_vector(dve, 4)
            norm_lo(dve, 4)
        late.close()
        upr = sb("expert_up_raw", [128, 2, H1 + HC], stack=late5)
        dnr = sb("expert_down_raw", [128, 2, HC * D], stack=late5)
        fcb = sb("expert_up_bias", [128, 2, HC], stack=late5)
        fch = whi[:, 0:2, :]
        fcl = wlo[:].rearrange("p a w -> p (a w)")[:, 0:2 * H1].rearrange("p (a w) -> p a w", a=2)
        hT = sb("expert_hidden", [128, 2, HC, T], stack=late5)
        acc = sb("experts_summed", [128, TT, D], stack=late5)
        p5 = sb("probs5", [128, TT, E1], stack=late5)
        mx5 = sb("max5", [128, TT], stack=late5)
        cT5 = sb("combine5_T", [E1, T], stack=late5)

        s_up = [sem(f"expert_up_loaded_{i}") for i in range(2)]
        s_dn = [sem(f"expert_down_loaded_{i}") for i in range(2)]
        s_fb = sem("expert_up_bias_copied")
        s_fh = sem("expert_up_hi_made")
        s_fl = sem("expert_up_lo_made")
        s_l5 = sem("logits5")
        s_d5 = sem("logits5_less_max")
        s_e5 = sem("exp5")
        s_c5 = sem("combine5")
        s_c5t = sem("combine5_turned")
        s_c5c = sem("combine5_turned_copied")
        s_fc = sem("expert_hidden_chunk_summed")
        s_ge = sem("expert_hidden_chunk_gelu")
        s_pj = sem("expert_output")
        s_ac = sem("expert_added")

        def load_up(sp, e, slot):
            sp.dma_start(upr[:, slot, :], up_w[e, :, :]).then_inc(s_up[slot], 16)

        def load_down(sp, e, slot):
            sp.dma_start(dnr[:, slot, :], down_w[e, :, :]).then_inc(s_dn[slot], 16)

        def stage5_sync(sp):
            sp.wait_ge(s_xn, 4 * TT)
            for e in range(2):
                load_up(sp, e, e)
                load_down(sp, e, e)
            with sp.Fori(0, E1 // 2 - 1) as it:
                for j in range(2):
                    sp.wait_ge(s_fb, it * 2 + j + 1)
                    load_up(sp, it * 2 + j + 2, j)
                    sp.wait_ge(s_pj, it * 2 + j + 1)
                    load_down(sp, it * 2 + j + 2, j)

        def expert_split(pool, e, par, turn):
            pool.wait_ge(s_up[par], turn * 16 + 16)
            pool.tensor_tensor(fch[:, par, :], upr[:, par, 0:H1], one1[:].broadcast_to([128, H1]),
                               ALU.mult).then_inc(s_fh, 1)
            pool.wait_ge(s_fh, e + 1)
            pool.tensor_tensor(fcl[:, par, :], upr[:, par, 0:H1], fch[:, par, :].bitcast(F32),
                               ALU.subtract).then_inc(s_fl, 1)
            pool.tensor_tensor(fcb[:, par, :], upr[:, par, H1:H1 + HC], one1[:].broadcast_to([128, HC]),
                               ALU.mult).then_inc(s_fb, 1)

        def stage5_pool(pool):
            expert_split(pool, 0, 0, 0)
            expert_split(pool, 1, 1, 0)
            with pool.Fori(0, E1 // 2 - 1) as it:
                for j in range(2):
                    pool.wait_ge(s_ge, it * 8 + j * 4 + 4)
                    expert_split(pool, it * 2 + j + 2, j, it + 1)
            norm_pool(pool, 5)

        def expert_up(pe, e, par, first=False):
            pe.wait_ge(s_fl, e + 1)
            for c in range(HC):
                if not first:
                    pe.wait_ge(s_ge, (e - 1) * 4 + c + 1)
                w = slice(c * 128, c * 128 + 128)
                three(pe, psum[:, c, :], fch[:, par, w], fcl[:, par, w], xh[:], xl[:]).then_inc(s_fc, 1)

        def expert_down(pe, e, par, turn):
            pe.wait_ge(s_dn[par], turn * 16 + 16)
            pe.wait_ge(s_ge, e * 4 + 4)
            pe.wait_ge(s_ac, e if isinstance(e, int) else e + 1)
            for i in range(TT):
                for c in range(HC):
                    ins = pe.matmul(psum[:, 4 + par, i * 128:i * 128 + 128], hT[:, par, c, i * 128:i * 128 + 128],
                                    dnr[:, par, c * D:c * D + D], start=c == 0, stop=c == HC - 1)
            ins.then_inc(s_pj, 1)

        def stage5_tensor(pe):
            pe.wait_ge(s_xh, 5)
            pe.wait_ge(s_xl, 4)
            for i in range(TT):
                t = slice(i * 128, i * 128 + 128)
                ins = three(pe, psum[:, 5, i * E1:i * E1 + E1], xh[:, t], xl[:, t], rwh[:], rwl[:])
            ins.then_inc(s_l5, 1)
            expert_up(pe, 0, 0, first=True)
            with pe.Fori(0, E1 // 2 - 1) as it:
                for j in range(2):
                    expert_up(pe, it * 2 + j + 1, 1 - j)
                    expert_down(pe, it * 2 + j, j, it)
            pe.wait_ge(s_c5, 1)
            for i in range(TT):
                ins = pe.transpose(psum[0:E1, 6, i * 128:i * 128 + 128], comb5[:, i, :], ident)
            ins.then_inc(s_c5t, 1)
            expert_up(pe, E1 - 1, 1)
            expert_down(pe, E1 - 2, 0, E1 // 2 - 1)
            pe.wait_ge(s_c5c, 1)
            pe.wait_ge(s_in["bproj"], 16)
            for i in range(TT):
                ins = pe.matmul(Y[:, i, :], cT5[:, i * 128:i * 128 + 128], bpj[:], start=True, stop=True)
            ins.then_inc(s_y, 1)
            expert_down(pe, E1 - 1, 1, E1 // 2 - 1)

        def expert_gelu(act, e, par):
            act.wait_ge(s_fb, e + 1)
            for c in range(HC):
                act.wait_ge(s_fc, e * 4 + c + 1)
                act.activation(hT[:, par, c, :], psum[:, c, :], ACT.Gelu_apprx_tanh,
                               bias=fcb[:, par, c:c + 1]).then_inc(s_ge, 1)

        def stage5_scalar(act):
            act.wait_ge(s_d5, 1)
            act.activation(p5[:], p5[:], ACT.Exp).then_inc(s_e5, 1)
            load_table(act, ACT.Gelu_apprx_tanh)
            expert_gelu(act, 0, 0)
            with act.Fori(0, E1 // 2 - 1) as it:
                for j in range(2):
                    expert_gelu(act, it * 2 + j + 1, 1 - j)
            act.wait_ge(s_c5t, 1)
            act.activation(cT5[:], psum[0:E1, 6, :], ACT.Copy).then_inc(s_c5c, 1)
            expert_gelu(act, E1 - 1, 1)

        def expert_add(dve, e, par):
            dve.wait_ge(s_ac, e + 1)
            dve.wait_ge(s_pj, e + 1)
            for i in range(TT):
                ins = dve.scalar_tensor_tensor(acc[:, i, :], psum[:, 4 + par, i * 128:i * 128 + 128],
                                               comb5e[:, i, e, :], acc[:, i, :], ALU.mult, ALU.add)
            ins.then_inc(s_ac, 1)

        comb5 = comb[:].rearrange("p t e -> p (t e)")[:, 0:TT * E1].rearrange("p (t e) -> p t e", t=TT)
        comb5e = comb[:].rearrange("p t e -> p (t e)")[:, 0:TT * E1].rearrange("p (t e o) -> p t e o", t=TT, o=1)

        def stage5_vector(dve):
            lg = psum[:, 5, 0:TT * E1].rearrange("p (t e) -> p t e", t=TT)
            dve.wait_ge(s_l5, 1)
            dstep(dve, dve.tensor_reduce(mx5[:], lg, AX, ALU.max))
            dve.tensor_tensor(p5[:], lg, bc(mx5[:], E1), ALU.subtract).then_inc(s_d5, 1)
            dve.tensor_copy(acc[:], x_tok[:]).then_inc(s_ac, 1)
            dve.wait_ge(s_e5, 1)
            dstep(dve, dve.tensor_reduce(mx5[:], p5[:], AX, ALU.add))
            dstep(dve, dve.reciprocal(mx5[:], mx5[:]))
            dstep(dve, dve.tensor_tensor(p5[:], p5[:], bc(mx5[:], E1), ALU.mult))
            chosen = top_k(dve, p5[:], E1, K1, at["reset8"])
            normalised(dve, p5[:], chosen, E1, 0.0, s_c5)
            dve.wait_ge(s_c5, 1)
            with dve.Fori(0, E1 // 2 - 1) as it:
                for j in range(2):
                    expert_add(dve, it * 2 + j, j)
            expert_add(dve, E1 - 2, 0)
            dve.wait_ge(s_ac, E1)
            dve.wait_ge(s_y, 6)
            dstep(dve, dve.tensor_tensor(acc[:], acc[:], Y, ALU.add))
            expert_add(dve, E1 - 1, 1)
            dve.wait_ge(s_ac, E1 + 1)
            norm_vector(dve, 5, acc[:])

        late5.close()

        late4.close()


        @block.sync
        def _(sp):
            for n in ("front", "ident", "local"):
                sp.dma_start(pk[n][:], packs[n]).then_inc(s_in[n], 16)
            sp.dma_start(rowb[:], rows.broadcast_to([128, width(ROWS)])).then_inc(s_in["rows"], 16)
            sp.dma_start(maskb[:], maskin.broadcast_to([128, C])).then_inc(s_in["mask"], 16)
            sp.dma_start(bpj[:], bproj).then_inc(s_in["bproj"], 16)
            for n in ("cross", "masked", "route", "heads"):
                sp.dma_start(pk[n][:], packs[n]).then_inc(s_in[n], 16)
            stage2_sync(sp)
            stage3_sync(sp)
            stage5_sync(sp)
            for i in range(0, TT, 2):
                sp.wait_ge(s_xn, (6 - 1) * TT + i + 2)
                sp.dma_start(out[:, i:i + 2, :], x_tok[:, i:i + 2, :]).then_inc(s_out, 16)
            sp.wait_ge(s_out, 32)

        @block.tensor
        def _(pe):
            stage0_tensor(pe)
            stage1_tensor(pe)
            stage2_tensor(pe)
            stage3_tensor(pe)
            stage4_tensor(pe)
            stage5_tensor(pe)

        @block.vector
        def _(dve):
            stage0_vector(dve)
            stage1_vector(dve)
            stage2_vector(dve)
            stage3_vector(dve)
            stage4_vector(dve)
            stage5_vector(dve)

        @block.scalar
        def _(act):
            stage0_scalar(act)
            stage1_scalar(act)
            stage2_scalar(act)
            stage3_scalar(act)
            stage4_scalar(act)
            stage5_scalar(act)

        @block.gpsimd
        def _(pool):
            stage0_pool(pool)
            stage1_pool(pool)
            stage2_pool(pool)
            stage3_pool(pool)
            stage4_pool(pool)
            stage5_pool(pool)


def kernel(**inputs):
    import concourse.bacc as bacc
    from concourse.bass_utils import run_bass_kernel_spmd

    g = {k: np.asarray(v) for k, v in inputs.items()}
    f = np.float32

    def col(v):
        return v.reshape(-1, 1)

    def tok(v):
        return v.reshape(-1, 128, v.shape[-1]).transpose(1, 0, 2).reshape(128, -1)

    part = np.arange(128)
    heads_of = (part[:, None] // HD == np.arange(NH)[None, :]).astype(f)
    blocks = (part[:, None] // HD == part[None, :] // HD).astype(f)
    causal = np.where(part[None, :] > part[:, None], f(NEG), f(0))
    half = np.stack([part < 64, part >= 64], 1).astype(f)
    sel = np.zeros((128, 12), f)
    sel[:, SEL_LO_Q] = -((part < MR) & (part % HR // HD == 2)).astype(f)
    sel[:, SEL_LO_K] = -((part < MR) & (part % HR // HD == 1)).astype(f)
    for j in range(4):
        sel[:, SEL_HEAD + j] = part // HR == j
        sel[:, SEL_MAX + j] = -(part == MR + j).astype(f)
    sel[:, SEL_MASK] = part == KR
    sel[:, SEL_MAXES] = (part >= MR) & (part < MR + 4)

    def packed_heads(w):
        w3 = np.repeat(w.reshape(4, 4, 1, HD, -1), 3, axis=2).reshape(4, MR, -1)
        return np.concatenate([w3, np.zeros((4, 128 - MR, w3.shape[-1]), f)], axis=1)

    def packed_w(w):
        return packed_heads(w).transpose(2, 0, 1).reshape(128, -1)

    def packed_b(b):
        return packed_heads(b.reshape(D, 1))[:, :, 0].T

    pair = (np.arange(NP)[:, None, None] * 2 + part[None, None, :] // I0)
    row = part[None, :, None] % E0
    spread = (row == pair).astype(f)
    up = lambda w: w.reshape(NP, 2 * I0, D).transpose(0, 2, 1)
    down = g["L0_ffn_ed_w"].reshape(NP, 2, D, I0).transpose(0, 1, 3, 2).reshape(NP, 2 * I0, D)
    routed = np.concatenate([up(g["L0_ffn_eg_w"]), up(g["L0_ffn_eu_w"]), down, spread], axis=2)
    shared = np.concatenate([g["L0_ffn_sg_w"].T, g["L0_ffn_su_w"].T, g["L0_ffn_sd_w"].T, np.zeros((128, 128), f)], axis=1)

    qkv = np.stack([g["L1_attn_w_q"], g["L1_attn_w_k"], g["L1_attn_w_v"]], 1)
    qkv = qkv.reshape(D, 3, HP, 2 * KQ).transpose(2, 0, 1, 3).reshape(HP, D, -1)
    wo = g["L1_attn_w_o"].reshape(D, HP, 2 * KQ).transpose(2, 1, 0).reshape(128, -1)
    reset = lambda n: np.broadcast_to((np.arange(TT * n) % n != 0).astype(f), (128, TT * n))

    parts = {
        "xT": g["x"].reshape(T, D).T, "WqT": g["L0_attn_Wq"].T,
        "WkvT": np.concatenate([g["L0_attn_Wk"].T, g["L0_attn_Wv"].T], 1),
        "conv": np.concatenate([g["L0_attn_conv_w"], col(g["L0_attn_conv_b"])], 1),
        "blocks": blocks, "heads": heads_of, "ident": np.eye(128, dtype=f),
        "x_tok": tok(g["x"].reshape(T, D)), "WpT": g["L0_attn_Wp"].T,
        "ctxT": g["ctx_1024"].reshape(C, D).T,
        "KsT_w": g["L0_xattn_Wk_s"].T, "QsT_w": g["L0_xattn_Wq_s"].T, "Vs_w": g["L0_xattn_Wv_s"].T,
        "QcT_w": g["L0_xattn_Wq_c"].T, "KcT_w": g["L0_xattn_Wk_c"].T, "Vc_w": g["L0_xattn_Wv_c"].T,
        "gate_w": np.concatenate([g["L0_xattn_Wg"][:, :D].T, g["L0_xattn_Wg"][:, D:].T], 1),
        "cols": np.stack([g["L0_xattn_" + n] for n in ("bk_s", "bq_s", "bq_c", "bk_c", "bg")], 1),
        "gw": g["L0_ffn_gate_w"].T, "reset8": reset(G0), "reset64": reset(E0), "rw": g["L1_ffn_router_w"].T,
        "wo": wo, "causal": causal, "half": half,
        "Kr_w": packed_w(g["L1_xattn_Wk"]), "Qr_w": packed_w(g["L1_xattn_Wq"]),
        "V_w": g["L1_xattn_Wv"].T, "O_w": g["L1_xattn_Wo"].T,
        "qb": packed_b(g["L1_xattn_bq"]), "kb": packed_b(g["L1_xattn_bk"]), "sel": sel,
    }
    arrays = {"pack_" + n: np.ascontiguousarray(np.concatenate([parts[k] for k, _ in p], axis=1))
              for n, p in PACKS.items()}
    arrays["rows"] = np.concatenate([g[k] for k in (
        "L0_attn_bp", "L0_xattn_bv_s", "L0_xattn_bv_c", "L0_ffn_gate_bias", "L1_xattn_bv", "L1_xattn_bo")])[None]
    arrays["bproj"] = np.ascontiguousarray(g["L1_ffn_b_proj"])
    arrays["mask_in"] = np.ascontiguousarray(g["mask_BxS2_bk0"]).reshape(1, C)
    arrays["pairs_w"] = np.concatenate([shared[None], routed], axis=0)
    arrays["up_w"] = np.concatenate([g["L1_ffn_w_fc"], g["L1_ffn_b_fc"].reshape(E1, HC, 128).transpose(0, 2, 1)], axis=2)
    arrays["down_w"] = np.ascontiguousarray(
        g["L1_ffn_w_proj"].reshape(E1, HC, 128, D).transpose(0, 2, 1, 3).reshape(E1, 128, -1))
    arrays["heads_w"] = np.ascontiguousarray(qkv)

    nc = bacc.Bacc("TRN2", target_bir_lowering=False, num_devices=1)
    aps = {n: nc.dram_tensor(n, a.shape, mybir.dt.from_np(a.dtype), kind="ExternalInput").ap()
           for n, a in arrays.items()}
    out = nc.dram_tensor("out", (T, D), F32, kind="ExternalOutput").ap()
    build(nc, {n: aps["pack_" + n] for n in PACKS}, aps["rows"], aps["bproj"], aps["mask_in"],
          aps["pairs_w"], aps["heads_w"], aps["up_w"], aps["down_w"],
          out.rearrange("(t p) d -> p t d", p=128))
    r = run_bass_kernel_spmd(nc, [arrays], core_ids=[0])
    return r.results[0]["out"].reshape(NB, S, D)
```
